# Optimizing a Trainium2 kernel written in Bass

```python
import numpy as np
import jax
import jax.numpy as jnp

def _softmax(x, axis=-1):
    return jax.nn.softmax(x, axis=axis)

def _gelu(x):
    return jax.nn.gelu(x, approximate=True)

def _silu(x):
    return jax.nn.silu(x)

def _sigmoid(x):
    return jax.nn.sigmoid(x)

def _layernorm(x, axis=-1, eps=1e-05):
    m = jnp.mean(x, axis=axis, keepdims=True)
    v = jnp.var(x, axis=axis, keepdims=True)
    return (x - m) / jnp.sqrt(v + eps)

def _scatter_add(tgt, idx, src, axis=0):
    return tgt.at[idx].add(src)

def _segment_sum(src, seg, n):
    return jax.ops.segment_sum(src, seg, n)
kernel_name = 'mk_flamingo_gated_d2_seqx_r4_b92ee8'

def setup_inputs(seed: int=0):
    np.random.seed(seed)
    _w = jnp.asarray

    def _rec_inputs():
        import jax
        import jax.numpy as jnp
        _rk = jax.random.key(seed)
        x = -0.0005207 + 1.001 * jax.random.normal(jax.random.fold_in(_rk, 1), (16, 112, 1024), jnp.float32)
        _lenS = 112 - jax.random.randint(jax.random.fold_in(_rk, 7), (16,), 0, max(1, 112 // 4) + 1, jnp.int32)
        _lenS2 = 375 - jax.random.randint(jax.random.fold_in(_rk, 8), (16,), 0, max(1, 375 // 4) + 1, jnp.int32)
        _ctx_4096P = jax.random.normal(jax.random.fold_in(_rk, 11), (16, 16, 1024), jnp.float32)
        _ctx_4096c = jax.random.dirichlet(jax.random.fold_in(_rk, 511), 0.3 * jnp.ones((16,), jnp.float32), (16, 375))
        _ctx_4096t = jnp.einsum('bsk,bkd->bsd', _ctx_4096c, _ctx_4096P)
        _ctx_4096t = _ctx_4096t * jax.lax.rsqrt(jnp.mean(jnp.square(_ctx_4096t)) + 1e-12) * 0.953939
        ctx_4096 = -0.00010331 + 0.999899 * (_ctx_4096t + 0.3 * jax.random.normal(jax.random.fold_in(_rk, 611), (16, 375, 1024), jnp.float32))
        _g = jax.random.normal(jax.random.fold_in(_rk, 9001), (2, 2), jnp.float32)
        _g = jnp.sign(_g) * jnp.maximum(jnp.abs(_g), 1.0) + (_g == 0) * 1.0
        g_xattn = _g[0]
        g_ffn = _g[1]
        return (x, ctx_4096, g_xattn, g_ffn)
    x, ctx_4096, g_xattn, g_ffn = _rec_inputs()

    def _L0_xattn_setup():
        import jax, jax.numpy as jnp
        import numpy as np
        B, Q, D = (8, 64, 1024)
        CTX = 1024
        H, KV, HD = (16, 4, 96)
        G = H // KV
        key = jax.random.key(seed)
        ks = jax.random.split(key, 6)
        s = 0.02
        return {'latents': jax.random.normal(ks[0], (B, Q, D), jnp.float32), 'context': jax.random.normal(ks[1], (B, CTX, D), jnp.float32), 'Wq': jax.random.normal(ks[2], (H * HD, D), jnp.float32) * s, 'Wk': jax.random.normal(ks[3], (KV * HD, D), jnp.float32) * s, 'Wv': jax.random.normal(ks[4], (KV * HD, D), jnp.float32) * s, 'Wo': jax.random.normal(ks[5], (D, H * HD), jnp.float32) * s}
    _L0_xattn_all = _L0_xattn_setup()
    _L0_xattn_in = {k: v for k, v in _L0_xattn_all.items() if k in ('Wq', 'Wk', 'Wv', 'Wo')}
    del _L0_xattn_all

    def _L0_ffn_setup():
        import jax, jax.numpy as jnp
        import numpy as np
        BLOCK_SIZE = 16
        FP4_VALUES = jnp.array([0.0, 0.5, 1.0, 1.5, 2.0, 3.0, 4.0, 6.0, -0.0, -0.5, -1.0, -1.5, -2.0, -3.0, -4.0, -6.0], dtype=jnp.float32)

        def dequantize_nvfp4_sim(weight_q, weight_scales, block_size=BLOCK_SIZE):
            O, I = weight_q.shape
            vals = FP4_VALUES[weight_q]
            w = vals.reshape(O, I // block_size, block_size) * weight_scales[:, :, None]
            return w.reshape(O, I)
        key = jax.random.key(seed)
        k1, k2, k3 = jax.random.split(key, 3)
        O, I = (1024, 1024)
        x = jax.random.normal(k1, (2, 256, I), dtype=jnp.float32)
        weight_scales = jax.random.uniform(k2, (O, I // BLOCK_SIZE), dtype=jnp.float32, minval=0.01, maxval=1.0)
        weight_q = jax.random.randint(k3, (O, I), 0, 16, dtype=jnp.int32)
        return {'x': x, 'weight_scales': weight_scales, 'weight_q': weight_q}
    _L0_ffn_all = _L0_ffn_setup()
    _L0_ffn_in = {k: v for k, v in _L0_ffn_all.items() if k in ('weight_scales', 'weight_q')}
    del _L0_ffn_all

    def _L1_xattn_setup():
        import jax, jax.numpy as jnp
        import numpy as np
        TEXT_DIM = 1024
        FEATURE_DIM = 1024

        def _xavier_uniform(key, shape):
            fan_in, fan_out = (shape[1], shape[0])
            limit = float(np.sqrt(6.0 / (fan_in + fan_out)))
            return jax.random.uniform(key, shape, jnp.float32, -limit, limit)
        key = jax.random.key(seed)
        k1, k2, k3, k4 = jax.random.split(key, 4)
        text = jax.random.normal(k1, (8, 512, TEXT_DIM), jnp.float32)
        features = jax.random.normal(k2, (8, 144, FEATURE_DIM), jnp.float32)
        Wq = _xavier_uniform(k3, (FEATURE_DIM, TEXT_DIM))
        bq = jnp.zeros((FEATURE_DIM,), jnp.float32)
        Wk = _xavier_uniform(k4, (FEATURE_DIM, FEATURE_DIM))
        bk = jnp.zeros((FEATURE_DIM,), jnp.float32)
        return {'text': text, 'features': features, 'Wq': Wq, 'bq': bq, 'Wk': Wk, 'bk': bk}
    _L1_xattn_all = _L1_xattn_setup()
    _L1_xattn_in = {k: v for k, v in _L1_xattn_all.items() if k in ('Wq', 'bq', 'Wk', 'bk')}
    del _L1_xattn_all

    def _L1_ffn_setup():
        import jax, jax.numpy as jnp
        import numpy as np
        RANKS = (8, 16, 32, 64)
        TOPK = 1
        SCALING = 1.0 / 4
        key = jax.random.key(seed)
        ks = jax.random.split(key, 7)
        D_IN, D_OUT, MAX_R, N_RANKS = (1024, 1024, 64, len(RANKS))
        B_, S_ = (4, 512)
        return {'hidden_states': jax.random.normal(ks[0], (B_, S_, D_IN), jnp.float32), 'W': jax.random.normal(ks[1], (D_OUT, D_IN), jnp.float32) * 0.02, 'b': jax.random.normal(ks[2], (D_OUT,), jnp.float32) * 0.02, 'A': jax.random.normal(ks[3], (MAX_R, D_IN), jnp.float32) * 0.02, 'B': jnp.zeros((D_OUT, MAX_R), jnp.float32) + jax.random.normal(ks[4], (D_OUT, MAX_R), jnp.float32) * 0.02, 'gate_w': jax.random.normal(ks[5], (N_RANKS, D_IN), jnp.float32) * 0.02, 'gate_b': jax.random.normal(ks[6], (N_RANKS,), jnp.float32) * 0.02}
    _L1_ffn_all = _L1_ffn_setup()
    _L1_ffn_in = {k: v for k, v in _L1_ffn_all.items() if k in ('W', 'b', 'A', 'B', 'gate_w', 'gate_b')}
    del _L1_ffn_all
    return {'x': x, 'ctx_4096': ctx_4096, 'g_xattn': g_xattn, 'g_ffn': g_ffn, 'L0_xattn_Wq': _L0_xattn_in['Wq'], 'L0_xattn_Wk': _L0_xattn_in['Wk'], 'L0_xattn_Wv': _L0_xattn_in['Wv'], 'L0_xattn_Wo': _L0_xattn_in['Wo'], 'L0_ffn_weight_scales': _L0_ffn_in['weight_scales'], 'L0_ffn_weight_q': _L0_ffn_in['weight_q'], 'L1_xattn_Wq': _L1_xattn_in['Wq'], 'L1_xattn_bq': _L1_xattn_in['bq'], 'L1_xattn_Wk': _L1_xattn_in['Wk'], 'L1_xattn_bk': _L1_xattn_in['bk'], 'L1_ffn_W': _L1_ffn_in['W'], 'L1_ffn_b': _L1_ffn_in['b'], 'L1_ffn_A': _L1_ffn_in['A'], 'L1_ffn_B': _L1_ffn_in['B'], 'L1_ffn_gate_w': _L1_ffn_in['gate_w'], 'L1_ffn_gate_b': _L1_ffn_in['gate_b']}

def reference(x, ctx_4096, g_xattn, g_ffn, L0_xattn_Wq, L0_xattn_Wk, L0_xattn_Wv, L0_xattn_Wo, L0_ffn_weight_scales, L0_ffn_weight_q, L1_xattn_Wq, L1_xattn_bq, L1_xattn_Wk, L1_xattn_bk, L1_ffn_W, L1_ffn_b, L1_ffn_A, L1_ffn_B, L1_ffn_gate_w, L1_ffn_gate_b):
    import jax
    import jax.numpy as jnp

    def _L0_xattn_ref(latents, context, Wq, Wk, Wv, Wo):
        import jax, jax.numpy as jnp
        import numpy as np
        B, Q, D = (8, 64, 1024)
        CTX = 1024
        H, KV, HD = (16, 4, 96)
        G = H // KV
        b, q_len, _ = latents.shape
        hidden = jnp.concatenate([context, latents], axis=1)
        s_len = hidden.shape[1]
        q = (latents @ Wq.T).reshape(b, q_len, H, HD)
        k = (hidden @ Wk.T).reshape(b, s_len, KV, HD)
        v = (hidden @ Wv.T).reshape(b, s_len, KV, HD)
        q = q.transpose(0, 2, 1, 3).reshape(b, KV, G, q_len, HD)
        k = k.transpose(0, 2, 1, 3)
        v = v.transpose(0, 2, 1, 3)
        scale = 1.0 / jnp.sqrt(jnp.asarray(HD, q.dtype))
        scores = jnp.einsum('bkgqd,bksd->bkgqs', q, k) * scale
        attn = jax.nn.softmax(scores.astype(jnp.float32), axis=-1).astype(q.dtype)
        out = jnp.einsum('bkgqs,bksd->bkgqd', attn, v)
        out = out.reshape(b, H, q_len, HD).transpose(0, 2, 1, 3).reshape(b, q_len, H * HD)
        return out @ Wo.T

    def _L0_ffn_ref(x, weight_scales, weight_q):
        import jax, jax.numpy as jnp
        import numpy as np
        BLOCK_SIZE = 16
        FP4_VALUES = jnp.array([0.0, 0.5, 1.0, 1.5, 2.0, 3.0, 4.0, 6.0, -0.0, -0.5, -1.0, -1.5, -2.0, -3.0, -4.0, -6.0], dtype=jnp.float32)

        def dequantize_nvfp4_sim(weight_q, weight_scales, block_size=BLOCK_SIZE):
            O, I = weight_q.shape
            vals = FP4_VALUES[weight_q]
            w = vals.reshape(O, I // block_size, block_size) * weight_scales[:, :, None]
            return w.reshape(O, I)
        w = dequantize_nvfp4_sim(weight_q, weight_scales).astype(jnp.bfloat16)
        x_bf16 = x.astype(jnp.bfloat16)
        out = jnp.einsum('bsi,oi->bso', x_bf16, w)
        return out.astype(x.dtype)

    def _L1_xattn_ref(text, features, Wq, bq, Wk, bk):
        import jax, jax.numpy as jnp
        import numpy as np
        TEXT_DIM = 1024
        FEATURE_DIM = 1024

        def _xavier_uniform(key, shape):
            fan_in, fan_out = (shape[1], shape[0])
            limit = float(np.sqrt(6.0 / (fan_in + fan_out)))
            return jax.random.uniform(key, shape, jnp.float32, -limit, limit)
        Q = jnp.einsum('btx,dx->btd', text, Wq) + bq
        K = jnp.einsum('bpx,dx->bpd', features, Wk) + bk
        scale = 1.0 / jnp.sqrt(jnp.asarray(K.shape[-1], K.dtype))
        scores = jnp.einsum('btd,bpd->btp', Q, K) * scale
        attn = jax.nn.softmax(scores, axis=-1)
        attended = jnp.einsum('btp,bpd->btd', attn, features)
        return attended

    def _L1_ffn_ref(hidden_states, W, b, A, B, gate_w, gate_b):
        import jax, jax.numpy as jnp
        import numpy as np
        RANKS = (8, 16, 32, 64)
        TOPK = 1
        SCALING = 1.0 / 4
        bsz, seq, d_in = hidden_states.shape
        out = jnp.einsum('bsd,od->bso', hidden_states, W) + b
        x = hidden_states.reshape(-1, d_in)
        scores = x @ gate_w.T + gate_b
        probs = jax.nn.softmax(scores, axis=-1)
        routing_weights, selected = jax.lax.top_k(probs, TOPK)
        routing_weights = routing_weights / jnp.sum(routing_weights, axis=-1, keepdims=True)
        lora_outputs = jnp.stack([x @ A[:r, :].T @ B[:, :r].T for r in RANKS], axis=1)
        sel = jnp.take_along_axis(lora_outputs, selected[:, :, None], axis=1)
        final = jnp.sum(sel * routing_weights[:, :, None], axis=1)
        return out + final.reshape(bsz, seq, -1)
    x = x + jnp.tanh(g_xattn[0]) * _L0_xattn_ref(_layernorm(x, axis=-1), ctx_4096, L0_xattn_Wq, L0_xattn_Wk, L0_xattn_Wv, L0_xattn_Wo)
    x = x + jnp.tanh(g_ffn[0]) * _L0_ffn_ref(_layernorm(x, axis=-1), L0_ffn_weight_scales, L0_ffn_weight_q)
    x = x + jnp.tanh(g_xattn[1]) * _L1_xattn_ref(_layernorm(x, axis=-1), ctx_4096, L1_xattn_Wq, L1_xattn_bq, L1_xattn_Wk, L1_xattn_bk)
    x = x + jnp.tanh(g_ffn[1]) * _L1_ffn_ref(_layernorm(x, axis=-1), L1_ffn_W, L1_ffn_b, L1_ffn_A, L1_ffn_B, L1_ffn_gate_w, L1_ffn_gate_b)
    return x

_drawn_inputs = setup_inputs


def setup_inputs(seed=0):
    import zlib

    import numpy as np

    out = dict(_drawn_inputs(seed))
    spreads = {'g_ffn': (-1.0, 0.6), 'L1_xattn_bq': (0.0, 2.0), 'L1_xattn_bk': (0.0, 2.0)}
    factors = {'L1_xattn_Wq': 8.0,
     'L1_xattn_Wk': 8.0,
     'L1_ffn_W': 4.385,
     'L1_ffn_b': 64.0,
     'L1_ffn_A': 8.0,
     'L1_ffn_B': 8.0,
     'L1_ffn_gate_w': 8.0,
     'L1_ffn_gate_b': 34.626}
    for name, (base, spread) in spreads.items():
        noise = np.random.default_rng([zlib.crc32(name.encode()), seed]).standard_normal(out[name].shape)
        drawn = base * np.exp(spread * noise) if base else spread * noise
        out[name] = jnp.asarray(drawn.astype(out[name].dtype))
    for name, factor in factors.items():
        out[name] = (out[name] * factor).astype(out[name].dtype)
    return out
```

```python
from contextlib import ExitStack

import concourse.bass as bass
from concourse import mybir

F32 = mybir.dt.float32
F16 = mybir.dt.float16
BF16 = mybir.dt.bfloat16
I32 = mybir.dt.int32
ALU = mybir.AluOpType
ACT = mybir.ActivationFunctionType
AX = mybir.AxisListType

P = 128
B, Q, D = 16, 112, 1024
S = 375
R = B * Q
TILES = R // P
KD = D // P
H, KV, HD = 16, 4, 96
G = H // KV
QW, KW = H * HD, KV * HD
WA = QW + 2 * KW
KO = QW // P
SA = S + Q
LR = 64
NG = 4
RANKS = (8, 16, 32, 64)
CH = [(0, 128), (128, 128), (256, 119)]
HALF = 512
EPS = 1e-5
WS = 64.0
MS = 16.0
PASSES = ((0, 0), (0, 1), (1, 0))


def wait(eng, sem, value):
    if isinstance(value, int) and value <= 0:
        return
    eng.wait_ge(sem, value)


def run_slots(eng, slot, n, ends=2):
    for s in range(ends):
        slot(s // 2, s % 2, s)
    with eng.Fori(ends // 2, (n - ends) // 2) as j:
        for p in (0, 1):
            slot(j, p, 2 * j + p)
    for s in range(n - ends, n):
        slot(s // 2, s % 2, s)


def inside(t, n):
    return not isinstance(t, int) or 0 <= t < n


def rows(t, size):
    return bass.ds(t * size, size)


def layernorm(sb, sem, name, neg_half):
    stats = sb(name + "_stats", [P, 2, 6], F32)
    mean_var = sb(name + "_mean_var", [P, 2], F32)
    var_eps = sb(name + "_var_eps", [P, 1], F32)
    rstd = sb(name + "_rstd", [P, 1], F32)
    waited = sb(name + "_waited", [P, 1], F32)
    stats_done = sem(name + "_stats_done")
    aggr_done = sem(name + "_aggr_done")
    var_ready = sem(name + "_var_ready")
    rstd_ready = sem(name + "_rstd_ready")

    def measure(dve, x, n, t):
        for i in range(2):
            dve.bn_stats(stats[0:n, i, :], x[:, i * HALF:(i + 1) * HALF]).then_inc(stats_done, 1)
        dve.wait_ge(stats_done, 2 * t + 2)
        dve.memset(waited[:, :], 0.0)
        dve.bn_aggr(mean_var[0:n, :], stats[0:n, :, :]).then_inc(aggr_done, 1)
        dve.wait_ge(aggr_done, t + 1)
        dve.tensor_scalar(var_eps[0:n, :], mean_var[0:n, 1:2], EPS, None, ALU.add).then_inc(var_ready, 1)

    def root(pool, n, t):
        pool.wait_ge(var_ready, t + 1)
        pool.tensor_tensor(rstd[0:n, :], var_eps[0:n, :], neg_half[0:n, :], ALU.pow).then_inc(rstd_ready, 1)

    def scaled(dve, out, x, n, t):
        dve.wait_ge(rstd_ready, t + 1)
        return dve.tensor_scalar(out, x, mean_var[0:n, 0:1], rstd[0:n, 0:1], ALU.subtract, ALU.mult)

    return measure, root, scaled


def build(nc, x, ctx_nat, ctx_t, gates, wa, wo, q4, sc4, wq1, wk1, bq1, bk1, w1, b1, wag, wb, gate_b, out):
    qk_s = nc.dram_tensor("qk_scratch", [2, HD, H + KV, R], F16).ap()
    v_s = nc.dram_tensor("v_scratch", [R, 2, KW], F16).ap()
    o_s = nc.dram_tensor("o_scratch", [2, QW, R], F16).ap()
    t_s = nc.dram_tensor("t_scratch", [2, P, KD, R], F16).ap()
    x2_s = nc.dram_tensor("x2_scratch", [R, D + 4], F32).ap()

    with ExitStack() as whole:
        def alloc(scope):
            def sb(name, shape, dt):
                return scope.enter_context(nc.sbuf_tensor(name, shape, dt))

            def pb(name, shape, dt):
                return scope.enter_context(nc.psum_tensor(name, shape, dt))
            return sb, pb

        used = []

        def sem(name):
            used.append(nc.alloc_semaphore(name=name))
            return used[-1]

        def retire_semaphores():
            for s in used:
                nc.gpsimd.sem_clear(s)
                nc.release_semaphore(s)
            del used[:]

        sb, _ = alloc(whole)
        ident32 = sb("ident32", [P, P], F32)
        ident = sb("ident", [P, P], F16)
        identb = sb("identb", [P, P], BF16)
        neg_half = sb("neg_half", [P, 1], F32)
        tg = sb("tg", [P, 4], F32)
        tg_wo = sb("tg_wo", [P, 1], F32)
        tg_w1 = sb("tg_w1", [P, 1], F32)
        with ExitStack() as mid:
            sb, _ = alloc(mid)
            Mt = sb("Mt", [P, 2, KD, D], F16)
            c_bc = sb("c_bc", [P, D], F32)
            u_bc = sb("u_bc", [P, D], F32)
            s0 = sb("s0", [P, 1], F32)
            w4 = sb("w4", [P, KD, D], BF16)

            mm = nc.tensor.matmul

            with ExitStack() as st:
                sb, pb = alloc(st)
                raw_q = sb("raw_q", [P, KD, D], F32)
                raw_k = sb("raw_k", [P, KD, D], F32)
                wq_p = sb("wq_p", [P, 2, KD, D], F16)
                wk_p = sb("wk_p", [P, 2, KD, D], F16)
                gate_in = sb("gate_in", [P, 4], F32)
                bqk = sb("bqk", [P, 2, KD], F32)
                bqk_hi = sb("bqk_hi", [P, 2, KD], F16)
                bqk_lo32 = sb("bqk_lo32", [P, 2, KD], F32)
                bqk_hi32 = sb("bqk_hi32", [P, 2, KD], F32)
                bk_p = sb("bk_p", [P, 2, KD], F16)
                ones = sb("ones", [P, P], F32)
                bias_bc = sb("bias_bc", [P, 2, 2, KD, P], F16)
                codes = sb("codes", [P, D], I32)
                scale4 = sb("scale4", [P, D], F32)
                sign8, mag, over4, over6 = (raw_q[:, k, :] for k in range(4))
                m_ps = pb("m_ps", [P, 4, HALF], F32)
                b_ps = pb("b_ps", [P, 2, HALF], F32)
                s_ps = pb("s_ps", [P, HALF], F32)

                q_loaded, k_loaded = sem("z_q_loaded"), sem("z_k_loaded")
                small_loaded = sem("z_small_loaded")
                codes_loaded = sem("z_codes_loaded")
                ident_zero, ident_ready = sem("z_ident_zero"), sem("z_ident_ready")
                ident_cast = sem("z_ident_cast")
                half_ready = sem("z_half_ready")
                tanh_ready, tanh_scaled = sem("z_tanh_ready"), sem("z_tanh_scaled")
                w_hi, w_lo = sem("z_w_hi"), sem("z_w_lo")
                bias_split, bias_ready = sem("z_bias_split"), sem("z_bias_ready")
                m_done, m_hi, m_lo = sem("z_m_done"), sem("z_m_hi"), sem("z_m_lo")
                b_done, b_read = sem("z_b_done"), sem("z_b_read")
                deq = sem("z_deq")
                codes_free = sem("z_codes_free")

                block = st.enter_context(nc.Block())

                @block.sync
                def _(sp):
                    for k in range(KD):
                        sp.dma_start(raw_q[:, k, :], wq1[:, k, :]).then_inc(q_loaded, 16)
                        sp.dma_start(raw_k[:, k, :], wk1[:, k, :]).then_inc(k_loaded, 16)
                    for k in range(KD):
                        if k:
                            sp.wait_ge(codes_free, k)
                        sp.dma_start(codes[:, :], q4[:, k, :]).then_inc(codes_loaded, 16)
                        blocks = sc4[k * 8:(k + 1) * 8, :].rearrange("b o -> b () o").to_broadcast([8, 16, D])
                        sp.dma_start(scale4[:, :], blocks).then_inc(codes_loaded, 16)

                @block.gpsimd
                def _(pool):
                    pool.memset(ident32[:, :], 0.0).then_inc(ident_zero, 1)
                    pool.memset(neg_half[:, :], -0.5).then_inc(half_ready, 1)
                    pool.memset(ones[:, :], 1.0).then_inc(half_ready, 1)
                    pool.wait_ge(ident_zero, 1)
                    pool.affine_select(out=ident32[:, :], in_=ident32[:, :], compare_op=ALU.not_equal, fill=1.0,
                                       base=0, pattern=[[-1, P]], channel_multiplier=1).then_inc(ident_ready, 1)
                    pool.wait_ge(ident_ready, 1)
                    pool.tensor_copy(ident[:, :], ident32[:, :]).then_inc(ident_cast, 1)
                    pool.tensor_copy(identb[:, :], ident32[:, :]).then_inc(ident_cast, 1)

                @block.scalar
                def _(act):
                    act.dma_start(gate_in[:, :], gates.to_broadcast([P, 4])).then_inc(small_loaded, 16)
                    act.dma_start(bqk[:, 0, :], bq1).then_inc(small_loaded, 16)
                    act.dma_start(bqk[:, 1, :], bk1).then_inc(small_loaded, 16)
                    act.wait_ge(small_loaded, 48)
                    act.activation(tg[:, :], gate_in[:, :], ACT.Tanh).then_inc(tanh_ready, 1)
                    for k in range(KD):
                        act.wait_ge(q_loaded, 16 * KD) if k == 0 else None
                        act.activation(wq_p[:, 0, k, :], raw_q[:, k, :], ACT.Copy, scale=WS).then_inc(w_hi, 1)
                        act.wait_ge(k_loaded, 16 * KD) if k == 0 else None
                        act.activation(wk_p[:, 0, k, :], raw_k[:, k, :], ACT.Copy, scale=WS).then_inc(w_hi, 1)
                    for i in range(2 * KD):
                        m, h = divmod(i, 2)
                        act.wait_ge(m_done, i + 1)
                        act.activation(Mt[:, 0, m, h * HALF:(h + 1) * HALF], m_ps[:, i % 4, :], ACT.Copy,
                                       scale=MS / (WS * WS)).then_inc(m_hi, 1)
                    for i, dst in enumerate((c_bc, u_bc)):
                        for h in range(2):
                            act.wait_ge(b_done, 2 * i + h + 1)
                            act.activation(dst[:, h * HALF:(h + 1) * HALF], b_ps[:, h, :], ACT.Copy,
                                           scale=1.0 / WS).then_inc(b_read, 1)
                    act.wait_ge(b_done, 5)
                    act.activation(s0[:, :], s_ps[:, 0:1], ACT.Copy).then_inc(b_read, 1)

                @block.vector
                def _(dve):
                    dve.wait_ge(small_loaded, 48)
                    dve.tensor_copy(bqk_hi[:, :, :], bqk[:, :, :]).then_inc(bias_split, 1)
                    dve.wait_ge(bias_split, 1)
                    dve.tensor_copy(bqk_hi32[:, :, :], bqk_hi[:, :, :]).then_inc(bias_split, 1)
                    dve.tensor_tensor(bqk_lo32[:, :, :], bqk[:, :, :], bqk_hi[:, :, :], ALU.subtract).then_inc(bias_split, 1)
                    dve.wait_ge(bias_split, 3)
                    dve.tensor_copy(bk_p[:, 0, :], bqk_hi[:, 1, :]).then_inc(bias_ready, 1)
                    dve.tensor_copy(bk_p[:, 1, :], bqk_lo32[:, 1, :]).then_inc(bias_ready, 1)
                    dve.wait_ge(half_ready, 2)
                    for i in range(2):
                        for part, src in ((0, bqk_hi32), (1, bqk_lo32)):
                            for k in range(KD):
                                dve.tensor_scalar(bias_bc[:, i, part, k, :], ones[:, :], src[:, i, k:k + 1], None,
                                                  ALU.mult).then_inc(bias_ready, 1)
                    dve.wait_ge(tanh_ready, 1)
                    dve.tensor_scalar(tg_wo[:, :], tg[:, 0:1], 1.0 / WS, None, ALU.mult).then_inc(tanh_scaled, 1)
                    dve.tensor_scalar(tg_w1[:, :], tg[:, 3:4], 1.0 / WS, None, ALU.mult).then_inc(tanh_scaled, 1)
                    dve.wait_ge(q_loaded, 16 * KD)
                    dve.wait_ge(k_loaded, 16 * KD)
                    for k in range(KD):
                        for i, (w, raw) in enumerate(((wq_p, raw_q), (wk_p, raw_k))):
                            dve.wait_ge(w_hi, 2 * k + i + 1)
                            dve.scalar_tensor_tensor(out=w[:, 1, k, :], in0=raw[:, k, :], scalar=WS,
                                                     in1=w[:, 0, k, :], op0=ALU.mult,
                                                     op1=ALU.subtract).then_inc(w_lo, 1)
                    done = [0]

                    def step(ins):
                        ins.then_inc(deq, 1)
                        done[0] += 1
                        dve.wait_ge(deq, done[0])

                    dve.wait_ge(w_lo, 2 * KD)
                    for k in range(KD):
                        dve.wait_ge(codes_loaded, 32 * (k + 1))
                        step(dve.tensor_scalar(sign8[:, :], codes[:, :], 8.0, 8.0, ALU.is_ge, ALU.mult))
                        step(dve.tensor_tensor(mag[:, :], codes[:, :], sign8[:, :], ALU.subtract))
                        step(dve.tensor_scalar(over4[:, :], mag[:, :], 4.0, 0.0, ALU.subtract, ALU.max))
                        step(dve.tensor_scalar(over6[:, :], mag[:, :], 6.0, 0.0, ALU.subtract, ALU.max))
                        step(dve.scalar_tensor_tensor(out=over4[:, :], in0=over4[:, :], scalar=0.5, in1=over6[:, :],
                                                      op0=ALU.mult, op1=ALU.add))
                        step(dve.scalar_tensor_tensor(out=mag[:, :], in0=mag[:, :], scalar=0.5, in1=over4[:, :],
                                                      op0=ALU.mult, op1=ALU.add))
                        step(dve.tensor_scalar(sign8[:, :], sign8[:, :], -0.25, 1.0, ALU.mult, ALU.add))
                        step(dve.tensor_tensor(mag[:, :], mag[:, :], sign8[:, :], ALU.mult))
                        dve.tensor_tensor(w4[:, k, :], mag[:, :], scale4[:, :], ALU.mult).then_inc(codes_free, 1)
                        dve.wait_ge(codes_free, k + 1)
                        for i in (2 * k, 2 * k + 1):
                            m, h = divmod(i, 2)
                            dve.wait_ge(m_hi, i + 1)
                            dve.scalar_tensor_tensor(out=Mt[:, 1, m, h * HALF:(h + 1) * HALF], in0=m_ps[:, i % 4, :],
                                                     scalar=MS / (WS * WS), in1=Mt[:, 0, m, h * HALF:(h + 1) * HALF],
                                                     op0=ALU.mult, op1=ALU.subtract).then_inc(m_lo, 1)

                @block.tensor
                def _(pe):
                    pe.wait_ge(w_lo, 2 * KD)
                    for i in range(2 * KD):
                        m, h = divmod(i, 2)
                        wait(pe, m_lo, i - 3)
                        for n, (a, b) in enumerate(PASSES):
                            for k in range(KD):
                                last = mm(m_ps[:, i % 4, :], wq_p[:, a, k, m * P:(m + 1) * P],
                                          wk_p[:, b, k, h * HALF:(h + 1) * HALF],
                                          start=(n == 0 and k == 0), stop=(n == 2 and k == KD - 1))
                        last.then_inc(m_done, 1)
                    pe.wait_ge(bias_ready, 2 + 4 * KD)
                    for i, w in enumerate((wk_p, wq_p)):
                        for h in range(2):
                            wait(pe, b_read, 2 * (i - 1) + h + 1)
                            for n, (a, b) in enumerate(PASSES):
                                for k in range(KD):
                                    last = mm(b_ps[:, h, :], bias_bc[:, i, a, k, :], w[:, b, k, h * HALF:(h + 1) * HALF],
                                              start=(n == 0 and k == 0), stop=(n == 2 and k == KD - 1))
                            last.then_inc(b_done, 1)
                    for n, (a, b) in enumerate(PASSES):
                        for k in range(KD):
                            last = mm(s_ps[:, 0:1], bias_bc[:, 0, a, k, :], bk_p[:, b, k:k + 1],
                                      start=(n == 0 and k == 0), stop=(n == 2 and k == KD - 1))
                    last.then_inc(b_done, 1)

            retire_semaphores()

            with ExitStack() as ab:
                sb, _ = alloc(ab)
                wkv_p = sb("wkv_p", [P, 2, KD, 2 * KW], F16)

                NC = WA // KW
                HC = NC - 1
                with ExitStack() as st:
                    sb, pb = alloc(st)
                    wq_p = sb("a_wq_p", [P, 2, KD, QW], F16)
                    stage = sb("a_stage", [P, 2, WA], F32)
                    xin = sb("a_x", [P, 2, D], F32)
                    y = sb("a_y", [P, D], F32)
                    y_p = sb("a_y_p", [P, 2, D], F16)
                    yT = sb("a_yT", [P, 2, 2, KD, P], F16)
                    nat = sb("a_nat", [P, 2, 2, KW], F16)
                    heads = sb("a_heads", [HD, 2, 2, H + KV, P], F16)
                    val = sb("a_val", [P, 2, 2, KW], F16)
                    pr = pb("a_pr", [P, 3, HALF], F32)
                    tr = pb("a_tr", [P, 2, KD * P], F16)
                    ht = pb("a_ht", [P, 2, 2 * G * P], F16)

                    w_loaded = [sem(f"a_w_loaded{i}") for i in range(2)]
                    w_hi, w_lo = sem("a_w_hi"), sem("a_w_lo")
                    x_loaded = [sem(f"a_x_loaded{i}") for i in range(2)]
                    y_ready, yh_ready, yl_ready = sem("a_y_ready"), sem("a_yh_ready"), sem("a_yl_ready")
                    ytr_done, yT_hi, yT_lo = sem("a_ytr_done"), sem("a_yT_hi"), sem("a_yT_lo")
                    proj, hi, lo = sem("a_proj"), sem("a_hi"), sem("a_lo")
                    htr = sem("a_htr")
                    ht_read = [sem(f"a_ht_read{i}") for i in range(2)]
                    qk_stored = [sem(f"a_qk_stored{i}") for i in range(2)]
                    v_stored = [sem(f"a_v_stored{i}") for i in range(2)]
                    norm_measure, norm_root, norm_scaled = layernorm(sb, sem, "a_norm", neg_half)

                    def weight(part, k, c):
                        if c < QW // KW:
                            return wq_p[:, part, k, c * KW:(c + 1) * KW]
                        return wkv_p[:, part, k, (c - QW // KW) * KW:(c - QW // KW + 1) * KW]

                    def split_cols(k, part):
                        return ((wq_p[:, part, k, :], 0, QW), (wkv_p[:, part, k, :], QW, WA))

                    block = st.enter_context(nc.Block())

                    @block.sync
                    def _(sp):
                        for t in range(2):
                            sp.dma_start(xin[:, t, :], x[t * P:(t + 1) * P, :]).then_inc(x_loaded[t], 16)
                        for k in range(KD):
                            wait(sp, w_lo, 2 * (k - 1))
                            sp.dma_start(stage[:, k % 2, :], wa[:, k, :]).then_inc(w_loaded[k % 2], 16)

                        def slot(j, p, t):
                            if inside(t + 2, TILES):
                                sp.wait_ge(y_ready, t + 1)
                                sp.dma_start(xin[:, p, :], x[rows(t + 2, P), :]).then_inc(x_loaded[p], 16)
                            sp.wait_ge(lo, NC * (t + 1))
                            sp.dma_start(v_s[rows(t, P), :, :], val[:, p, :, :]).then_inc(v_stored[p], 16)

                        run_slots(sp, slot, TILES)
                        for p in range(2):
                            sp.wait_ge(v_stored[p], 16 * (TILES // 2))
                            sp.wait_ge(qk_stored[p], 32 * (TILES // 2))

                    @block.gpsimd
                    def _(pool):
                        def norm_of(t):
                            norm_root(pool, P, t)
                            pool.wait_ge(yh_ready, t + 1)
                            pool.tensor_tensor(y_p[:, 1, :], y[:, :], y_p[:, 0, :], ALU.subtract).then_inc(yl_ready, 1)

                        norm_of(0)

                        def slot(j, p, t):
                            if inside(t + 1, TILES):
                                norm_of(t + 1)

                        run_slots(pool, slot, TILES)

                    @block.scalar
                    def _(act):
                        def y_high(t):
                            act.wait_ge(y_ready, t + 1)
                            wait(act, ytr_done, t)
                            act.activation(y_p[:, 0, :], y[:, :], ACT.Copy).then_inc(yh_ready, 1)

                        def yT_high(p, t):
                            act.wait_ge(ytr_done, t + 1)
                            act.activation(yT[:, p, 0, :, :], tr[:, 0, :].rearrange("p (k r) -> p k r", k=KD),
                                           ACT.Copy).then_inc(yT_hi, 1)

                        y_high(0)
                        for k in range(KD):
                            act.wait_ge(w_loaded[k % 2], 16 * (k // 2 + 1))
                            for dst, a, b in split_cols(k, 0):
                                act.activation(dst, stage[:, k % 2, a:b], ACT.Copy, scale=WS).then_inc(w_hi, 1)
                        yT_high(0, 0)

                        def chunk(j, p, t, c):
                            act.wait_ge(proj, NC * t + c + 1)
                            if c < HC:
                                wait(act, htr, HC * t + c - 1)
                                dst = nat[:, (p + c) % 2, 0, :]
                            else:
                                wait(act, v_stored[p], 16 * j)
                                dst = val[:, p, 0, :]
                            scale = (1.0 if c >= QW // KW else HD ** -0.5) / WS
                            act.activation(dst, pr[:, c % 3, 0:KW], ACT.Copy, scale=scale).then_inc(hi, 1)

                        def head_read(j, p, t, c):
                            if (p + c) % 2 == 0:
                                act.wait_ge(htr, HC * t + c + 1)
                                if c < 2:
                                    wait(act, qk_stored[p], 32 * j)
                                act.activation(heads[:, p, :, G * c:G * (c + 1), :],
                                               ht[0:HD, 0, :].rearrange("d (l g r) -> d l g r", l=2, g=G),
                                               ACT.Copy).then_inc(ht_read[0], 1)

                        def store_heads(j, p, t):
                            n = HC * (p + 1)
                            act.wait_ge(ht_read[0], HC * j + (n + 1) // 2)
                            act.wait_ge(ht_read[1], HC * j + n // 2)
                            for part in range(2):
                                act.dma_start(qk_s[part, :, :, rows(t, P)], heads[:, p, part, :, :]).then_inc(qk_stored[p], 16)

                        def slot(j, p, t):
                            for c in range(NC):
                                chunk(j, p, t, c)
                                if c == 0 and inside(t - 1, TILES):
                                    store_heads(j - 1 + p, 1 - p, t - 1)
                                if c:
                                    head_read(j, p, t, c - 1)
                                if c == 0 and inside(t + 1, TILES):
                                    y_high(t + 1)
                                if c == 3 and inside(t + 1, TILES):
                                    yT_high(1 - p, t + 1)

                        run_slots(act, slot, TILES)
                        store_heads(TILES // 2 - 1, 1, TILES - 1)

                    @block.vector
                    def _(dve):
                        def y_of(j, p, t):
                            dve.wait_ge(x_loaded[p], 16 * (j + 1))
                            norm_measure(dve, xin[:, p, :], P, t)
                            wait(dve, yl_ready, t)
                            norm_scaled(dve, y[:, :], xin[:, p, :], P, t).then_inc(y_ready, 1)

                        def yT_low(p, t):
                            dve.wait_ge(ytr_done, t + 1)
                            dve.tensor_copy(yT[:, p, 1, :, :],
                                            tr[:, 1, :].rearrange("p (k r) -> p k r", k=KD)).then_inc(yT_lo, 1)

                        y_of(0, 0, 0)
                        for k in range(KD):
                            for i, ((dst, a, b), (high, _, _)) in enumerate(zip(split_cols(k, 1), split_cols(k, 0))):
                                dve.wait_ge(w_hi, 2 * k + i + 1)
                                dve.scalar_tensor_tensor(out=dst, in0=stage[:, k % 2, a:b], scalar=WS, in1=high,
                                                         op0=ALU.mult, op1=ALU.subtract).then_inc(w_lo, 1)
                        yT_low(0, 0)

                        def chunk(j, p, t, c):
                            dve.wait_ge(hi, NC * t + c + 1)
                            both = nat[:, (p + c) % 2, :, :] if c < HC else val[:, p, :, :]
                            scale = (1.0 if c >= QW // KW else HD ** -0.5) / WS
                            dve.scalar_tensor_tensor(out=both[:, 1, :], in0=pr[:, c % 3, 0:KW], scalar=scale,
                                                     in1=both[:, 0, :], op0=ALU.mult, op1=ALU.subtract).then_inc(lo, 1)

                        def head_read(j, p, t, c):
                            if (p + c) % 2 == 1:
                                dve.wait_ge(htr, HC * t + c + 1)
                                if c < 2:
                                    wait(dve, qk_stored[p], 32 * j)
                                dve.tensor_copy(heads[:, p, :, G * c:G * (c + 1), :],
                                                ht[0:HD, 1, :].rearrange("d (l g r) -> d l g r", l=2, g=G)
                                                ).then_inc(ht_read[1], 1)

                        def slot(j, p, t):
                            for c in range(NC):
                                chunk(j, p, t, c)
                                if c:
                                    head_read(j, p, t, c - 1)
                                if c == 0 and inside(t + 1, TILES):
                                    y_of(j + p, 1 - p, t + 1)
                                if c == 3 and inside(t + 1, TILES):
                                    yT_low(1 - p, t + 1)

                        run_slots(dve, slot, TILES)

                    @block.tensor
                    def _(pe):
                        def y_transposes(t):
                            pe.wait_ge(yl_ready, t + 1)
                            for part in range(2):
                                for k in range(KD):
                                    last = pe.transpose(tr[:, part, k * P:(k + 1) * P], y_p[:, part, k * P:(k + 1) * P],
                                                        ident[:, :])
                            last.then_inc(ytr_done, 1)

                        def project(j, p, t, c):
                            wait(pe, lo, NC * t + c - 2)
                            for n, (a, b) in enumerate(PASSES):
                                for k in range(KD):
                                    last = mm(pr[:, c % 3, 0:KW], yT[:, p, a, k, :], weight(b, k, c),
                                              start=(n == 0 and k == 0), stop=(n == 2 and k == KD - 1))
                            last.then_inc(proj, 1)

                        def head_transposes(j, p, t, c):
                            bank = (p + c) % 2
                            pe.wait_ge(lo, NC * t + c + 1)
                            n = HC * p + c
                            wait(pe, ht_read[bank], HC * j + n // 2)
                            for part in range(2):
                                for g in range(G):
                                    last = pe.transpose(ht[0:HD, bank, (part * G + g) * P:(part * G + g + 1) * P],
                                                        nat[:, bank, part, g * HD:(g + 1) * HD], ident[:, :])
                            last.then_inc(htr, 1)

                        y_transposes(0)
                        pe.wait_ge(w_lo, 2 * KD)

                        def slot(j, p, t):
                            pe.wait_ge(yT_hi, t + 1)
                            pe.wait_ge(yT_lo, t + 1)
                            for c in range(NC):
                                project(j, p, t, c)
                                if c:
                                    head_transposes(j, p, t, c - 1)
                                if c == 3 and inside(t + 1, TILES):
                                    y_transposes(t + 1)

                        run_slots(pe, slot, TILES)

                retire_semaphores()

                with ExitStack() as st:
                    sb, pb = alloc(st)
                    raw = sb("b_raw", [P, KD, S], F32)
                    cT = sb("b_cT", [P, 2, 2, KD, S + 1], F16)
                    kT = sb("b_kT", [HD, 2, 2, KV, SA + 1], F16)
                    vv = sb("b_v", [P, 2, 4, 2, KW], F16)
                    qT = sb("b_qT", [HD, 2, 2, H, Q], F16)
                    kn = sb("b_kn", [P, 2, KW], F16)
                    ex = sb("b_exp", [Q, 2, SA + 1], F32)
                    pn = sb("b_prob", [Q, 2, SA + 1], F32)
                    pp = sb("b_prob_p", [Q, 2, 2, SA + 1], F16)
                    pT = sb("b_probT", [P, 2, 2, 4, G, Q], F16)
                    oo = sb("b_o", [HD, 2, 2, G * Q], F16)
                    nmax = sb("b_nmax", [Q, 4], F32)
                    esum = sb("b_esum", [Q, 4], F32)
                    rsum = sb("b_rsum", [Q, 4], F32)
                    kv_ps = pb("b_kv_ps", [P, 2, HALF], F32)
                    s_ps = pb("b_s_ps", [P, 2, HALF], F32)
                    pt_ps = pb("b_pt_ps", [P, 2, 1024], F16)
                    o_ps = pb("b_o_ps", [P, HALF], F32)
                    kt_ps = pb("b_kt_ps", [P, 1024], F16)

                    raw_loaded = sem("b_raw_loaded")
                    q_loaded = [sem(f"b_q_loaded{i}") for i in range(2)]
                    kv_loaded = [sem(f"b_kv_loaded{i}") for i in range(2)]
                    split_hi, split_lo = sem("b_split_hi"), sem("b_split_lo")
                    kv_done, kv_hi, kv_lo = sem("b_kv_done"), sem("b_kv_hi"), sem("b_kv_lo")
                    ktr, kt_read = sem("b_ktr"), sem("b_kt_read")
                    scored, maxed, exped = sem("b_scored"), sem("b_maxed"), sem("b_exped")
                    inverted, normed, p_hi, p_lo = sem("b_inverted"), sem("b_normed"), sem("b_p_hi"), sem("b_p_lo")
                    ptr = sem("b_ptr")
                    pt_read = [sem(f"b_pt_read{i}") for i in range(2)]
                    pv, o_hi, o_lo = sem("b_pv"), sem("b_o_hi"), sem("b_o_lo")
                    o_stored = [sem(f"b_o_stored{i}") for i in range(2)]
                    pt_cleared = sem("b_pt_cleared")

                    BLOCK = 3 * KD
                    PER_STEP = 6 * BLOCK // H
                    READ_AT = [(BLOCK * (k + 1) - 1) // PER_STEP + 1 for k in range(6)]

                    def block_out(p, k, part):
                        n = CH[k % 3][1]
                        return kn[0:n, part, :] if k < 3 else vv[0:n, p, k - 3, part, :]

                    KEYS = [(Q + a, n) for a, n in CH] + [(0, Q)]

                    block = st.enter_context(nc.Block())

                    @block.sync
                    def _(sp):
                        def load_raw(b):
                            wait(sp, split_hi, KD * b)
                            wait(sp, split_lo, KD * b)
                            sp.dma_start(raw[:, :, :], ctx_t[bass.ds(b, 1), :, :, :].rearrange("b p k s -> p (b k) s")
                                         ).then_inc(raw_loaded, 16)

                        def load_latents(j, p, b):
                            wait(sp, pv, KV * (b - 1))
                            for part in range(2):
                                sp.dma_start(qT[:, p, part, :, :], qk_s[part, :, 0:H, rows(b, Q)]).then_inc(q_loaded[p], 16)
                                sp.dma_start(kT[:, p, part, :, 0:Q],
                                             qk_s[part, :, H:H + KV, rows(b, Q)]).then_inc(q_loaded[p], 16)
                            sp.dma_start(vv[0:Q, p, 3, :, :], v_s[rows(b, Q), :, :]).then_inc(kv_loaded[p], 16)

                        def store(b, g):
                            sp.wait_ge(o_lo, KV * b + g + 1)
                            for part in range(2):
                                dst = o_s[part, g * G * HD:(g + 1) * G * HD, rows(b, Q)].rearrange("(h d) r -> d h r", h=G)
                                src = oo[:, g % 2, part, :].rearrange("d (h r) -> d h r", h=G)
                                sp.dma_start(dst, src).then_inc(o_stored[g % 2], 16)

                        load_raw(0)
                        load_latents(0, 0, 0)
                        load_raw(1)
                        load_latents(0, 1, 1)

                        def slot(j, p, b):
                            if inside(b - 1, B):
                                store(b - 1, KV - 1)
                                if inside(b + 1, B):
                                    load_latents(j, 1 - p, b + 1)
                            if inside(b + 2, B):
                                load_raw(b + 2)
                            for g in range(KV - 1):
                                store(b, g)

                        run_slots(sp, slot, B)
                        store(B - 1, KV - 1)
                        for i in range(2):
                            sp.wait_ge(o_stored[i], 32 * B * KV // 2)

                    @block.gpsimd
                    def _(pool):
                        def split_piece(p, b, k):
                            if k == 0:
                                wait(pool, kv_done, 6 * (b - 1))
                            pool.wait_ge(split_hi, KD * b + k + 1)
                            pool.tensor_tensor(cT[:, p, 1, k, 0:S], raw[:, k, :], cT[:, p, 0, k, 0:S],
                                               ALU.subtract).then_inc(split_lo, 1)

                        def prob_low(b, h):
                            n = H * b + h
                            pool.wait_ge(p_hi, n + 1)
                            wait(pool, ptr, n - 1)
                            pool.tensor_tensor(pp[:, h % 2, 1, 0:SA], pn[:, h % 2, 0:SA], pp[:, h % 2, 0, 0:SA],
                                               ALU.subtract).then_inc(p_lo, 1)

                        for b in range(2):
                            for k in range(KD):
                                split_piece(b, b, k)
                        prob_low(0, 0)

                        def slot(j, p, b):
                            for i in range(H):
                                if i < H - 1:
                                    prob_low(b, i + 1)
                                elif inside(b + 1, B):
                                    prob_low(b + 1, 0)
                                if 4 <= i < 4 + KD and inside(b + 2, B):
                                    split_piece(p, b + 2, i - 4)

                        run_slots(pool, slot, B)

                    @block.scalar
                    def _(act):
                        def split_piece(p, b, k):
                            if k == 0:
                                act.wait_ge(raw_loaded, 16 * (b + 1))
                                wait(act, kv_done, 6 * (b - 1))
                            act.activation(cT[:, p, 0, k, 0:S], raw[:, k, :], ACT.Copy).then_inc(split_hi, 1)

                        def block_high(p, b, k):
                            n = CH[k % 3][1]
                            act.wait_ge(kv_done, 6 * b + k + 1)
                            if k < 3:
                                wait(act, ktr, 3 * b + k)
                            act.activation(block_out(p, k, 0), kv_ps[0:n, k % 2, 0:KW], ACT.Copy, scale=1.0 / WS).then_inc(kv_hi, 1)

                        def keys_read(p, b, c):
                            a, n = KEYS[c]
                            act.wait_ge(ktr, 3 * b + c + 1)
                            act.activation(kT[:, p, :, :, a:a + n],
                                           kt_ps[0:HD, :].rearrange("d (l g r) -> d l g r", l=2, g=KV)[:, :, :, 0:n],
                                           ACT.Copy).then_inc(kt_read, 1)

                        def exponent(b, h):
                            n = H * b + h
                            act.wait_ge(maxed, n + 1)
                            wait(act, normed, n - 1)
                            act.activation(ex[:, h % 2, 0:SA], s_ps[0:Q, h % 2, 0:SA], ACT.Exp, bias=nmax[:, h % 4:h % 4 + 1],
                                           accum_out=esum[:, h % 4:h % 4 + 1]).then_inc(exped, 1)

                        def probs_read(j, p, b, h):
                            if h % 2 == 0:
                                act.wait_ge(ptr, H * b + h + 1)
                                g = h // G
                                wait(act, pv, KV * b + g - 1)
                                act.activation(pT[:, g % 2, :, :, h % G, :],
                                               pt_ps[:, 0, 0:8 * Q].rearrange("s (l c r) -> s l c r", l=2, c=4),
                                               ACT.Copy).then_inc(pt_read[0], 1)

                        def out_high(b, g):
                            act.wait_ge(pv, KV * b + g + 1)
                            wait(act, o_stored[g % 2], 32 * (2 * b + g // 2))
                            act.activation(oo[:, g % 2, 0, :], o_ps[0:HD, 0:G * Q], ACT.Copy).then_inc(o_hi, 1)

                        for b in range(2):
                            for k in range(KD):
                                split_piece(b, b, k)
                        for k in range(6):
                            block_high(0, 0, k)
                            if k < 3:
                                keys_read(0, 0, k)
                        for h in range(2):
                            exponent(0, h)

                        def slot(j, p, b):
                            for i in range(H):
                                if i == 0 and inside(b - 1, B):
                                    block_high(p, b, 5)
                                if i in READ_AT and inside(b + 1, B):
                                    block_high(1 - p, b + 1, READ_AT.index(i))
                                if i < H - 2:
                                    exponent(b, i + 2)
                                elif inside(b + 1, B):
                                    exponent(b + 1, i + 2 - H)
                                probs_read(j, p, b, i)
                                if i - 2 in READ_AT[0:3] and inside(b + 1, B):
                                    keys_read(1 - p, b + 1, READ_AT.index(i - 2))
                                if i % G == 0:
                                    if i:
                                        out_high(b, i // G - 1)
                                    elif inside(b - 1, B):
                                        out_high(b - 1, KV - 1)
                                if 4 <= i < 4 + KD and inside(b + 2, B):
                                    split_piece(p, b + 2, i - 4)

                        run_slots(act, slot, B)
                        out_high(B - 1, KV - 1)

                    @block.vector
                    def _(dve):
                        for i in range(2):
                            dve.memset(pt_ps[:, i, :].bitcast(F32), 0.0).then_inc(pt_cleared, 1)

                        def block_low(p, b, k):
                            n = CH[k % 3][1]
                            dve.wait_ge(kv_hi, 6 * b + k + 1)
                            dve.scalar_tensor_tensor(out=block_out(p, k, 1), in0=kv_ps[0:n, k % 2, 0:KW], scalar=1.0 / WS,
                                                         in1=block_out(p, k, 0), op0=ALU.mult, op1=ALU.subtract).then_inc(kv_lo, 1)

                        def maximum(b, h):
                            dve.wait_ge(scored, H * b + h + 1)
                            wait(dve, exped, H * b + h - 3)
                            dve.tensor_reduce(nmax[:, h % 4:h % 4 + 1], s_ps[0:Q, h % 2, 0:SA], AX.X, ALU.max,
                                              negate=True).then_inc(maxed, 1)

                        def normalize(b, h):
                            n = H * b + h
                            c = h % 4
                            dve.wait_ge(exped, n + 1)
                            dve.reciprocal(rsum[:, c:c + 1], esum[:, c:c + 1]).then_inc(inverted, 1)
                            dve.wait_ge(inverted, n + 1)
                            wait(dve, p_lo, n - 1)
                            dve.tensor_scalar(pn[:, h % 2, 0:SA], ex[:, h % 2, 0:SA], rsum[:, c:c + 1], None,
                                              ALU.mult).then_inc(normed, 1)
                            dve.wait_ge(normed, n + 1)
                            wait(dve, ptr, n - 1)
                            dve.tensor_copy(pp[:, h % 2, 0, 0:SA], pn[:, h % 2, 0:SA]).then_inc(p_hi, 1)

                        def probs_read(j, p, b, h):
                            if h % 2 == 1:
                                dve.wait_ge(ptr, H * b + h + 1)
                                g = h // G
                                wait(dve, pv, KV * b + g - 1)
                                dve.tensor_copy(pT[:, g % 2, :, :, h % G, :],
                                                pt_ps[:, 1, 0:8 * Q].rearrange("s (l c r) -> s l c r", l=2, c=4)
                                                ).then_inc(pt_read[1], 1)

                        def out_low(b, g):
                            dve.wait_ge(o_hi, KV * b + g + 1)
                            dve.tensor_tensor(oo[:, g % 2, 1, :], o_ps[0:HD, 0:G * Q], oo[:, g % 2, 0, :],
                                              ALU.subtract).then_inc(o_lo, 1)

                        for k in range(6):
                            block_low(0, 0, k)
                        for h in range(2):
                            maximum(0, h)
                        normalize(0, 0)

                        def slot(j, p, b):
                            for i in range(H):
                                if i < H - 1:
                                    normalize(b, i + 1)
                                elif inside(b + 1, B):
                                    normalize(b + 1, 0)
                                if i == 0 and inside(b - 1, B):
                                    block_low(p, b, 5)
                                if i in READ_AT and inside(b + 1, B):
                                    block_low(1 - p, b + 1, READ_AT.index(i))
                                if i < H - 2:
                                    maximum(b, i + 2)
                                elif inside(b + 1, B):
                                    maximum(b + 1, i + 2 - H)
                                probs_read(j, p, b, i)
                                if i % G == 0:
                                    if i:
                                        out_low(b, i // G - 1)
                                    elif inside(b - 1, B):
                                        out_low(b - 1, KV - 1)

                        run_slots(dve, slot, B)
                        out_low(B - 1, KV - 1)

                    @block.tensor
                    def _(pe):
                        def project(p, b, step, count):
                            for m in range(step * count, (step + 1) * count):
                                k, r = divmod(m, BLOCK)
                                i, d = divmod(r, KD)
                                a, n = CH[k % 3]
                                if m == 0:
                                    pe.wait_ge(split_lo, KD * (b + 1))
                                if r == 0:
                                    wait(pe, kv_lo, 6 * b + k - 1)
                                u, w = PASSES[i]
                                last = mm(kv_ps[0:n, k % 2, 0:KW], cT[:, p, u, d, a:a + n],
                                          wkv_p[:, w, d, (k // 3) * KW:(k // 3 + 1) * KW], start=(r == 0), stop=(r == BLOCK - 1))
                                if r == BLOCK - 1:
                                    last.then_inc(kv_done, 1)

                        def key_transposes(b, c):
                            n = CH[c][1]
                            pe.wait_ge(kv_lo, 6 * b + c + 1)
                            wait(pe, kt_read, 3 * b + c)
                            for part in range(2):
                                for g in range(KV):
                                    o = (part * KV + g) * P
                                    last = pe.transpose(kt_ps[0:HD, o:o + n], kn[0:n, part, g * HD:(g + 1) * HD],
                                                        ident[0:n, 0:n])
                            last.then_inc(ktr, 1)

                        def scores(j, p, b, h):
                            n = H * b + h
                            if h == 0:
                                pe.wait_ge(kt_read, 3 * (b + 1))
                                pe.wait_ge(q_loaded[p], 64 * (j + 1))
                            wait(pe, exped, n - 1)
                            for i, (u, w) in enumerate(PASSES):
                                last = mm(s_ps[0:Q, h % 2, 0:SA], qT[:, p, u, h, :], kT[:, p, w, h // G, 0:SA],
                                          start=(i == 0), stop=(i == 2))
                            last.then_inc(scored, 1)

                        def prob_transposes(j, p, b, h):
                            pe.wait_ge(p_lo, H * b + h + 1)
                            wait(pe, pt_read[h % 2], 8 * b + h // 2)
                            for part in range(2):
                                for c, (a, n) in enumerate(KEYS):
                                    o = (part * 4 + c) * Q
                                    last = pe.transpose(pt_ps[0:n, h % 2, o:o + Q], pp[:, h % 2, part, a:a + n],
                                                        ident[0:Q, 0:Q])
                            last.then_inc(ptr, 1)

                        def attend(j, p, b, g):
                            if g == 0:
                                pe.wait_ge(kv_lo, 6 * (b + 1))
                                pe.wait_ge(kv_loaded[p], 16 * (j + 1))
                            for i in range(2):
                                pe.wait_ge(pt_read[i], 8 * b + 2 * g + 2)
                            wait(pe, o_lo, KV * b + g)
                            for i, (u, w) in enumerate(PASSES):
                                for c, (a, n) in enumerate(KEYS):
                                    last = mm(o_ps[0:HD, 0:G * Q], vv[0:n, p, c, u, g * HD:(g + 1) * HD],
                                              pT[0:n, g % 2, w, c, :, :],
                                              start=(i == 0 and c == 0), stop=(i == 2 and c == 3))
                            last.then_inc(pv, 1)

                        for k in range(6):
                            project(0, 0, k, BLOCK)
                            if k < 3:
                                key_transposes(0, k)
                        for h in range(2):
                            scores(0, 0, 0, h)
                        pe.wait_ge(pt_cleared, 2)

                        def slot(j, p, b):
                            for i in range(H):
                                if i < H - 2:
                                    scores(j, p, b, i + 2)
                                elif inside(b + 1, B):
                                    scores(j + p, 1 - p, b + 1, i + 2 - H)
                                prob_transposes(j, p, b, i)
                                if i % G == 0:
                                    if i:
                                        attend(j, p, b, i // G - 1)
                                    elif inside(b - 1, B):
                                        attend(j - 1 + p, 1 - p, b - 1, KV - 1)
                                if i - 1 in READ_AT[0:3] and inside(b + 1, B):
                                    key_transposes(b + 1, READ_AT.index(i - 1))
                                if inside(b + 1, B):
                                    project(1 - p, b + 1, i, PER_STEP)

                        run_slots(pe, slot, B)
                        attend(B // 2 - 1, 1, B - 1, KV - 1)

                del used[:]

            with ExitStack() as st:
                sb, pb = alloc(st)
                wo_p = sb("c_wo_p", [P, 2, KO, D], F16)
                stage = sb("c_stage", [P, 4, D], F32)
                xin = sb("c_x", [P, 2, D], F32)
                oT = sb("c_oT", [P, 2, 2, KO, P], F16)
                x1 = sb("c_x1", [P, 2, D], F32)
                y1 = sb("c_y1", [P, D], BF16)
                y1T = sb("c_y1T", [P, KD * P], BF16)
                f_b = sb("c_f", [P, 2, HALF], BF16)
                x2 = sb("c_x2", [P, 2, D + 4], F32)
                y2 = sb("c_y2", [P, D], F32)
                y2_p = sb("c_y2_p", [P, 2, D], F16)
                y2T = sb("c_y2T", [P, 2, KD * P], F16)
                t32 = sb("c_t32", [P, D], F32)
                t_p = sb("c_t_p", [P, 2, D], F16)
                tT = sb("c_tT", [P, 2, KD * P], F16)
                junk = sb("c_junk", [P, D], F32)
                qb = sb("c_qb", [P, 1], F32)
                x_ps = pb("c_x_ps", [P, 2, HALF], F32)
                f_ps = pb("c_f_ps", [P, 2, HALF], F32)
                t_ps = pb("c_t_ps", [P, 2, HALF], F32)
                tr = pb("c_tr", [P, 2, 1024], F16)

                w_loaded = [sem(f"c_w_loaded{i}") for i in range(4)]
                w_hi, w_lo = sem("c_w_hi"), sem("c_w_lo")
                x_loaded = [sem(f"c_x_loaded{i}") for i in range(2)]
                o_loaded = [sem(f"c_o_loaded{i}") for i in range(2)]
                wo_done, x1_ready = sem("c_wo_done"), sem("c_x1_ready")
                y1_ready, y1tr, y1T_ready = sem("c_y1_ready"), sem("c_y1tr"), sem("c_y1T_ready")
                f_done, f_read, x2_ready = sem("c_f_done"), sem("c_f_read"), sem("c_x2_ready")
                y2_ready, y2_hi, y2_lo = sem("c_y2_ready"), sem("c_y2_hi"), sem("c_y2_lo")
                y2tr, y2T_hi, y2T_lo = sem("c_y2tr"), sem("c_y2T_hi"), sem("c_y2T_lo")
                dotted, qb_ready = sem("c_dotted"), sem("c_qb_ready")
                t_done, t32_ready, t_hi, t_lo = sem("c_t_done"), sem("c_t32_ready"), sem("c_t_hi"), sem("c_t_lo")
                ttr, tT_hi, tT_lo = sem("c_ttr"), sem("c_tT_hi"), sem("c_tT_lo")
                x2_stored = [sem(f"c_x2_stored{i}") for i in range(2)]
                t_stored = sem("c_t_stored")
                norm1_measure, norm1_root, norm1_scaled = layernorm(sb, sem, "c_norm1", neg_half)
                norm2_measure, norm2_root, norm2_scaled = layernorm(sb, sem, "c_norm2", neg_half)

                SLOTS = TILES + 2

                block = st.enter_context(nc.Block())

                @block.sync
                def _(sp):
                    def load(j, p, t):
                        wait(sp, x1_ready, 2 * (t - 1))
                        sp.dma_start(xin[:, p, :], x[rows(t, P), :]).then_inc(x_loaded[p], 16)
                        for part in range(2):
                            sp.dma_start(oT[:, p, part, :, :], o_s[part, :, rows(t, P)].rearrange(
                                "(k p) r -> p k r", p=P)).then_inc(o_loaded[p], 16)

                    load(0, 0, 0)
                    for k in range(KO):
                        wait(sp, w_lo, k - 3)
                        sp.dma_start(stage[:, k % 4, :], wo[:, k, :]).then_inc(w_loaded[k % 4], 16)
                    load(0, 1, 1)

                    def slot(j, p, s):
                        if inside(s, TILES) and inside(s + 1, TILES) and not (isinstance(s, int) and s == 0):
                            load(j + p, 1 - p, s + 1)
                        if inside(s - 1, TILES):
                            sp.wait_ge(x2_ready, 2 * s)
                            sp.wait_ge(qb_ready, s)
                            sp.dma_start(x2_s[rows(s - 1, P), 0:D + 1], x2[:, 1 - p, 0:D + 1]
                                         ).then_inc(x2_stored[1 - p], 16)

                    run_slots(sp, slot, SLOTS, 4)
                    for i in range(2):
                        sp.wait_ge(x2_stored[i], 16 * (TILES // 2))
                    sp.wait_ge(t_stored, 32 * TILES)

                @block.gpsimd
                def _(pool):
                    def slot(j, p, s):
                        if inside(s - 2, TILES):
                            pool.wait_ge(t_hi, s - 1)
                            pool.tensor_tensor(t_p[:, 1, :], t32[:, :], t_p[:, 0, :], ALU.subtract).then_inc(t_lo, 1)
                        if inside(s - 1, TILES):
                            norm2_root(pool, P, s - 1)
                            pool.wait_ge(y2_hi, s)
                            pool.tensor_tensor(y2_p[:, 1, :], y2[:, :], y2_p[:, 0, :], ALU.subtract).then_inc(y2_lo, 1)
                        if inside(s, TILES):
                            norm1_root(pool, P, s)

                    run_slots(pool, slot, SLOTS, 4)

                @block.scalar
                def _(act):
                    for k in range(KO):
                        act.wait_ge(w_loaded[k % 4], 16 * (k // 4 + 1))
                        act.activation(wo_p[:, 0, k, :], stage[:, k % 4, :], ACT.Copy, scale=WS).then_inc(w_hi, 1)

                    def slot(j, p, s):
                        if inside(s - 1, TILES):
                            act.wait_ge(y1tr, s)
                            act.activation(y1T[:, :], tr[:, 0, :].bitcast(BF16), ACT.Copy).then_inc(y1T_ready, 1)
                        if inside(s - 2, TILES):
                            act.wait_ge(t32_ready, 2 * (s - 1))
                            wait(act, ttr, s - 2)
                            act.activation(t_p[:, 0, :], t32[:, :], ACT.Copy).then_inc(t_hi, 1)
                        if inside(s - 1, TILES):
                            for h in range(2):
                                act.wait_ge(f_done, 2 * (s - 1) + h + 1)
                                wait(act, x2_ready, 2 * (s - 2) + h + 1)
                                act.activation(f_b[:, h, :], f_ps[:, h, :], ACT.Copy).then_inc(f_read, 1)
                        if inside(s - 2, TILES):
                            act.wait_ge(ttr, s - 1)
                            wait(act, t_stored, 32 * (s - 2))
                            act.activation(tT[:, 0, :], tr[:, 0, :], ACT.Copy).then_inc(tT_hi, 1)
                        if inside(s - 1, TILES):
                            act.wait_ge(y2_ready, s)
                            wait(act, y2tr, s - 1)
                            act.activation(y2_p[:, 0, :], y2[:, :], ACT.Copy).then_inc(y2_hi, 1)
                        if inside(s - 2, TILES):
                            act.wait_ge(tT_hi, s - 1)
                            act.wait_ge(tT_lo, s - 1)
                            for part in range(2):
                                act.dma_start(t_s[part, :, :, rows(s - 2, P)],
                                              tT[:, part, :].rearrange("p (k r) -> p k r", k=KD)).then_inc(t_stored, 16)
                        if inside(s - 1, TILES):
                            act.wait_ge(y2tr, s)
                            act.activation(y2T[:, 0, :], tr[:, 0, :], ACT.Copy).then_inc(y2T_hi, 1)

                    run_slots(act, slot, SLOTS, 4)

                @block.vector
                def _(dve):
                    for k in range(KO):
                        dve.wait_ge(w_hi, k + 1)
                        dve.scalar_tensor_tensor(out=wo_p[:, 1, k, :], in0=stage[:, k % 4, :], scalar=WS,
                                                 in1=wo_p[:, 0, k, :], op0=ALU.mult, op1=ALU.subtract).then_inc(w_lo, 1)

                    def residual1(j, p, t, h):
                        cols = slice(h * HALF, (h + 1) * HALF)
                        if h == 0:
                            dve.wait_ge(x_loaded[p], 16 * (j + 1))
                        dve.wait_ge(wo_done, 2 * t + h + 1)
                        dve.scalar_tensor_tensor(out=x1[:, p, cols], in0=x_ps[:, h, :], scalar=tg_wo[:, :],
                                                 in1=xin[:, p, cols], op0=ALU.mult, op1=ALU.add).then_inc(x1_ready, 1)

                    def slot(j, p, s):
                        if inside(s, TILES):
                            residual1(j, p, s, 0)
                        if inside(s - 1, TILES):
                            t = s - 1
                            if inside(t - 2, TILES):
                                dve.wait_ge(x2_stored[1 - p], 16 * (j - 1 + p))
                            for h in range(2):
                                cols = slice(h * HALF, (h + 1) * HALF)
                                dve.wait_ge(f_read, 2 * t + h + 1)
                                dve.scalar_tensor_tensor(out=x2[:, 1 - p, cols], in0=f_b[:, h, :], scalar=tg[:, 1:2],
                                                         in1=x1[:, 1 - p, cols], op0=ALU.mult, op1=ALU.add
                                                         ).then_inc(x2_ready, 1)
                            dve.wait_ge(x2_ready, 2 * t + 2)
                            norm2_measure(dve, x2[:, 1 - p, 0:D], P, t)
                            wait(dve, y2_lo, t)
                            norm2_scaled(dve, y2[:, :], x2[:, 1 - p, 0:D], P, t).then_inc(y2_ready, 1)
                        if inside(s - 2, TILES):
                            dve.wait_ge(ttr, s - 1)
                            wait(dve, t_stored, 32 * (s - 2))
                            dve.tensor_copy(tT[:, 1, :], tr[:, 1, :]).then_inc(tT_lo, 1)
                        if inside(s - 1, TILES):
                            dve.wait_ge(y2_ready, s)
                            dve.tensor_tensor_reduce(out=junk[:, :], in0=y2[:, :], in1=u_bc[:, :], scale=1.0, scalar=0.0,
                                                     op0=ALU.mult, op1=ALU.add, accum_out=qb[:, :]).then_inc(dotted, 1)
                            dve.wait_ge(dotted, s)
                            dve.tensor_scalar(x2[:, 1 - p, D:D + 1], qb[:, :], s0[:, 0:1], None,
                                              ALU.add).then_inc(qb_ready, 1)
                        if inside(s, TILES):
                            residual1(j, p, s, 1)
                            dve.wait_ge(x1_ready, 2 * s + 2)
                            norm1_measure(dve, x1[:, p, :], P, s)
                        if inside(s - 1, TILES):
                            dve.wait_ge(y2tr, s)
                            dve.tensor_copy(y2T[:, 1, :], tr[:, 1, :]).then_inc(y2T_lo, 1)
                        if inside(s, TILES):
                            wait(dve, y1tr, s)
                            norm1_scaled(dve, y1[:, :], x1[:, p, :], P, s).then_inc(y1_ready, 1)
                        if inside(s - 1, TILES):
                            wait(dve, t_lo, s - 1)
                            for h in range(2):
                                cols = slice(h * HALF, (h + 1) * HALF)
                                dve.wait_ge(t_done, 2 * (s - 1) + h + 1)
                                dve.scalar_tensor_tensor(out=t32[:, cols], in0=t_ps[:, h, :], scalar=1.0 / MS,
                                                         in1=c_bc[:, cols], op0=ALU.mult, op1=ALU.add
                                                         ).then_inc(t32_ready, 1)

                    run_slots(dve, slot, SLOTS, 4)

                @block.tensor
                def _(pe):
                    def out_proj(j, p, t, h):
                        if h == 0:
                            pe.wait_ge(o_loaded[p], 32 * (j + 1))
                        wait(pe, x1_ready, 2 * (t - 1) + h + 1)
                        for n, (a, b) in enumerate(PASSES):
                            for k in range(KO):
                                last = mm(x_ps[:, h, :], oT[:, p, a, k, :], wo_p[:, b, k, h * HALF:(h + 1) * HALF],
                                          start=(n == 0 and k == 0), stop=(n == 2 and k == KO - 1))
                        last.then_inc(wo_done, 1)

                    def both_parts(src, done):
                        for part in range(2):
                            for k in range(KD):
                                last = pe.transpose(tr[:, part, k * P:(k + 1) * P], src[:, part, k * P:(k + 1) * P],
                                                    ident[:, :])
                        last.then_inc(done, 1)

                    pe.wait_ge(w_lo, KO)

                    def slot(j, p, s):
                        if inside(s - 1, TILES):
                            pe.wait_ge(y1_ready, s)
                            for k in range(KD):
                                last = pe.transpose(tr[:, 0, k * P:(k + 1) * P].bitcast(BF16), y1[:, k * P:(k + 1) * P],
                                                    identb[:, :])
                            last.then_inc(y1tr, 1)
                        if inside(s, TILES):
                            out_proj(j, p, s, 0)
                        if inside(s - 1, TILES):
                            pe.wait_ge(y1T_ready, s)
                            for h in range(2):
                                wait(pe, f_read, 2 * (s - 2) + h + 1)
                                for k in range(KD):
                                    last = mm(f_ps[:, h, :], y1T[:, k * P:(k + 1) * P], w4[:, k, h * HALF:(h + 1) * HALF],
                                              start=(k == 0), stop=(k == KD - 1))
                                last.then_inc(f_done, 1)
                        if inside(s - 2, TILES):
                            pe.wait_ge(t_lo, s - 1)
                            both_parts(t_p, ttr)
                        if inside(s, TILES):
                            out_proj(j, p, s, 1)
                        if inside(s - 1, TILES):
                            pe.wait_ge(y2_lo, s)
                            if inside(s - 2, TILES):
                                pe.wait_ge(tT_hi, s - 1)
                                pe.wait_ge(tT_lo, s - 1)
                            both_parts(y2_p, y2tr)
                            pe.wait_ge(y2T_hi, s)
                            pe.wait_ge(y2T_lo, s)
                            for h in range(2):
                                wait(pe, t32_ready, 2 * (s - 2) + h + 1)
                                for n, (a, b) in enumerate(PASSES):
                                    for k in range(KD):
                                        last = mm(t_ps[:, h, :], y2T[:, a, k * P:(k + 1) * P],
                                                  Mt[:, b, k, h * HALF:(h + 1) * HALF],
                                                  start=(n == 0 and k == 0), stop=(n == 2 and k == KD - 1))
                                last.then_inc(t_done, 1)

                    run_slots(pe, slot, SLOTS, 4)


        AG = LR + NG
        with ExitStack() as st:
            sb, pb = alloc(st)
            w1_p = sb("d_w1_p", [P, 2, KD, D], F16)
            wag_p = sb("d_wag_p", [P, 2, KD, AG], F16)
            wb_p = sb("d_wb_p", [LR, 2, D], F16)
            stage = sb("d_stage", [P, 2, D], F32)
            ag_in = sb("d_ag_in", [P, KD, AG], F32)
            b_in = sb("d_b_in", [LR, D], F32)
            tg_b = sb("d_tg_b", [P, D], F32)
            gate_bias = sb("d_gate_bias", [P, NG], F32)
            cn_raw = sb("d_cn_raw", [P, 3, D], F32)
            ct_raw = sb("d_ct_raw", [P, KD, S], F32)
            cn = sb("d_cn", [P, 2, 3, D], F16)
            cT = sb("d_cT", [P, 2, KD, S + 1], F16)
            tT = sb("d_tT", [P, 2, 2, KD, Q], F16)
            x2 = sb("d_x2", [Q, 2, D + 4], F32)
            ex = sb("d_exp", [Q, S + 1], F32)
            pn = sb("d_prob", [Q, S + 1], F32)
            pp = sb("d_prob_p", [Q, 2, S + 1], F16)
            pT = sb("d_probT", [P, 2, 3, Q], F16)
            x3 = sb("d_x3", [Q, D], F32)
            x3b = sb("d_x3b", [Q, 2, D], F32)
            y3 = sb("d_y3", [Q, D], F32)
            y3_p = sb("d_y3_p", [Q, 2, D], F16)
            y3T = sb("d_y3T", [P, 2, KD, Q], F16)
            low = sb("d_low", [Q, LR], F32)
            low_p = sb("d_low_p", [Q, 2, P], F16)
            lowT = sb("d_lowT", [LR, 2, Q], F16)
            sm = sb("d_small", [Q, 24], F32)
            gs = sb("d_gs", [Q, NG], F32)
            gp = sb("d_gp", [Q, NG], F32)
            res = sb("d_res", [Q, 2, D], F32)
            s_ps = pb("d_s_ps", [P, HALF], F32)
            a_ps = pb("d_a_ps", [P, 2, HALF], F32)
            f_ps = pb("d_f_ps", [P, 2, HALF], F32)
            ag_ps = pb("d_ag_ps", [P, HALF], F32)
            tr = pb("d_tr", [P, 2, 1024], F16)

            w_loaded = [sem(f"d_w_loaded{i}") for i in range(2)]
            w_hi, w_lo = sem("d_w_hi"), sem("d_w_lo")
            small_loaded, small_split, small_ready = sem("d_small_loaded"), sem("d_small_split"), sem("d_small_ready")
            cn_loaded, ct_loaded = sem("d_cn_loaded"), sem("d_ct_loaded")
            tx_loaded = [sem(f"d_tx_loaded{i}") for i in range(2)]
            cn_hi, cn_lo, ct_hi, ct_lo = sem("d_cn_hi"), sem("d_cn_lo"), sem("d_ct_hi"), sem("d_ct_lo")
            scored, maxed, biased, exped = sem("d_scored"), sem("d_maxed"), sem("d_biased"), sem("d_exped")
            shifted = sem("d_shifted")
            inverted, normed, p_hi, p_lo = sem("d_inverted"), sem("d_normed"), sem("d_p_hi"), sem("d_p_lo")
            ptr, pT_ready = sem("d_ptr"), sem("d_pT_ready")
            attended, x3_ready, x3b_ready = sem("d_attended"), sem("d_x3_ready"), sem("d_x3b_ready")
            y3_ready, y3_hi, y3_lo = sem("d_y3_ready"), sem("d_y3_hi"), sem("d_y3_lo")
            y3tr, y3T_hi, y3T_lo = sem("d_y3tr"), sem("d_y3T_hi"), sem("d_y3T_lo")
            ag_done, gate, gate_exp = sem("d_ag_done"), sem("d_gate"), sem("d_gate_exp")
            low_hi, low_lo, ltr, lowT_ready = sem("d_low_hi"), sem("d_low_lo"), sem("d_ltr"), sem("d_lowT_ready")
            ffn_done, res_ready = sem("d_ffn_done"), sem("d_res_ready")
            stored = [sem(f"d_stored{i}") for i in range(2)]
            norm_measure, norm_root, norm_scaled = layernorm(sb, sem, "d_norm", neg_half)

            SCALE = D ** -0.5
            GATE_STEPS = 9

            block = st.enter_context(nc.Block())

            def split_weights(eng_steps):
                return [(w1_p[:, :, k, :], stage[:, k % 2, :]) for k in range(KD)]

            @block.sync
            def _(sp):
                sp.dma_start(ag_in[:, :, :], wag).then_inc(small_loaded, 16)
                sp.dma_start(b_in[:, :], wb).then_inc(small_loaded, 16)
                sp.dma_start(tg_b[:, :], b1.to_broadcast([P, D])).then_inc(small_loaded, 16)
                sp.dma_start(gate_bias[:, :], gate_b.to_broadcast([P, NG])).then_inc(small_loaded, 16)

                def load_context(b):
                    wait(sp, cn_lo, 3 * b)
                    for c, (a, n) in enumerate(CH):
                        sp.dma_start(cn_raw[0:n, c, :], ctx_nat[bass.ds(b, 1), a:a + n, :].rearrange(
                            "b s d -> (b s) d")).then_inc(cn_loaded, 16)
                    wait(sp, ct_lo, KD * b)
                    sp.dma_start(ct_raw[:, :, :], ctx_t[bass.ds(b, 1), :, :, :].rearrange("b p k s -> p (b k) s")
                                 ).then_inc(ct_loaded, 16)

                def load_rows(p, b):
                    wait(sp, x3_ready, 2 * (b - 1))
                    for part in range(2):
                        sp.dma_start(tT[:, p, part, :, :], t_s[part, :, :, rows(b, Q)]).then_inc(tx_loaded[p], 16)
                    sp.dma_start(x2[:, p, 0:D + 1], x2_s[rows(b, Q), 0:D + 1]).then_inc(tx_loaded[p], 16)

                load_context(0)
                load_rows(0, 0)
                for k in range(KD):
                    wait(sp, w_lo, k - 1)
                    sp.dma_start(stage[:, k % 2, :], w1[:, k, :]).then_inc(w_loaded[k % 2], 16)
                load_rows(1, 1)

                def slot(j, p, s):
                    if inside(s + 1, B):
                        load_context(s + 1)
                        if not (isinstance(s, int) and s == 0):
                            load_rows(1 - p, s + 1)
                    if inside(s - 1, B):
                        sp.wait_ge(res_ready, 2 * s)
                        sp.dma_start(out[rows(s - 1, Q), :], res[:, 1 - p, :]).then_inc(stored[1 - p], 16)

                run_slots(sp, slot, B + 2, 4)
                for i in range(2):
                    sp.wait_ge(stored[i], 16 * (B // 2))

            def split_pieces():
                cts = [(ct_raw[:, k, :], cT[:, 0, k, 0:S], cT[:, 1, k, 0:S], ct_hi, ct_lo, KD, k, ct_loaded, 16)
                       for k in range(KD)]
                cns = [(cn_raw[0:n, c, :], cn[0:n, 0, c, :], cn[0:n, 1, c, :], cn_hi, cn_lo, 3, c, cn_loaded, 48)
                       for c, (a, n) in enumerate(CH)]
                return cts, cns

            @block.gpsimd
            def _(pool):
                cts, cns = split_pieces()

                def piece(b, item):
                    raw, high, lo_dst, hi_sem, lo_sem, per, i, _, _ = item
                    pool.wait_ge(hi_sem, per * b + i + 1)
                    pool.tensor_tensor(lo_dst, raw, high, ALU.subtract).then_inc(lo_sem, 1)

                for item in cts + cns:
                    piece(0, item)

                def slot(j, p, s):
                    if inside(s, B):
                        pool.wait_ge(p_hi, s + 1)
                        wait(pool, ptr, s)
                        pool.tensor_tensor(pp[:, 1, 0:S], pn[:, 0:S], pp[:, 0, 0:S], ALU.subtract).then_inc(p_lo, 1)
                    if inside(s + 1, B):
                        for item in cts:
                            piece(s + 1, item)
                    if inside(s, B):
                        norm_root(pool, Q, s)
                        pool.wait_ge(y3_hi, s + 1)
                        pool.tensor_tensor(y3_p[:, 1, :], y3[:, :], y3_p[:, 0, :], ALU.subtract).then_inc(y3_lo, 1)
                    if inside(s + 1, B):
                        for item in cns:
                            piece(s + 1, item)

                run_slots(pool, slot, B + 2, 4)

            @block.scalar
            def _(act):
                cts, cns = split_pieces()
                act.wait_ge(small_loaded, 64)
                act.activation(wag_p[:, 0, :, :], ag_in[:, :, :], ACT.Copy, scale=WS).then_inc(small_split, 1)
                act.activation(wb_p[:, 0, :], b_in[:, :], ACT.Copy, scale=WS).then_inc(small_split, 1)

                def piece(b, item):
                    raw, high, _, hi_sem, _, per, i, ld, inc = item
                    if i == 0:
                        act.wait_ge(ld, inc * (b + 1))
                        wait(act, scored if per == KD else attended, b if per == KD else 2 * b)
                    act.activation(high, raw, ACT.Copy).then_inc(hi_sem, 1)

                for item in cts + cns:
                    piece(0, item)
                for k in range(KD):
                    act.wait_ge(w_loaded[k % 2], 16 * (k // 2 + 1))
                    act.activation(w1_p[:, 0, k, :], stage[:, k % 2, :], ACT.Copy, scale=WS).then_inc(w_hi, 1)

                def slot(j, p, s):
                    if inside(s - 1, B):
                        act.wait_ge(y3tr, s)
                        act.activation(y3T[:, 0, :, :], tr[:, 0, 0:KD * Q].rearrange("p (k r) -> p k r", k=KD),
                                       ACT.Copy).then_inc(y3T_hi, 1)
                    if inside(s, B):
                        act.wait_ge(biased, s + 1)
                        wait(act, normed, s)
                        act.activation(ex[:, 0:S], s_ps[0:Q, 0:S], ACT.Exp, bias=sm[:, 2:3], scale=SCALE,
                                       accum_out=sm[:, 3:4]).then_inc(exped, 1)
                    if inside(s - 1, B):
                        act.wait_ge(gate, GATE_STEPS * (s - 1) + 3)
                        act.activation(gp[:, :], gs[:, :], ACT.Exp, accum_out=sm[:, 12:13]).then_inc(gate_exp, 1)
                    if inside(s, B):
                        act.wait_ge(ptr, s + 1)
                        for c, (a, n) in enumerate(CH):
                            for part in range(2):
                                o = (part * 3 + c) * Q
                                act.activation(pT[0:n, part, c, :], tr[0:n, 0, o:o + Q], ACT.Copy).then_inc(pT_ready, 1)
                    if inside(s - 1, B):
                        act.wait_ge(ltr, s)
                        act.activation(lowT[:, :, :], tr[0:LR, 1, 0:2 * Q].rearrange("p (l r) -> p l r", l=2),
                                       ACT.Copy).then_inc(lowT_ready, 1)
                    if inside(s + 1, B):
                        for item in cts:
                            piece(s + 1, item)
                    if inside(s, B):
                        act.wait_ge(y3_ready, s + 1)
                        wait(act, y3tr, s)
                        act.activation(y3_p[:, 0, :], y3[:, :], ACT.Copy).then_inc(y3_hi, 1)
                    if inside(s + 1, B):
                        for item in cns:
                            piece(s + 1, item)

                run_slots(act, slot, B + 2, 4)

            @block.vector
            def _(dve):
                dve.memset(low_p[:, :, :].rearrange("q l c -> q (l c)"), 0.0).then_inc(small_ready, 1)
                dve.wait_ge(small_loaded, 64)
                dve.wait_ge(small_split, 2)
                dve.scalar_tensor_tensor(out=wag_p[:, 1, :, :], in0=ag_in[:, :, :], scalar=WS, in1=wag_p[:, 0, :, :],
                                         op0=ALU.mult, op1=ALU.subtract).then_inc(small_ready, 1)
                dve.scalar_tensor_tensor(out=wb_p[:, 1, :], in0=b_in[:, :], scalar=WS, in1=wb_p[:, 0, :],
                                         op0=ALU.mult, op1=ALU.subtract).then_inc(small_ready, 1)
                dve.tensor_scalar(tg_b[:, :], tg_b[:, :], tg[:, 3:4], None, ALU.mult).then_inc(small_ready, 1)
                for k in range(KD):
                    dve.wait_ge(w_hi, k + 1)
                    dve.scalar_tensor_tensor(out=w1_p[:, 1, k, :], in0=stage[:, k % 2, :], scalar=WS,
                                             in1=w1_p[:, 0, k, :], op0=ALU.mult, op1=ALU.subtract).then_inc(w_lo, 1)
                dve.wait_ge(small_ready, 4)

                def softmax_head(j, p, s):
                    dve.wait_ge(scored, s + 1)
                    dve.wait_ge(tx_loaded[p], 48 * (j + 1))
                    wait(dve, exped, s)
                    dve.tensor_reduce(sm[:, 0:1], s_ps[0:Q, 0:S], AX.X, ALU.max).then_inc(maxed, 1)
                    dve.wait_ge(maxed, s + 1)
                    dve.tensor_scalar(sm[:, 1:2], sm[:, 0:1], x2[:, p, D:D + 1], None, ALU.add).then_inc(shifted, 1)
                    dve.wait_ge(shifted, s + 1)
                    dve.tensor_scalar(sm[:, 2:3], x2[:, p, D:D + 1], sm[:, 1:2], SCALE, ALU.subtract,
                                      ALU.mult).then_inc(biased, 1)

                def softmax_tail(s):
                    dve.wait_ge(exped, s + 1)
                    dve.reciprocal(sm[:, 4:5], sm[:, 3:4]).then_inc(inverted, 1)
                    dve.wait_ge(inverted, s + 1)
                    wait(dve, p_lo, s)
                    dve.tensor_scalar(pn[:, 0:S], ex[:, 0:S], sm[:, 4:5], None, ALU.mult).then_inc(normed, 1)
                    dve.wait_ge(normed, s + 1)
                    wait(dve, ptr, s)
                    dve.tensor_copy(pp[:, 0, 0:S], pn[:, 0:S]).then_inc(p_hi, 1)

                def gate_head(t):
                    base = GATE_STEPS * t
                    dve.wait_ge(ag_done, t + 1)
                    dve.scalar_tensor_tensor(out=gs[:, :], in0=ag_ps[0:Q, LR:AG], scalar=1.0 / WS,
                                             in1=gate_bias[0:Q, :], op0=ALU.mult, op1=ALU.add).then_inc(gate, 1)
                    dve.wait_ge(gate, base + 1)
                    dve.tensor_reduce(sm[:, 5:6], gs[:, :], AX.X, ALU.max).then_inc(gate, 1)
                    dve.wait_ge(gate, base + 2)
                    dve.tensor_scalar(gs[:, :], gs[:, :], sm[:, 5:6], None, ALU.subtract).then_inc(gate, 1)

                def gate_tail(t):
                    base = GATE_STEPS * t
                    dve.wait_ge(gate_exp, t + 1)
                    dve.reciprocal(sm[:, 13:14], sm[:, 12:13]).then_inc(gate, 1)
                    dve.wait_ge(gate, base + 4)
                    dve.tensor_scalar(gp[:, :], gp[:, :], sm[:, 13:14], None, ALU.mult).then_inc(gate, 1)
                    dve.wait_ge(gate, base + 5)
                    dve.tensor_tensor_scan(sm[:, 8:12], gp[:, :], gp[:, :], 0.0, ALU.max, ALU.max).then_inc(gate, 1)
                    dve.wait_ge(gate, base + 6)
                    dve.reciprocal(sm[:, 14:15], sm[:, 11:12]).then_inc(gate, 1)
                    dve.tensor_scalar(sm[:, 16:19], sm[:, 8:11], sm[:, 11:12], None, ALU.is_lt).then_inc(gate, 1)
                    dve.wait_ge(gate, base + 8)
                    dve.tensor_scalar(sm[:, 15:16], sm[:, 11:12], sm[:, 14:15], 1.0 / WS, ALU.mult,
                                      ALU.mult).then_inc(gate, 1)
                    dve.wait_ge(gate, base + 9)
                    wait(dve, low_lo, t)
                    dve.tensor_scalar(low[:, 0:RANKS[0]], ag_ps[0:Q, 0:RANKS[0]], sm[:, 15:16], None,
                                      ALU.mult).then_inc(low_hi, 1)
                    for i in range(3):
                        a, b = RANKS[i], RANKS[i + 1]
                        dve.tensor_scalar(low[:, a:b], ag_ps[0:Q, a:b], sm[:, 16 + i:17 + i], sm[:, 15:16],
                                          ALU.mult, ALU.mult).then_inc(low_hi, 1)
                    dve.wait_ge(low_hi, 5 * t + 4)
                    wait(dve, ltr, t)
                    dve.tensor_copy(low_p[:, 0, 0:LR], low[:, :]).then_inc(low_hi, 1)
                    dve.wait_ge(low_hi, 5 * t + 5)
                    dve.tensor_tensor(low_p[:, 1, 0:LR], low[:, :], low_p[:, 0, 0:LR], ALU.subtract).then_inc(low_lo, 1)

                def slot(j, p, s):
                    if inside(s - 1, B):
                        dve.wait_ge(y3tr, s)
                        dve.tensor_copy(y3T[:, 1, :, :], tr[:, 1, 0:KD * Q].rearrange("p (k r) -> p k r", k=KD)
                                        ).then_inc(y3T_lo, 1)
                    if inside(s, B):
                        softmax_head(j, p, s)
                    if inside(s - 1, B):
                        gate_head(s - 1)
                    if inside(s, B):
                        softmax_tail(s)
                    if inside(s - 1, B):
                        gate_tail(s - 1)
                    if inside(s, B):
                        for h in range(2):
                            cols = slice(h * HALF, (h + 1) * HALF)
                            dve.wait_ge(attended, 2 * s + h + 1)
                            dve.scalar_tensor_tensor(out=x3[:, cols], in0=a_ps[0:Q, h, :], scalar=tg[0:Q, 2:3],
                                                     in1=x2[:, p, cols], op0=ALU.mult, op1=ALU.add
                                                     ).then_inc(x3_ready, 1)
                        dve.wait_ge(x3_ready, 2 * s + 2)
                        norm_measure(dve, x3[:, :], Q, s)
                        wait(dve, y3_lo, s)
                        norm_scaled(dve, y3[:, :], x3[:, :], Q, s).then_inc(y3_ready, 1)
                        dve.tensor_tensor(x3b[:, p, :], x3[:, :], tg_b[0:Q, :], ALU.add).then_inc(x3b_ready, 1)
                    if inside(s - 1, B):
                        if inside(s - 3, B):
                            dve.wait_ge(stored[1 - p], 16 * (j - 1 + p))
                        dve.wait_ge(x3b_ready, s)
                        for h in range(2):
                            cols = slice(h * HALF, (h + 1) * HALF)
                            dve.wait_ge(ffn_done, 2 * (s - 1) + h + 1)
                            dve.scalar_tensor_tensor(out=res[:, 1 - p, cols], in0=f_ps[0:Q, h, :],
                                                     scalar=tg_w1[0:Q, :], in1=x3b[:, 1 - p, cols],
                                                     op0=ALU.mult, op1=ALU.add).then_inc(res_ready, 1)

                run_slots(dve, slot, B + 2, 4)

            @block.tensor
            def _(pe):
                def ffn(t, h):
                    wait(pe, res_ready, 2 * (t - 1) + h + 1)
                    for n, (a, b) in enumerate(PASSES):
                        for k in range(KD):
                            mm(f_ps[0:Q, h, :], y3T[:, a, k, :], w1_p[:, b, k, h * HALF:(h + 1) * HALF],
                               start=(n == 0 and k == 0), stop=False)

                def low_rank(t):
                    pe.wait_ge(lowT_ready, t + 1)
                    for h in range(2):
                        for n, (a, b) in enumerate(PASSES):
                            last = mm(f_ps[0:Q, h, :], lowT[:, a, :], wb_p[:, b, h * HALF:(h + 1) * HALF],
                                      start=False, stop=(n == 2))
                        last.then_inc(ffn_done, 1)

                pe.wait_ge(w_lo, KD)
                pe.wait_ge(small_ready, 4)

                def slot(j, p, s):
                    if inside(s - 1, B):
                        pe.wait_ge(y3_lo, s)
                        if inside(s - 2, B):
                            pe.wait_ge(lowT_ready, s - 1)
                            pe.wait_ge(pT_ready, 6 * s)
                        for part in range(2):
                            for k in range(KD):
                                last = pe.transpose(tr[:, part, k * Q:(k + 1) * Q], y3_p[:, part, k * P:(k + 1) * P],
                                                    ident[0:Q, 0:Q])
                        last.then_inc(y3tr, 1)
                    if inside(s, B):
                        pe.wait_ge(ct_lo, KD * (s + 1))
                        pe.wait_ge(tx_loaded[p], 48 * (j + 1))
                        wait(pe, exped, s)
                        for n, (a, b) in enumerate(PASSES):
                            for k in range(KD):
                                last = mm(s_ps[0:Q, 0:S], tT[:, p, a, k, :], cT[:, b, k, 0:S],
                                          start=(n == 0 and k == 0), stop=(n == 2 and k == KD - 1))
                        last.then_inc(scored, 1)
                    if inside(s - 1, B):
                        pe.wait_ge(y3T_hi, s)
                        pe.wait_ge(y3T_lo, s)
                        wait(pe, low_lo, s - 1)
                        for n, (a, b) in enumerate(PASSES):
                            for k in range(KD):
                                last = mm(ag_ps[0:Q, 0:AG], y3T[:, a, k, :], wag_p[:, b, k, :],
                                          start=(n == 0 and k == 0), stop=(n == 2 and k == KD - 1))
                        last.then_inc(ag_done, 1)
                        ffn(s - 1, 0)
                    if inside(s, B):
                        pe.wait_ge(p_lo, s + 1)
                        for part in range(2):
                            for c, (a, n) in enumerate(CH):
                                o = (part * 3 + c) * Q
                                last = pe.transpose(tr[0:n, 0, o:o + Q], pp[:, part, a:a + n], ident[0:Q, 0:Q])
                        last.then_inc(ptr, 1)
                    if inside(s - 1, B):
                        pe.wait_ge(low_lo, s)
                        for part in range(2):
                            last = pe.transpose(tr[:, 1, part * Q:(part + 1) * Q], low_p[:, part, :],
                                                ident[0:Q, 0:Q])
                        last.then_inc(ltr, 1)
                    if inside(s, B):
                        pe.wait_ge(cn_lo, 3 * (s + 1))
                        pe.wait_ge(pT_ready, 6 * (s + 1))
                        for h in range(2):
                            wait(pe, x3_ready, 2 * (s - 1) + h + 1)
                            for i, (a, b) in enumerate(PASSES):
                                for c, (_, n) in enumerate(CH):
                                    last = mm(a_ps[0:Q, h, :], pT[0:n, a, c, :],
                                              cn[0:n, b, c, h * HALF:(h + 1) * HALF],
                                              start=(i == 0 and c == 0), stop=(i == 2 and c == 2))
                            last.then_inc(attended, 1)
                    if inside(s - 1, B):
                        ffn(s - 1, 1)
                        low_rank(s - 1)

                run_slots(pe, slot, B + 2, 4)


def chunked(a):
    import numpy as np
    return np.ascontiguousarray(a.reshape(-1, P, a.shape[1]).transpose(1, 0, 2))


def kernel(**inputs):
    import numpy as np
    import concourse.bacc as bacc
    from concourse.bass_utils import run_bass_kernel_spmd as run

    i = {k: np.asarray(v) for k, v in inputs.items()}
    ctx = i["ctx_4096"]
    arrays = {
        "x": i["x"].reshape(R, D),
        "ctx_nat": ctx,
        "ctx_t": ctx.reshape(B, S, KD, P).transpose(0, 3, 2, 1),
        "gates": np.stack([i["g_xattn"][0], i["g_ffn"][0], i["g_xattn"][1], i["g_ffn"][1]]).reshape(1, 4),
        "wa": chunked(np.concatenate([i["L0_xattn_Wq"], i["L0_xattn_Wk"], i["L0_xattn_Wv"]], 0).T),
        "wo": chunked(i["L0_xattn_Wo"].T),
        "q4": chunked(i["L0_ffn_weight_q"].T),
        "sc4": i["L0_ffn_weight_scales"].T,
        "wq1": chunked(i["L1_xattn_Wq"]),
        "wk1": chunked(i["L1_xattn_Wk"]),
        "bq1": i["L1_xattn_bq"].reshape(KD, P).T,
        "bk1": i["L1_xattn_bk"].reshape(KD, P).T,
        "w1": chunked(i["L1_ffn_W"].T),
        "b1": i["L1_ffn_b"].reshape(1, D),
        "wag": chunked(np.concatenate([i["L1_ffn_A"], i["L1_ffn_gate_w"]], 0).T),
        "wb": i["L1_ffn_B"].T,
        "gate_b": i["L1_ffn_gate_b"].reshape(1, NG),
    }
    nc = bacc.Bacc("TRN2", target_bir_lowering=False, num_devices=1)
    arrays = {f"in_{k}": np.ascontiguousarray(v) for k, v in arrays.items()}
    args = [nc.dram_tensor(k, v.shape, mybir.dt.from_np(v.dtype), kind="ExternalInput").ap()
            for k, v in arrays.items()]
    out = nc.dram_tensor("out_rows", [R, D], F32, kind="ExternalOutput").ap()
    build(nc, *args, out)
    r = run(nc, [arrays], core_ids=[0])
    return r.results[0]["out_rows"].reshape(B, Q, D)
```

```python
from contextlib import ExitStack

import concourse.bass as bass
from concourse import mybir

F32 = mybir.dt.float32
F16 = mybir.dt.float16
BF16 = mybir.dt.bfloat16
I32 = mybir.dt.int32
ALU = mybir.AluOpType
ACT = mybir.ActivationFunctionType
AX = mybir.AxisListType

P = 128
B, Q, D = 16, 112, 1024
S = 375
R = B * Q
TILES = R // P
KD = D // P
H, KV, HD = 16, 4, 96
G = H // KV
QW, KW = H * HD, KV * HD
WA = QW + 2 * KW
KO = QW // P
SA = S + Q
LR = 64
NG = 4
RANKS = (8, 16, 32, 64)
CH = [(0, 128), (128, 128), (256, 119)]
HALF = 512
RING = 4
EPS = 1e-5
WS = 64.0
MS = 16.0
PASSES = ((0, 0), (0, 1), (1, 0))


def wait(eng, sem, value):
    if isinstance(value, int) and value <= 0:
        return
    eng.wait_ge(sem, value)


def run_slots(eng, slot, n, ends=2):
    for s in range(ends):
        slot(s // 2, s % 2, s)
    with eng.Fori(ends // 2, (n - ends) // 2) as j:
        for p in (0, 1):
            slot(j, p, 2 * j + p)
    for s in range(n - ends, n):
        slot(s // 2, s % 2, s)


def inside(t, n):
    return not isinstance(t, int) or 0 <= t < n


def rows(t, size):
    return bass.ds(t * size, size)


def layernorm(sb, sem, name, neg_half):
    stats = sb(name + "_stats", [P, 2, 6], F32)
    mean_var = sb(name + "_mean_var", [P, 2], F32)
    var_eps = sb(name + "_var_eps", [P, 1], F32)
    rstd = sb(name + "_rstd", [P, 1], F32)
    waited = sb(name + "_waited", [P, 1], F32)
    stats_done = sem(name + "_stats_done")
    aggr_done = sem(name + "_aggr_done")
    var_ready = sem(name + "_var_ready")
    rstd_ready = sem(name + "_rstd_ready")

    def measure(dve, x, n, t):
        for i in range(2):
            dve.bn_stats(stats[0:n, i, :], x[:, i * HALF:(i + 1) * HALF]).then_inc(stats_done, 1)
        dve.wait_ge(stats_done, 2 * t + 2)
        dve.memset(waited[:, :], 0.0)
        dve.bn_aggr(mean_var[0:n, :], stats[0:n, :, :]).then_inc(aggr_done, 1)
        dve.wait_ge(aggr_done, t + 1)
        dve.tensor_scalar(var_eps[0:n, :], mean_var[0:n, 1:2], EPS, None, ALU.add).then_inc(var_ready, 1)

    def root(pool, n, t):
        pool.wait_ge(var_ready, t + 1)
        pool.tensor_tensor(rstd[0:n, :], var_eps[0:n, :], neg_half[0:n, :], ALU.pow).then_inc(rstd_ready, 1)

    def scaled(dve, out, x, n, t):
        dve.wait_ge(rstd_ready, t + 1)
        return dve.tensor_scalar(out, x, mean_var[0:n, 0:1], rstd[0:n, 0:1], ALU.subtract, ALU.mult)

    return measure, root, scaled


def build(nc, x, ctx_nat, ctx_t, gates, wa, wo, q4, sc4, wq1, wk1, bq1, bk1, w1, b1, wag, wb, gate_b, out):
    qk_s = nc.dram_tensor("qk_scratch", [2, HD, H + KV, R], F16).ap()
    v_s = nc.dram_tensor("v_scratch", [R, 2, KW], F16).ap()
    o_s = nc.dram_tensor("o_scratch", [2, QW, R], F16).ap()
    t_s = nc.dram_tensor("t_scratch", [2, P, KD, R], F16).ap()
    x2_s = nc.dram_tensor("x2_scratch", [R, D + 4], F32).ap()
    w4_s = nc.dram_tensor("w4_scratch", [P, KD * D], BF16).ap()

    with ExitStack() as whole:
        def alloc(scope):
            def sb(name, shape, dt):
                return scope.enter_context(nc.sbuf_tensor(name, shape, dt))

            def pb(name, shape, dt):
                return scope.enter_context(nc.psum_tensor(name, shape, dt))
            return sb, pb

        used = []

        def sem(name):
            used.append(nc.alloc_semaphore(name=name))
            return used[-1]

        def retire_semaphores():
            for s in used:
                nc.gpsimd.sem_clear(s)
                nc.release_semaphore(s)
            del used[:]

        sb, _ = alloc(whole)
        ident32 = sb("ident32", [P, P], F32)
        ident = sb("ident", [P, P], F16)
        identb = sb("identb", [P, P], BF16)
        neg_half = sb("neg_half", [P, 1], F32)
        tg = sb("tg", [P, 4], F32)
        tg_wo = sb("tg_wo", [P, 1], F32)
        tg_w1 = sb("tg_w1", [P, 1], F32)
        with ExitStack() as mid:
            sb, _ = alloc(mid)
            Mt = sb("Mt", [P, 2, KD, D], F16)
            c_bc = sb("c_bc", [P, D], F32)
            u_bc = sb("u_bc", [P, D], F32)
            s0 = sb("s0", [P, 1], F32)

            mm = nc.tensor.matmul

            with ExitStack() as ab:
                sb, _ = alloc(ab)
                wkv_p = sb("wkv_p", [P, 2, KD, 2 * KW], F16)
                with ExitStack() as aw:
                    sb, _ = alloc(aw)
                    proj_q_p = sb("proj_q_p", [P, 2, KD, QW], F16)

                    with ExitStack() as st:
                        sb, pb = alloc(st)
                        raw = sb("raw", [P, RING, D], F32)
                        wq_p = sb("wq_p", [P, 2, KD, D], F16)
                        wk_p = sb("wk_p", [P, 2, KD, D], F16)
                        gate_in = sb("gate_in", [P, 4], F32)
                        bqk = sb("bqk", [P, 2, KD], F32)
                        bqk_hi = sb("bqk_hi", [P, 2, KD], F16)
                        bqk_lo32 = sb("bqk_lo32", [P, 2, KD], F32)
                        bqk_hi32 = sb("bqk_hi32", [P, 2, KD], F32)
                        bk_p = sb("bk_p", [P, 2, KD], F16)
                        ones = sb("ones", [P, P], F32)
                        bias_bc = sb("bias_bc", [P, 2, 2, KD, P], F16)
                        BANKS = 8
                        m_ps = pb("m_ps", [P, BANKS, HALF], F32)

                        loaded = [sem(f"z_loaded{i}") for i in range(RING)]
                        small_loaded = sem("z_small_loaded")
                        ident_zero, ident_ready = sem("z_ident_zero"), sem("z_ident_ready")
                        ident_cast = sem("z_ident_cast")
                        half_ready = sem("z_half_ready")
                        tanh_ready, tanh_scaled = sem("z_tanh_ready"), sem("z_tanh_scaled")
                        w_hi, w_lo = sem("z_w_hi"), sem("z_w_lo")
                        bias_split, bias_ready = sem("z_bias_split"), sem("z_bias_ready")
                        m_done, m_hi, m_lo = sem("z_m_done"), sem("z_m_hi"), sem("z_m_lo")
                        b_done, b_read = sem("z_b_done"), sem("z_b_read")

                        PC = 2 * KW
                        pieces = []
                        for k in range(KD):
                            for w, dst in ((wq1, wq_p), (wk1, wk_p)):
                                pieces.append((w[:, k, :], dst[:, 0, k, :], dst[:, 1, k, :], D))
                        for k in range(KD):
                            for c in range(0, WA, PC):
                                dst, at = (proj_q_p, c) if c < QW else (wkv_p, c - QW)
                                pieces.append((wa[:, k, c:c + PC], dst[:, 0, k, at:at + PC], dst[:, 1, k, at:at + PC], PC))
                        M_PIECES = 2 * KD
                        PER_ROW = 2

                        block = st.enter_context(nc.Block())

                        @block.sync
                        def _(sp):
                            for n, (src, _, _, cols) in enumerate(pieces):
                                wait(sp, w_lo, n - RING + 1)
                                sp.dma_start(raw[:, n % RING, 0:cols], src).then_inc(loaded[n % RING], 16)

                        @block.gpsimd
                        def _(pool):
                            pool.memset(ident32[:, :], 0.0).then_inc(ident_zero, 1)
                            pool.memset(neg_half[:, :], -0.5).then_inc(half_ready, 1)
                            pool.memset(ones[:, :], 1.0).then_inc(half_ready, 1)
                            pool.wait_ge(ident_zero, 1)
                            pool.affine_select(out=ident32[:, :], in_=ident32[:, :], compare_op=ALU.not_equal, fill=1.0,
                                               base=0, pattern=[[-1, P]], channel_multiplier=1).then_inc(ident_ready, 1)
                            pool.wait_ge(ident_ready, 1)
                            pool.tensor_copy(ident[:, :], ident32[:, :]).then_inc(ident_cast, 1)
                            pool.tensor_copy(identb[:, :], ident32[:, :]).then_inc(ident_cast, 1)

                        @block.scalar
                        def _(act):
                            act.dma_start(gate_in[:, :], gates.to_broadcast([P, 4])).then_inc(small_loaded, 16)
                            act.dma_start(bqk[:, 0, :], bq1).then_inc(small_loaded, 16)
                            act.dma_start(bqk[:, 1, :], bk1).then_inc(small_loaded, 16)
                            act.wait_ge(small_loaded, 48)
                            act.activation(tg[:, :], gate_in[:, :], ACT.Tanh).then_inc(tanh_ready, 1)

                            def high(n):
                                _, dst, _, cols = pieces[n]
                                act.wait_ge(loaded[n % RING], 16 * (n // RING + 1))
                                act.activation(dst, raw[:, n % RING, 0:cols], ACT.Copy, scale=WS).then_inc(w_hi, 1)

                            for n in range(M_PIECES):
                                high(n)
                            n = M_PIECES
                            for i in range(2 * KD):
                                m, h = divmod(i, 2)
                                act.wait_ge(m_done, i + 1)
                                act.activation(Mt[:, 0, m, h * HALF:(h + 1) * HALF], m_ps[:, i % BANKS, :], ACT.Copy,
                                               scale=MS / (WS * WS)).then_inc(m_hi, 1)
                                if i >= BANKS - 1:
                                    high(n)
                                    high(n + 1)
                                    n += PER_ROW
                            for i, dst in enumerate((c_bc, u_bc)):
                                for h in range(2):
                                    act.wait_ge(b_done, 2 * i + h + 1)
                                    act.activation(dst[:, h * HALF:(h + 1) * HALF], m_ps[:, 2 * i + h, :], ACT.Copy,
                                                   scale=1.0 / WS).then_inc(b_read, 1)
                                    if n < len(pieces):
                                        high(n)
                                        high(n + 1)
                                        n += PER_ROW
                            act.wait_ge(b_done, 5)
                            act.activation(s0[:, :], m_ps[:, 4, 0:1], ACT.Copy).then_inc(b_read, 1)

                        @block.vector
                        def _(dve):
                            def low(n):
                                _, hi_part, dst, cols = pieces[n]
                                dve.wait_ge(loaded[n % RING], 16 * (n // RING + 1))
                                dve.wait_ge(w_hi, n + 1)
                                dve.scalar_tensor_tensor(out=dst, in0=raw[:, n % RING, 0:cols], scalar=WS, in1=hi_part,
                                                         op0=ALU.mult, op1=ALU.subtract).then_inc(w_lo, 1)

                            for n in range(M_PIECES):
                                low(n)
                            dve.wait_ge(small_loaded, 48)
                            dve.tensor_copy(bqk_hi[:, :, :], bqk[:, :, :]).then_inc(bias_split, 1)
                            dve.wait_ge(bias_split, 1)
                            dve.tensor_copy(bqk_hi32[:, :, :], bqk_hi[:, :, :]).then_inc(bias_split, 1)
                            dve.tensor_tensor(bqk_lo32[:, :, :], bqk[:, :, :], bqk_hi[:, :, :], ALU.subtract).then_inc(bias_split, 1)
                            dve.wait_ge(bias_split, 3)
                            dve.tensor_copy(bk_p[:, 0, :], bqk_hi[:, 1, :]).then_inc(bias_ready, 1)
                            dve.tensor_copy(bk_p[:, 1, :], bqk_lo32[:, 1, :]).then_inc(bias_ready, 1)
                            dve.wait_ge(half_ready, 2)
                            for i in range(2):
                                for part, src in ((0, bqk_hi32), (1, bqk_lo32)):
                                    for k in range(KD):
                                        dve.tensor_scalar(bias_bc[:, i, part, k, :], ones[:, :], src[:, i, k:k + 1], None,
                                                          ALU.mult).then_inc(bias_ready, 1)
                            dve.wait_ge(tanh_ready, 1)
                            dve.tensor_scalar(tg_wo[:, :], tg[:, 0:1], 1.0 / WS, None, ALU.mult).then_inc(tanh_scaled, 1)
                            dve.tensor_scalar(tg_w1[:, :], tg[:, 3:4], 1.0 / WS, None, ALU.mult).then_inc(tanh_scaled, 1)
                            n = M_PIECES
                            for i in range(2 * KD):
                                m, h = divmod(i, 2)
                                dve.wait_ge(m_hi, i + 1)
                                dve.scalar_tensor_tensor(out=Mt[:, 1, m, h * HALF:(h + 1) * HALF],
                                                         in0=m_ps[:, i % BANKS, :], scalar=MS / (WS * WS),
                                                         in1=Mt[:, 0, m, h * HALF:(h + 1) * HALF],
                                                         op0=ALU.mult, op1=ALU.subtract).then_inc(m_lo, 1)
                                if i >= BANKS - 1:
                                    low(n)
                                    low(n + 1)
                                    n += PER_ROW
                            for n in range(n, len(pieces)):
                                low(n)

                        @block.tensor
                        def _(pe):
                            def product(i, part, k, start, stop):
                                m, h = divmod(i, 2)
                                return mm(m_ps[:, i % BANKS, :], wq_p[:, part[0], k, m * P:(m + 1) * P],
                                          wk_p[:, part[1], k, h * HALF:(h + 1) * HALF], start=start, stop=stop)

                            for k in range(KD):
                                pe.wait_ge(w_lo, 2 * (k + 1))
                                for i in range(BANKS):
                                    for n, part in enumerate(PASSES):
                                        last = product(i, part, k, k == 0 and n == 0, k == KD - 1 and n == 2)
                                    if k == KD - 1:
                                        last.then_inc(m_done, 1)
                            for i in range(BANKS, 2 * KD):
                                pe.wait_ge(m_lo, i - BANKS + 1)
                                for n, part in enumerate(PASSES):
                                    for k in range(KD):
                                        last = product(i, part, k, n == 0 and k == 0, n == 2 and k == KD - 1)
                                last.then_inc(m_done, 1)
                            pe.wait_ge(bias_ready, 2 + 4 * KD)
                            for i, w in enumerate((wk_p, wq_p)):
                                for h in range(2):
                                    pe.wait_ge(m_lo, BANKS + 2 * i + h + 1)
                                    for n, (a, b) in enumerate(PASSES):
                                        for k in range(KD):
                                            last = mm(m_ps[:, 2 * i + h, :], bias_bc[:, i, a, k, :],
                                                      w[:, b, k, h * HALF:(h + 1) * HALF],
                                                      start=(n == 0 and k == 0), stop=(n == 2 and k == KD - 1))
                                    last.then_inc(b_done, 1)
                            pe.wait_ge(m_lo, BANKS + 5)
                            for n, (a, b) in enumerate(PASSES):
                                for k in range(KD):
                                    last = mm(m_ps[:, 4, 0:1], bias_bc[:, 0, a, k, :], bk_p[:, b, k:k + 1],
                                              start=(n == 0 and k == 0), stop=(n == 2 and k == KD - 1))
                            last.then_inc(b_done, 1)

                    retire_semaphores()

                    ctx_raw = ab.enter_context(nc.sbuf_tensor("ctx_raw", [P, KD, S], F32, side="right"))
                    cT = ab.enter_context(nc.sbuf_tensor("b_cT", [P, 2, 2, KD, S + 1], F16, side="right"))
                    raw_loaded = nc.alloc_semaphore(name="b_raw_loaded")
                    split_hi, split_lo = nc.alloc_semaphore(name="b_split_hi"), nc.alloc_semaphore(name="b_split_lo")

                    def load_raw(sp, b):
                        wait(sp, split_hi, KD * b)
                        wait(sp, split_lo, KD * b)
                        sp.dma_start(ctx_raw[:, :, :], ctx_t[bass.ds(b, 1), :, :, :].rearrange("b p k s -> p (b k) s")
                                     ).then_inc(raw_loaded, 16)

                    def split_high(act, p, b, k):
                        if k == 0:
                            act.wait_ge(raw_loaded, 16 * (b + 1))
                        act.activation(cT[:, p, 0, k, 0:S], ctx_raw[:, k, :], ACT.Copy).then_inc(split_hi, 1)

                    def split_low(pool, p, b, k):
                        pool.wait_ge(split_hi, KD * b + k + 1)
                        pool.tensor_tensor(cT[:, p, 1, k, 0:S], ctx_raw[:, k, :], cT[:, p, 0, k, 0:S],
                                           ALU.subtract).then_inc(split_lo, 1)

                    NC = WA // KW
                    HC = NC - 1
                    with ExitStack() as st:
                        sb, pb = alloc(st)
                        xin = sb("a_x", [P, 2, D], F32)
                        y_p = sb("a_y_p", [P, 2, D], F16)
                        yT = sb("a_yT", [P, 2, 2, KD, P], F16)
                        nat = sb("a_nat", [P, 2, 2, KW], F16)
                        heads = sb("a_heads", [HD, 2, 2, H + KV, P], F16)
                        val = sb("a_val", [P, 2, 2, KW], F16)
                        codes = sb("a_codes", [P, HALF], I32)
                        scale4 = sb("a_scale4", [P, HALF], F32)
                        sign8, mag = sb("a_sign8", [P, HALF], F32), sb("a_mag", [P, HALF], F32)
                        over4 = sb("a_over4", [P, HALF], F32)
                        over6 = codes[:, :].bitcast(F32)
                        w4_out = sb("a_w4_out", [P, 2, HALF], BF16)
                        pr = pb("a_pr", [P, 3, HALF], F32)
                        tr = pb("a_tr", [P, 2, KD * P], F16)
                        ht = pb("a_ht", [P, 2, 2 * G * P], F16)

                        x_loaded = [sem(f"a_x_loaded{i}") for i in range(2)]
                        y_ready, yh_ready, yl_ready = sem("a_y_ready"), sem("a_yh_ready"), sem("a_yl_ready")
                        ytr_done, yT_hi, yT_lo = sem("a_ytr_done"), sem("a_yT_hi"), sem("a_yT_lo")
                        proj, hi, lo = sem("a_proj"), sem("a_hi"), sem("a_lo")
                        htr = sem("a_htr")
                        ht_read = [sem(f"a_ht_read{i}") for i in range(2)]
                        qk_stored = [sem(f"a_qk_stored{i}") for i in range(2)]
                        v_stored = [sem(f"a_v_stored{i}") for i in range(2)]
                        codes_loaded, codes_free, deq = sem("a_codes_loaded"), sem("a_codes_free"), sem("a_deq")
                        w4_stored = [sem(f"a_w4_stored{i}") for i in range(2)]
                        norm_measure, norm_root, norm_scaled = layernorm(sb, sem, "a_norm", neg_half)

                        W4N = 2 * KD
                        DEQ_PARTS = NC
                        assert W4N == TILES + 2

                        def pieces_of(j, p, t):
                            return (([(0, 0, 0)] if isinstance(t, int) and t == 0 else []) + [(t + 1, j + p, 1 - p)]
                                    + ([(W4N - 1, KD - 1, 1)] if isinstance(t, int) and t == TILES - 1 else []))

                        def weight(part, k, c):
                            if c < QW // KW:
                                return proj_q_p[:, part, k, c * KW:(c + 1) * KW]
                            return wkv_p[:, part, k, (c - QW // KW) * KW:(c - QW // KW + 1) * KW]

                        block = st.enter_context(nc.Block())

                        @block.sync
                        def _(sp):
                            for t in range(2):
                                sp.dma_start(xin[:, t, :], x[t * P:(t + 1) * P, :]).then_inc(x_loaded[t], 16)

                            def load_codes(n, k, h):
                                wait(sp, codes_free, n)
                                sp.dma_start(codes[:, :], q4.rearrange("p k d -> p (k d)")[:, rows(n, HALF)]
                                             ).then_inc(codes_loaded, 16)
                                scales = sc4[rows(k, 8), h * HALF:(h + 1) * HALF]
                                sp.dma_start(scale4[:, :], scales.rearrange("b o -> b () o").to_broadcast([8, 16, HALF])
                                             ).then_inc(codes_loaded, 16)

                            def slot(j, p, t):
                                for n, k, h in pieces_of(j, p, t):
                                    load_codes(n, k, h)
                                if isinstance(t, int) and t >= TILES - 2:
                                    load_raw(sp, t - (TILES - 2))
                                if inside(t + 2, TILES):
                                    sp.wait_ge(yl_ready, t + 1)
                                    sp.wait_ge(yh_ready, t + 1)
                                    sp.dma_start(xin[:, p, :], x[rows(t + 2, P), :]).then_inc(x_loaded[p], 16)
                                sp.wait_ge(lo, NC * (t + 1))
                                sp.dma_start(v_s[rows(t, P), :, :], val[:, p, :, :]).then_inc(v_stored[p], 16)

                            run_slots(sp, slot, TILES)
                            for p in range(2):
                                sp.wait_ge(v_stored[p], 16 * (TILES // 2))
                                sp.wait_ge(qk_stored[p], 32 * (TILES // 2))
                                sp.wait_ge(w4_stored[p], 16 * KD)

                        @block.gpsimd
                        def _(pool):
                            def norm_of(p, t):
                                norm_root(pool, P, t)
                                pool.wait_ge(yh_ready, t + 1)
                                pool.tensor_tensor(y_p[:, 1, :], xin[:, p, :], y_p[:, 0, :], ALU.subtract).then_inc(yl_ready, 1)

                            norm_of(0, 0)

                            def slot(j, p, t):
                                if inside(t + 1, TILES):
                                    norm_of(1 - p, t + 1)
                                if isinstance(t, int) and t >= TILES - 2:
                                    for k in range(KD):
                                        split_low(pool, t - (TILES - 2), t - (TILES - 2), k)

                            run_slots(pool, slot, TILES)

                        @block.scalar
                        def _(act):
                            def y_high(p, t):
                                act.wait_ge(y_ready, t + 1)
                                wait(act, ytr_done, t)
                                act.activation(y_p[:, 0, :], xin[:, p, :], ACT.Copy).then_inc(yh_ready, 1)

                            def yT_high(p, t):
                                act.wait_ge(ytr_done, t + 1)
                                act.activation(yT[:, p, 0, :, :], tr[:, 0, :].rearrange("p (k r) -> p k r", k=KD),
                                               ACT.Copy).then_inc(yT_hi, 1)

                            y_high(0, 0)
                            yT_high(0, 0)

                            def chunk(j, p, t, c):
                                act.wait_ge(proj, NC * t + c + 1)
                                if c < HC:
                                    wait(act, htr, HC * t + c - 1)
                                    dst = nat[:, (p + c) % 2, 0, :]
                                else:
                                    wait(act, v_stored[p], 16 * j)
                                    dst = val[:, p, 0, :]
                                scale = (1.0 if c >= QW // KW else HD ** -0.5) / WS
                                act.activation(dst, pr[:, c % 3, 0:KW], ACT.Copy, scale=scale).then_inc(hi, 1)

                            def head_read(j, p, t, c):
                                if (p + c) % 2 == 0:
                                    act.wait_ge(htr, HC * t + c + 1)
                                    if c < 2:
                                        wait(act, qk_stored[p], 32 * j)
                                    act.activation(heads[:, p, :, G * c:G * (c + 1), :],
                                                   ht[0:HD, 0, :].rearrange("d (l g r) -> d l g r", l=2, g=G),
                                                   ACT.Copy).then_inc(ht_read[0], 1)

                            def store_heads(j, p, t):
                                n = HC * (p + 1)
                                act.wait_ge(ht_read[0], HC * j + (n + 1) // 2)
                                act.wait_ge(ht_read[1], HC * j + n // 2)
                                for part in range(2):
                                    act.dma_start(qk_s[part, :, :, rows(t, P)], heads[:, p, part, :, :]).then_inc(qk_stored[p], 16)

                            def store_w4(j, p, t):
                                for n, k, h in pieces_of(j, p, t):
                                    act.wait_ge(codes_free, n + 1)
                                    act.dma_start(w4_s[:, rows(n, HALF)], w4_out[:, h, :]).then_inc(w4_stored[h], 16)

                            def slot(j, p, t):
                                for c in range(NC):
                                    chunk(j, p, t, c)
                                    if c == 0 and inside(t - 1, TILES):
                                        store_heads(j - 1 + p, 1 - p, t - 1)
                                        store_w4(j - 1 + p, 1 - p, t - 1)
                                    if c:
                                        head_read(j, p, t, c - 1)
                                    if c == 0 and inside(t + 1, TILES):
                                        y_high(1 - p, t + 1)
                                    if c == 3 and inside(t + 1, TILES):
                                        yT_high(1 - p, t + 1)
                                    if isinstance(t, int) and t >= TILES - 2 and c >= 2:
                                        for k in (2 * c - 4, 2 * c - 3):
                                            split_high(act, t - (TILES - 2), t - (TILES - 2), k)

                            run_slots(act, slot, TILES)
                            store_heads(TILES // 2 - 1, 1, TILES - 1)
                            store_w4(TILES // 2 - 1, 1, TILES - 1)

                        @block.vector
                        def _(dve):
                            def y_of(j, p, t):
                                dve.wait_ge(x_loaded[p], 16 * (j + 1))
                                norm_measure(dve, xin[:, p, :], P, t)
                                norm_scaled(dve, xin[:, p, :], xin[:, p, :], P, t).then_inc(y_ready, 1)

                            def yT_low(p, t):
                                dve.wait_ge(ytr_done, t + 1)
                                dve.tensor_copy(yT[:, p, 1, :, :],
                                                tr[:, 1, :].rearrange("p (k r) -> p k r", k=KD)).then_inc(yT_lo, 1)

                            y_of(0, 0, 0)
                            yT_low(0, 0)

                            def chunk(j, p, t, c):
                                dve.wait_ge(hi, NC * t + c + 1)
                                both = nat[:, (p + c) % 2, :, :] if c < HC else val[:, p, :, :]
                                scale = (1.0 if c >= QW // KW else HD ** -0.5) / WS
                                dve.scalar_tensor_tensor(out=both[:, 1, :], in0=pr[:, c % 3, 0:KW], scalar=scale,
                                                         in1=both[:, 0, :], op0=ALU.mult, op1=ALU.subtract).then_inc(lo, 1)

                            def head_read(j, p, t, c):
                                if (p + c) % 2 == 1:
                                    dve.wait_ge(htr, HC * t + c + 1)
                                    if c < 2:
                                        wait(dve, qk_stored[p], 32 * j)
                                    dve.tensor_copy(heads[:, p, :, G * c:G * (c + 1), :],
                                                    ht[0:HD, 1, :].rearrange("d (l g r) -> d l g r", l=2, g=G)
                                                    ).then_inc(ht_read[1], 1)

                            def step(n, i, ins):
                                ins.then_inc(deq, 1)
                                dve.wait_ge(deq, 8 * n + i + 1)

                            def dequantize(n, k, h, part):
                                if part == 0:
                                    dve.wait_ge(codes_loaded, 32 * (n + 1))
                                    step(n, 0, dve.tensor_scalar(sign8[:, :], codes[:, :], 8.0, 8.0, ALU.is_ge, ALU.mult))
                                    step(n, 1, dve.tensor_tensor(mag[:, :], codes[:, :], sign8[:, :], ALU.subtract))
                                if part == 1:
                                    step(n, 2, dve.tensor_scalar(over4[:, :], mag[:, :], 4.0, 0.0, ALU.subtract, ALU.max))
                                    step(n, 3, dve.tensor_scalar(over6[:, :], mag[:, :], 6.0, 0.0, ALU.subtract, ALU.max))
                                if part == 2:
                                    step(n, 4, dve.scalar_tensor_tensor(out=over4[:, :], in0=over4[:, :], scalar=0.5,
                                                                        in1=over6[:, :], op0=ALU.mult, op1=ALU.add))
                                if part == 3:
                                    step(n, 5, dve.scalar_tensor_tensor(out=mag[:, :], in0=mag[:, :], scalar=0.5,
                                                                        in1=over4[:, :], op0=ALU.mult, op1=ALU.add))
                                if part == 4:
                                    step(n, 6, dve.tensor_scalar(sign8[:, :], sign8[:, :], -0.25, 1.0, ALU.mult, ALU.add))
                                    step(n, 7, dve.tensor_tensor(mag[:, :], mag[:, :], sign8[:, :], ALU.mult))
                                if part == 5:
                                    wait(dve, w4_stored[h], 16 * k)
                                    dve.tensor_tensor(w4_out[:, h, :], mag[:, :], scale4[:, :], ALU.mult).then_inc(codes_free, 1)
                                    dve.wait_ge(codes_free, n + 1)

                            def slot(j, p, t):
                                for n, k, h in pieces_of(j, p, t)[:-1]:
                                    for c in range(DEQ_PARTS):
                                        dequantize(n, k, h, c)
                                for c in range(NC):
                                    chunk(j, p, t, c)
                                    for n, k, h in pieces_of(j, p, t)[-1:]:
                                        dequantize(n, k, h, c)
                                    if c:
                                        head_read(j, p, t, c - 1)
                                    if c == 0 and inside(t + 1, TILES):
                                        y_of(j + p, 1 - p, t + 1)
                                    if c == 3 and inside(t + 1, TILES):
                                        yT_low(1 - p, t + 1)

                            run_slots(dve, slot, TILES)

                        @block.tensor
                        def _(pe):
                            def y_transposes(t):
                                pe.wait_ge(yl_ready, t + 1)
                                for part in range(2):
                                    for k in range(KD):
                                        last = pe.transpose(tr[:, part, k * P:(k + 1) * P], y_p[:, part, k * P:(k + 1) * P],
                                                            ident[:, :])
                                last.then_inc(ytr_done, 1)

                            def project(j, p, t, c):
                                wait(pe, lo, NC * t + c - 2)
                                for n, (a, b) in enumerate(PASSES):
                                    for k in range(KD):
                                        last = mm(pr[:, c % 3, 0:KW], yT[:, p, a, k, :], weight(b, k, c),
                                                  start=(n == 0 and k == 0), stop=(n == 2 and k == KD - 1))
                                last.then_inc(proj, 1)

                            def head_transposes(j, p, t, c):
                                bank = (p + c) % 2
                                pe.wait_ge(lo, NC * t + c + 1)
                                n = HC * p + c
                                wait(pe, ht_read[bank], HC * j + n // 2)
                                for part in range(2):
                                    for g in range(G):
                                        last = pe.transpose(ht[0:HD, bank, (part * G + g) * P:(part * G + g + 1) * P],
                                                            nat[:, bank, part, g * HD:(g + 1) * HD], ident[:, :])
                                last.then_inc(htr, 1)

                            y_transposes(0)

                            def slot(j, p, t):
                                pe.wait_ge(yT_hi, t + 1)
                                pe.wait_ge(yT_lo, t + 1)
                                for c in range(NC):
                                    project(j, p, t, c)
                                    if c:
                                        head_transposes(j, p, t, c - 1)
                                    if c == 3 and inside(t + 1, TILES):
                                        y_transposes(t + 1)

                            run_slots(pe, slot, TILES)

                    retire_semaphores()

                with ExitStack() as st:
                    sb, pb = alloc(st)
                    kT = sb("b_kT", [HD, 2, 2, KV, SA + 1], F16)
                    vv = sb("b_v", [P, 2, 4, 2, KW], F16)
                    qT = sb("b_qT", [HD, 2, 2, H, Q], F16)
                    kn = sb("b_kn", [P, 2, KW], F16)
                    ex = sb("b_exp", [Q, 2, SA + 1], F32)
                    pn = sb("b_prob", [Q, 2, SA + 1], F32)
                    pp = sb("b_prob_p", [Q, 2, 2, SA + 1], F16)
                    pT = sb("b_probT", [P, 2, 2, 4, G, Q], F16)
                    oo = sb("b_o", [HD, 2, 2, G * Q], F16)
                    nmax = sb("b_nmax", [Q, 4], F32)
                    esum = sb("b_esum", [Q, 4], F32)
                    rsum = sb("b_rsum", [Q, 4], F32)
                    kv_ps = pb("b_kv_ps", [P, 2, HALF], F32)
                    s_ps = pb("b_s_ps", [P, 2, HALF], F32)
                    pt_ps = pb("b_pt_ps", [P, 2, 1024], F16)
                    o_ps = pb("b_o_ps", [P, HALF], F32)
                    kt_ps = pb("b_kt_ps", [P, 1024], F16)

                    q_loaded = [sem(f"b_q_loaded{i}") for i in range(2)]
                    kv_loaded = [sem(f"b_kv_loaded{i}") for i in range(2)]
                    kv_done, kv_hi, kv_lo = sem("b_kv_done"), sem("b_kv_hi"), sem("b_kv_lo")
                    ktr, kt_read = sem("b_ktr"), sem("b_kt_read")
                    scored, maxed, exped = sem("b_scored"), sem("b_maxed"), sem("b_exped")
                    inverted, normed, p_hi, p_lo = sem("b_inverted"), sem("b_normed"), sem("b_p_hi"), sem("b_p_lo")
                    ptr = sem("b_ptr")
                    pt_read = [sem(f"b_pt_read{i}") for i in range(2)]
                    pv, o_hi, o_lo = sem("b_pv"), sem("b_o_hi"), sem("b_o_lo")
                    o_stored = [sem(f"b_o_stored{i}") for i in range(2)]
                    pt_cleared = sem("b_pt_cleared")

                    BLOCK = 3 * KD
                    PER_STEP = 6 * BLOCK // H
                    READ_AT = [(BLOCK * (k + 1) - 1) // PER_STEP + 1 for k in range(6)]

                    def block_out(p, k, part):
                        n = CH[k % 3][1]
                        return kn[0:n, part, :] if k < 3 else vv[0:n, p, k - 3, part, :]

                    KEYS = [(Q + a, n) for a, n in CH] + [(0, Q)]

                    block = st.enter_context(nc.Block())

                    @block.sync
                    def _(sp):
                        def load_latents(j, p, b):
                            wait(sp, pv, KV * (b - 1))
                            for part in range(2):
                                sp.dma_start(qT[:, p, part, :, :], qk_s[part, :, 0:H, rows(b, Q)]).then_inc(q_loaded[p], 16)
                                sp.dma_start(kT[:, p, part, :, 0:Q],
                                             qk_s[part, :, H:H + KV, rows(b, Q)]).then_inc(q_loaded[p], 16)
                            sp.dma_start(vv[0:Q, p, 3, :, :], v_s[rows(b, Q), :, :]).then_inc(kv_loaded[p], 16)

                        def store(b, g):
                            sp.wait_ge(o_lo, KV * b + g + 1)
                            for part in range(2):
                                dst = o_s[part, g * G * HD:(g + 1) * G * HD, rows(b, Q)].rearrange("(h d) r -> d h r", h=G)
                                src = oo[:, g % 2, part, :].rearrange("d (h r) -> d h r", h=G)
                                sp.dma_start(dst, src).then_inc(o_stored[g % 2], 16)

                        load_latents(0, 0, 0)
                        load_latents(0, 1, 1)

                        def slot(j, p, b):
                            if inside(b - 1, B):
                                store(b - 1, KV - 1)
                                if inside(b + 1, B):
                                    load_latents(j, 1 - p, b + 1)
                            if inside(b + 2, B):
                                load_raw(sp, b + 2)
                            for g in range(KV - 1):
                                store(b, g)

                        run_slots(sp, slot, B)
                        store(B - 1, KV - 1)
                        for i in range(2):
                            sp.wait_ge(o_stored[i], 32 * B * KV // 2)

                    @block.gpsimd
                    def _(pool):
                        def split_piece(p, b, k):
                            if k == 0:
                                wait(pool, kv_done, 6 * (b - 1))
                            split_low(pool, p, b, k)

                        def prob_low(b, h):
                            n = H * b + h
                            pool.wait_ge(p_hi, n + 1)
                            wait(pool, ptr, n - 1)
                            pool.tensor_tensor(pp[:, h % 2, 1, 0:SA], pn[:, h % 2, 0:SA], pp[:, h % 2, 0, 0:SA],
                                               ALU.subtract).then_inc(p_lo, 1)

                        prob_low(0, 0)

                        def slot(j, p, b):
                            for i in range(H):
                                if i < H - 1:
                                    prob_low(b, i + 1)
                                elif inside(b + 1, B):
                                    prob_low(b + 1, 0)
                                if 4 <= i < 4 + KD and inside(b + 2, B):
                                    split_piece(p, b + 2, i - 4)

                        run_slots(pool, slot, B)

                    @block.scalar
                    def _(act):
                        def split_piece(p, b, k):
                            if k == 0:
                                wait(act, kv_done, 6 * (b - 1))
                            split_high(act, p, b, k)

                        def block_high(p, b, k):
                            n = CH[k % 3][1]
                            act.wait_ge(kv_done, 6 * b + k + 1)
                            if k < 3:
                                wait(act, ktr, 3 * b + k)
                            act.activation(block_out(p, k, 0), kv_ps[0:n, k % 2, 0:KW], ACT.Copy, scale=1.0 / WS).then_inc(kv_hi, 1)

                        def keys_read(p, b, c):
                            a, n = KEYS[c]
                            act.wait_ge(ktr, 3 * b + c + 1)
                            act.activation(kT[:, p, :, :, a:a + n],
                                           kt_ps[0:HD, :].rearrange("d (l g r) -> d l g r", l=2, g=KV)[:, :, :, 0:n],
                                           ACT.Copy).then_inc(kt_read, 1)

                        def exponent(b, h):
                            n = H * b + h
                            act.wait_ge(maxed, n + 1)
                            wait(act, normed, n - 1)
                            act.activation(ex[:, h % 2, 0:SA], s_ps[0:Q, h % 2, 0:SA], ACT.Exp, bias=nmax[:, h % 4:h % 4 + 1],
                                           accum_out=esum[:, h % 4:h % 4 + 1]).then_inc(exped, 1)

                        def probs_read(j, p, b, h):
                            if h % 2 == 0:
                                act.wait_ge(ptr, H * b + h + 1)
                                g = h // G
                                wait(act, pv, KV * b + g - 1)
                                act.activation(pT[:, g % 2, :, :, h % G, :],
                                               pt_ps[:, 0, 0:8 * Q].rearrange("s (l c r) -> s l c r", l=2, c=4),
                                               ACT.Copy).then_inc(pt_read[0], 1)

                        def out_high(b, g):
                            act.wait_ge(pv, KV * b + g + 1)
                            wait(act, o_stored[g % 2], 32 * (2 * b + g // 2))
                            act.activation(oo[:, g % 2, 0, :], o_ps[0:HD, 0:G * Q], ACT.Copy).then_inc(o_hi, 1)

                        for k in range(6):
                            block_high(0, 0, k)
                            if k < 3:
                                keys_read(0, 0, k)
                        for h in range(2):
                            exponent(0, h)

                        def slot(j, p, b):
                            for i in range(H):
                                if i == 0 and inside(b - 1, B):
                                    block_high(p, b, 5)
                                if i in READ_AT and inside(b + 1, B):
                                    block_high(1 - p, b + 1, READ_AT.index(i))
                                if i < H - 2:
                                    exponent(b, i + 2)
                                elif inside(b + 1, B):
                                    exponent(b + 1, i + 2 - H)
                                probs_read(j, p, b, i)
                                if i - 2 in READ_AT[0:3] and inside(b + 1, B):
                                    keys_read(1 - p, b + 1, READ_AT.index(i - 2))
                                if i % G == 0:
                                    if i:
                                        out_high(b, i // G - 1)
                                    elif inside(b - 1, B):
                                        out_high(b - 1, KV - 1)
                                if 4 <= i < 4 + KD and inside(b + 2, B):
                                    split_piece(p, b + 2, i - 4)

                        run_slots(act, slot, B)
                        out_high(B - 1, KV - 1)

                    @block.vector
                    def _(dve):
                        for i in range(2):
                            dve.memset(pt_ps[:, i, :].bitcast(F32), 0.0).then_inc(pt_cleared, 1)

                        def block_low(p, b, k):
                            n = CH[k % 3][1]
                            dve.wait_ge(kv_hi, 6 * b + k + 1)
                            dve.scalar_tensor_tensor(out=block_out(p, k, 1), in0=kv_ps[0:n, k % 2, 0:KW], scalar=1.0 / WS,
                                                         in1=block_out(p, k, 0), op0=ALU.mult, op1=ALU.subtract).then_inc(kv_lo, 1)

                        def maximum(b, h):
                            dve.wait_ge(scored, H * b + h + 1)
                            wait(dve, exped, H * b + h - 3)
                            dve.tensor_reduce(nmax[:, h % 4:h % 4 + 1], s_ps[0:Q, h % 2, 0:SA], AX.X, ALU.max,
                                              negate=True).then_inc(maxed, 1)

                        def normalize(b, h):
                            n = H * b + h
                            c = h % 4
                            dve.wait_ge(exped, n + 1)
                            dve.reciprocal(rsum[:, c:c + 1], esum[:, c:c + 1]).then_inc(inverted, 1)
                            dve.wait_ge(inverted, n + 1)
                            wait(dve, p_lo, n - 1)
                            dve.tensor_scalar(pn[:, h % 2, 0:SA], ex[:, h % 2, 0:SA], rsum[:, c:c + 1], None,
                                              ALU.mult).then_inc(normed, 1)
                            dve.wait_ge(normed, n + 1)
                            wait(dve, ptr, n - 1)
                            dve.tensor_copy(pp[:, h % 2, 0, 0:SA], pn[:, h % 2, 0:SA]).then_inc(p_hi, 1)

                        def probs_read(j, p, b, h):
                            if h % 2 == 1:
                                dve.wait_ge(ptr, H * b + h + 1)
                                g = h // G
                                wait(dve, pv, KV * b + g - 1)
                                dve.tensor_copy(pT[:, g % 2, :, :, h % G, :],
                                                pt_ps[:, 1, 0:8 * Q].rearrange("s (l c r) -> s l c r", l=2, c=4)
                                                ).then_inc(pt_read[1], 1)

                        def out_low(b, g):
                            dve.wait_ge(o_hi, KV * b + g + 1)
                            dve.tensor_tensor(oo[:, g % 2, 1, :], o_ps[0:HD, 0:G * Q], oo[:, g % 2, 0, :],
                                              ALU.subtract).then_inc(o_lo, 1)

                        for k in range(6):
                            block_low(0, 0, k)
                        for h in range(2):
                            maximum(0, h)
                        normalize(0, 0)

                        def slot(j, p, b):
                            for i in range(H):
                                if i < H - 1:
                                    normalize(b, i + 1)
                                elif inside(b + 1, B):
                                    normalize(b + 1, 0)
                                if i == 0 and inside(b - 1, B):
                                    block_low(p, b, 5)
                                if i in READ_AT and inside(b + 1, B):
                                    block_low(1 - p, b + 1, READ_AT.index(i))
                                if i < H - 2:
                                    maximum(b, i + 2)
                                elif inside(b + 1, B):
                                    maximum(b + 1, i + 2 - H)
                                probs_read(j, p, b, i)
                                if i % G == 0:
                                    if i:
                                        out_low(b, i // G - 1)
                                    elif inside(b - 1, B):
                                        out_low(b - 1, KV - 1)

                        run_slots(dve, slot, B)
                        out_low(B - 1, KV - 1)

                    @block.tensor
                    def _(pe):
                        def project(p, b, step, count):
                            for m in range(step * count, (step + 1) * count):
                                k, r = divmod(m, BLOCK)
                                i, d = divmod(r, KD)
                                a, n = CH[k % 3]
                                if m == 0:
                                    pe.wait_ge(split_lo, KD * (b + 1))
                                if r == 0:
                                    wait(pe, kv_lo, 6 * b + k - 1)
                                u, w = PASSES[i]
                                last = mm(kv_ps[0:n, k % 2, 0:KW], cT[:, p, u, d, a:a + n],
                                          wkv_p[:, w, d, (k // 3) * KW:(k // 3 + 1) * KW], start=(r == 0), stop=(r == BLOCK - 1))
                                if r == BLOCK - 1:
                                    last.then_inc(kv_done, 1)

                        def key_transposes(b, c):
                            n = CH[c][1]
                            pe.wait_ge(kv_lo, 6 * b + c + 1)
                            wait(pe, kt_read, 3 * b + c)
                            for part in range(2):
                                for g in range(KV):
                                    o = (part * KV + g) * P
                                    last = pe.transpose(kt_ps[0:HD, o:o + n], kn[0:n, part, g * HD:(g + 1) * HD],
                                                        ident[0:n, 0:n])
                            last.then_inc(ktr, 1)

                        def scores(j, p, b, h):
                            n = H * b + h
                            if h == 0:
                                pe.wait_ge(kt_read, 3 * (b + 1))
                                pe.wait_ge(q_loaded[p], 64 * (j + 1))
                            wait(pe, exped, n - 1)
                            for i, (u, w) in enumerate(PASSES):
                                last = mm(s_ps[0:Q, h % 2, 0:SA], qT[:, p, u, h, :], kT[:, p, w, h // G, 0:SA],
                                          start=(i == 0), stop=(i == 2))
                            last.then_inc(scored, 1)

                        def prob_transposes(j, p, b, h):
                            pe.wait_ge(p_lo, H * b + h + 1)
                            wait(pe, pt_read[h % 2], 8 * b + h // 2)
                            for part in range(2):
                                for c, (a, n) in enumerate(KEYS):
                                    o = (part * 4 + c) * Q
                                    last = pe.transpose(pt_ps[0:n, h % 2, o:o + Q], pp[:, h % 2, part, a:a + n],
                                                        ident[0:Q, 0:Q])
                            last.then_inc(ptr, 1)

                        def attend(j, p, b, g):
                            if g == 0:
                                pe.wait_ge(kv_lo, 6 * (b + 1))
                                pe.wait_ge(kv_loaded[p], 16 * (j + 1))
                            for i in range(2):
                                pe.wait_ge(pt_read[i], 8 * b + 2 * g + 2)
                            wait(pe, o_lo, KV * b + g)
                            for i, (u, w) in enumerate(PASSES):
                                for c, (a, n) in enumerate(KEYS):
                                    last = mm(o_ps[0:HD, 0:G * Q], vv[0:n, p, c, u, g * HD:(g + 1) * HD],
                                              pT[0:n, g % 2, w, c, :, :],
                                              start=(i == 0 and c == 0), stop=(i == 2 and c == 3))
                            last.then_inc(pv, 1)

                        for k in range(6):
                            project(0, 0, k, BLOCK)
                            if k < 3:
                                key_transposes(0, k)
                        for h in range(2):
                            scores(0, 0, 0, h)
                        pe.wait_ge(pt_cleared, 2)

                        def slot(j, p, b):
                            for i in range(H):
                                if i < H - 2:
                                    scores(j, p, b, i + 2)
                                elif inside(b + 1, B):
                                    scores(j + p, 1 - p, b + 1, i + 2 - H)
                                prob_transposes(j, p, b, i)
                                if i % G == 0:
                                    if i:
                                        attend(j, p, b, i // G - 1)
                                    elif inside(b - 1, B):
                                        attend(j - 1 + p, 1 - p, b - 1, KV - 1)
                                if i - 1 in READ_AT[0:3] and inside(b + 1, B):
                                    key_transposes(b + 1, READ_AT.index(i - 1))
                                if inside(b + 1, B):
                                    project(1 - p, b + 1, i, PER_STEP)

                        run_slots(pe, slot, B)
                        attend(B // 2 - 1, 1, B - 1, KV - 1)

                del used[:]

            with ExitStack() as st:
                sb, pb = alloc(st)
                wo_p = sb("c_wo_p", [P, 2, KO, D], F16)
                stage = sb("c_stage", [P, 4, D], F32)
                xin = sb("c_x", [P, 2, D], F32)
                oT = sb("c_oT", [P, 2, 2, KO, P], F16)
                x1 = sb("c_x1", [P, 2, D], F32)
                w4 = sb("c_w4", [P, KD * D], BF16)
                y1 = sb("c_y1", [P, D], BF16)
                y1T = sb("c_y1T", [P, KD * P], BF16)
                f_b = sb("c_f", [P, 2, HALF], BF16)
                x2 = sb("c_x2", [P, 2, D + 4], F32)
                y2 = sb("c_y2", [P, D], F32)
                y2_p = sb("c_y2_p", [P, 2, D], F16)
                y2T = sb("c_y2T", [P, 2, KD * P], F16)
                t32 = sb("c_t32", [P, D], F32)
                t_p = sb("c_t_p", [P, 2, D], F16)
                tT = sb("c_tT", [P, 2, KD * P], F16)
                junk = sb("c_junk", [P, D], F32)
                qb = sb("c_qb", [P, 1], F32)
                x_ps = pb("c_x_ps", [P, 2, HALF], F32)
                f_ps = pb("c_f_ps", [P, 2, HALF], F32)
                t_ps = pb("c_t_ps", [P, 2, HALF], F32)
                tr = pb("c_tr", [P, 2, 1024], F16)

                w_loaded = [sem(f"c_w_loaded{i}") for i in range(4)]
                w_hi, w_lo = sem("c_w_hi"), sem("c_w_lo")
                w4_loaded = sem("c_w4_loaded")
                x_loaded = [sem(f"c_x_loaded{i}") for i in range(2)]
                o_loaded = [sem(f"c_o_loaded{i}") for i in range(2)]
                wo_done, x1_ready = sem("c_wo_done"), sem("c_x1_ready")
                y1_ready, y1tr, y1T_ready = sem("c_y1_ready"), sem("c_y1tr"), sem("c_y1T_ready")
                f_done, f_read, x2_ready = sem("c_f_done"), sem("c_f_read"), sem("c_x2_ready")
                y2_ready, y2_hi, y2_lo = sem("c_y2_ready"), sem("c_y2_hi"), sem("c_y2_lo")
                y2tr, y2T_hi, y2T_lo = sem("c_y2tr"), sem("c_y2T_hi"), sem("c_y2T_lo")
                dotted, qb_ready = sem("c_dotted"), sem("c_qb_ready")
                t_done, t32_ready, t_hi, t_lo = sem("c_t_done"), sem("c_t32_ready"), sem("c_t_hi"), sem("c_t_lo")
                ttr, tT_hi, tT_lo = sem("c_ttr"), sem("c_tT_hi"), sem("c_tT_lo")
                x2_stored = [sem(f"c_x2_stored{i}") for i in range(2)]
                t_stored = sem("c_t_stored")
                norm1_measure, norm1_root, norm1_scaled = layernorm(sb, sem, "c_norm1", neg_half)
                norm2_measure, norm2_root, norm2_scaled = layernorm(sb, sem, "c_norm2", neg_half)

                SLOTS = TILES + 2

                block = st.enter_context(nc.Block())

                @block.sync
                def _(sp):
                    def load(j, p, t):
                        wait(sp, x1_ready, 2 * (t - 1))
                        sp.dma_start(xin[:, p, :], x[rows(t, P), :]).then_inc(x_loaded[p], 16)
                        for part in range(2):
                            sp.dma_start(oT[:, p, part, :, :], o_s[part, :, rows(t, P)].rearrange(
                                "(k p) r -> p k r", p=P)).then_inc(o_loaded[p], 16)

                    load(0, 0, 0)
                    for k in range(KO):
                        wait(sp, w_lo, k - 3)
                        sp.dma_start(stage[:, k % 4, :], wo[:, k, :]).then_inc(w_loaded[k % 4], 16)
                    sp.dma_start(w4[:, :], w4_s[:, :]).then_inc(w4_loaded, 16)
                    load(0, 1, 1)

                    def slot(j, p, s):
                        if inside(s, TILES) and inside(s + 1, TILES) and not (isinstance(s, int) and s == 0):
                            load(j + p, 1 - p, s + 1)
                        if inside(s - 1, TILES):
                            sp.wait_ge(x2_ready, 2 * s)
                            sp.wait_ge(qb_ready, s)
                            sp.dma_start(x2_s[rows(s - 1, P), 0:D + 1], x2[:, 1 - p, 0:D + 1]
                                         ).then_inc(x2_stored[1 - p], 16)

                    run_slots(sp, slot, SLOTS, 4)
                    for i in range(2):
                        sp.wait_ge(x2_stored[i], 16 * (TILES // 2))
                    sp.wait_ge(t_stored, 32 * TILES)

                @block.gpsimd
                def _(pool):
                    def slot(j, p, s):
                        if inside(s - 2, TILES):
                            pool.wait_ge(t_hi, s - 1)
                            pool.tensor_tensor(t_p[:, 1, :], t32[:, :], t_p[:, 0, :], ALU.subtract).then_inc(t_lo, 1)
                        if inside(s - 1, TILES):
                            norm2_root(pool, P, s - 1)
                            pool.wait_ge(y2_hi, s)
                            pool.tensor_tensor(y2_p[:, 1, :], y2[:, :], y2_p[:, 0, :], ALU.subtract).then_inc(y2_lo, 1)
                        if inside(s, TILES):
                            norm1_root(pool, P, s)

                    run_slots(pool, slot, SLOTS, 4)

                @block.scalar
                def _(act):
                    for k in range(KO):
                        act.wait_ge(w_loaded[k % 4], 16 * (k // 4 + 1))
                        act.activation(wo_p[:, 0, k, :], stage[:, k % 4, :], ACT.Copy, scale=WS).then_inc(w_hi, 1)

                    def slot(j, p, s):
                        if inside(s - 1, TILES):
                            act.wait_ge(y1tr, s)
                            act.activation(y1T[:, :], tr[:, 0, :].bitcast(BF16), ACT.Copy).then_inc(y1T_ready, 1)
                        if inside(s - 2, TILES):
                            act.wait_ge(t32_ready, 2 * (s - 1))
                            wait(act, ttr, s - 2)
                            act.activation(t_p[:, 0, :], t32[:, :], ACT.Copy).then_inc(t_hi, 1)
                        if inside(s - 1, TILES):
                            for h in range(2):
                                act.wait_ge(f_done, 2 * (s - 1) + h + 1)
                                wait(act, x2_ready, 2 * (s - 2) + h + 1)
                                act.activation(f_b[:, h, :], f_ps[:, h, :], ACT.Copy).then_inc(f_read, 1)
                        if inside(s - 2, TILES):
                            act.wait_ge(ttr, s - 1)
                            wait(act, t_stored, 32 * (s - 2))
                            act.activation(tT[:, 0, :], tr[:, 0, :], ACT.Copy).then_inc(tT_hi, 1)
                        if inside(s - 1, TILES):
                            act.wait_ge(y2_ready, s)
                            wait(act, y2tr, s - 1)
                            act.activation(y2_p[:, 0, :], y2[:, :], ACT.Copy).then_inc(y2_hi, 1)
                        if inside(s - 2, TILES):
                            act.wait_ge(tT_hi, s - 1)
                            act.wait_ge(tT_lo, s - 1)
                            for part in range(2):
                                act.dma_start(t_s[part, :, :, rows(s - 2, P)],
                                              tT[:, part, :].rearrange("p (k r) -> p k r", k=KD)).then_inc(t_stored, 16)
                        if inside(s - 1, TILES):
                            act.wait_ge(y2tr, s)
                            act.activation(y2T[:, 0, :], tr[:, 0, :], ACT.Copy).then_inc(y2T_hi, 1)

                    run_slots(act, slot, SLOTS, 4)

                @block.vector
                def _(dve):
                    for k in range(KO):
                        dve.wait_ge(w_hi, k + 1)
                        dve.scalar_tensor_tensor(out=wo_p[:, 1, k, :], in0=stage[:, k % 4, :], scalar=WS,
                                                 in1=wo_p[:, 0, k, :], op0=ALU.mult, op1=ALU.subtract).then_inc(w_lo, 1)

                    def residual1(j, p, t, h):
                        cols = slice(h * HALF, (h + 1) * HALF)
                        if h == 0:
                            dve.wait_ge(x_loaded[p], 16 * (j + 1))
                        dve.wait_ge(wo_done, 2 * t + h + 1)
                        dve.scalar_tensor_tensor(out=x1[:, p, cols], in0=x_ps[:, h, :], scalar=tg_wo[:, :],
                                                 in1=xin[:, p, cols], op0=ALU.mult, op1=ALU.add).then_inc(x1_ready, 1)

                    def slot(j, p, s):
                        if inside(s, TILES):
                            residual1(j, p, s, 0)
                        if inside(s - 1, TILES):
                            t = s - 1
                            if inside(t - 2, TILES):
                                dve.wait_ge(x2_stored[1 - p], 16 * (j - 1 + p))
                            for h in range(2):
                                cols = slice(h * HALF, (h + 1) * HALF)
                                dve.wait_ge(f_read, 2 * t + h + 1)
                                dve.scalar_tensor_tensor(out=x2[:, 1 - p, cols], in0=f_b[:, h, :], scalar=tg[:, 1:2],
                                                         in1=x1[:, 1 - p, cols], op0=ALU.mult, op1=ALU.add
                                                         ).then_inc(x2_ready, 1)
                            dve.wait_ge(x2_ready, 2 * t + 2)
                            norm2_measure(dve, x2[:, 1 - p, 0:D], P, t)
                            wait(dve, y2_lo, t)
                            norm2_scaled(dve, y2[:, :], x2[:, 1 - p, 0:D], P, t).then_inc(y2_ready, 1)
                        if inside(s - 2, TILES):
                            dve.wait_ge(ttr, s - 1)
                            wait(dve, t_stored, 32 * (s - 2))
                            dve.tensor_copy(tT[:, 1, :], tr[:, 1, :]).then_inc(tT_lo, 1)
                        if inside(s - 1, TILES):
                            dve.wait_ge(y2_ready, s)
                            dve.tensor_tensor_reduce(out=junk[:, :], in0=y2[:, :], in1=u_bc[:, :], scale=1.0, scalar=0.0,
                                                     op0=ALU.mult, op1=ALU.add, accum_out=qb[:, :]).then_inc(dotted, 1)
                            dve.wait_ge(dotted, s)
                            dve.tensor_scalar(x2[:, 1 - p, D:D + 1], qb[:, :], s0[:, 0:1], None,
                                              ALU.add).then_inc(qb_ready, 1)
                        if inside(s, TILES):
                            residual1(j, p, s, 1)
                            dve.wait_ge(x1_ready, 2 * s + 2)
                            norm1_measure(dve, x1[:, p, :], P, s)
                        if inside(s - 1, TILES):
                            dve.wait_ge(y2tr, s)
                            dve.tensor_copy(y2T[:, 1, :], tr[:, 1, :]).then_inc(y2T_lo, 1)
                        if inside(s, TILES):
                            wait(dve, y1tr, s)
                            norm1_scaled(dve, y1[:, :], x1[:, p, :], P, s).then_inc(y1_ready, 1)
                        if inside(s - 1, TILES):
                            wait(dve, t_lo, s - 1)
                            for h in range(2):
                                cols = slice(h * HALF, (h + 1) * HALF)
                                dve.wait_ge(t_done, 2 * (s - 1) + h + 1)
                                dve.scalar_tensor_tensor(out=t32[:, cols], in0=t_ps[:, h, :], scalar=1.0 / MS,
                                                         in1=c_bc[:, cols], op0=ALU.mult, op1=ALU.add
                                                         ).then_inc(t32_ready, 1)

                    run_slots(dve, slot, SLOTS, 4)

                @block.tensor
                def _(pe):
                    def out_proj(j, p, t, h):
                        if h == 0:
                            pe.wait_ge(o_loaded[p], 32 * (j + 1))
                        wait(pe, x1_ready, 2 * (t - 1) + h + 1)
                        for n, (a, b) in enumerate(PASSES):
                            for k in range(KO):
                                last = mm(x_ps[:, h, :], oT[:, p, a, k, :], wo_p[:, b, k, h * HALF:(h + 1) * HALF],
                                          start=(n == 0 and k == 0), stop=(n == 2 and k == KO - 1))
                        last.then_inc(wo_done, 1)

                    def both_parts(src, done):
                        for part in range(2):
                            for k in range(KD):
                                last = pe.transpose(tr[:, part, k * P:(k + 1) * P], src[:, part, k * P:(k + 1) * P],
                                                    ident[:, :])
                        last.then_inc(done, 1)

                    pe.wait_ge(w_lo, KO)

                    def slot(j, p, s):
                        if inside(s - 1, TILES):
                            pe.wait_ge(y1_ready, s)
                            for k in range(KD):
                                last = pe.transpose(tr[:, 0, k * P:(k + 1) * P].bitcast(BF16), y1[:, k * P:(k + 1) * P],
                                                    identb[:, :])
                            last.then_inc(y1tr, 1)
                        if inside(s, TILES):
                            out_proj(j, p, s, 0)
                        if inside(s - 1, TILES):
                            pe.wait_ge(y1T_ready, s)
                            if isinstance(s, int) and s == 1:
                                pe.wait_ge(w4_loaded, 16)
                            for h in range(2):
                                wait(pe, f_read, 2 * (s - 2) + h + 1)
                                for k in range(KD):
                                    last = mm(f_ps[:, h, :], y1T[:, k * P:(k + 1) * P], w4[:, k * D + h * HALF:k * D + (h + 1) * HALF],
                                              start=(k == 0), stop=(k == KD - 1))
                                last.then_inc(f_done, 1)
                        if inside(s - 2, TILES):
                            pe.wait_ge(t_lo, s - 1)
                            both_parts(t_p, ttr)
                        if inside(s, TILES):
                            out_proj(j, p, s, 1)
                        if inside(s - 1, TILES):
                            pe.wait_ge(y2_lo, s)
                            if inside(s - 2, TILES):
                                pe.wait_ge(tT_hi, s - 1)
                                pe.wait_ge(tT_lo, s - 1)
                            both_parts(y2_p, y2tr)
                            pe.wait_ge(y2T_hi, s)
                            pe.wait_ge(y2T_lo, s)
                            for h in range(2):
                                wait(pe, t32_ready, 2 * (s - 2) + h + 1)
                                for n, (a, b) in enumerate(PASSES):
                                    for k in range(KD):
                                        last = mm(t_ps[:, h, :], y2T[:, a, k * P:(k + 1) * P],
                                                  Mt[:, b, k, h * HALF:(h + 1) * HALF],
                                                  start=(n == 0 and k == 0), stop=(n == 2 and k == KD - 1))
                                last.then_inc(t_done, 1)

                    run_slots(pe, slot, SLOTS, 4)


        AG = LR + NG
        with ExitStack() as st:
            sb, pb = alloc(st)
            w1_p = sb("d_w1_p", [P, 2, KD, D], F16)
            wag_p = sb("d_wag_p", [P, 2, KD, AG], F16)
            wb_p = sb("d_wb_p", [LR, 2, D], F16)
            stage = sb("d_stage", [P, 2, D], F32)
            ag_in = sb("d_ag_in", [P, KD, AG], F32)
            b_in = sb("d_b_in", [LR, D], F32)
            tg_b = sb("d_tg_b", [P, D], F32)
            gate_bias = sb("d_gate_bias", [P, NG], F32)
            cn_raw = sb("d_cn_raw", [P, 3, D], F32)
            ct_raw = sb("d_ct_raw", [P, KD, S], F32)
            cn = sb("d_cn", [P, 2, 3, D], F16)
            cT = sb("d_cT", [P, 2, KD, S + 1], F16)
            tT = sb("d_tT", [P, 2, 2, KD, Q], F16)
            x2 = sb("d_x2", [Q, 2, D + 4], F32)
            ex = sb("d_exp", [Q, S + 1], F32)
            pn = sb("d_prob", [Q, S + 1], F32)
            pp = sb("d_prob_p", [Q, 2, S + 1], F16)
            pT = sb("d_probT", [P, 2, 3, Q], F16)
            x3 = sb("d_x3", [Q, D], F32)
            x3b = sb("d_x3b", [Q, 2, D], F32)
            y3 = sb("d_y3", [Q, D], F32)
            y3_p = sb("d_y3_p", [Q, 2, D], F16)
            y3T = sb("d_y3T", [P, 2, KD, Q], F16)
            low = sb("d_low", [Q, LR], F32)
            low_p = sb("d_low_p", [Q, 2, P], F16)
            lowT = sb("d_lowT", [LR, 2, Q], F16)
            sm = sb("d_small", [Q, 24], F32)
            gs = sb("d_gs", [Q, NG], F32)
            gp = sb("d_gp", [Q, NG], F32)
            res = sb("d_res", [Q, 2, D], F32)
            s_ps = pb("d_s_ps", [P, HALF], F32)
            a_ps = pb("d_a_ps", [P, 2, HALF], F32)
            f_ps = pb("d_f_ps", [P, 2, HALF], F32)
            ag_ps = pb("d_ag_ps", [P, HALF], F32)
            tr = pb("d_tr", [P, 2, 1024], F16)

            w_loaded = [sem(f"d_w_loaded{i}") for i in range(2)]
            w_hi, w_lo = sem("d_w_hi"), sem("d_w_lo")
            small_loaded, small_split, small_ready = sem("d_small_loaded"), sem("d_small_split"), sem("d_small_ready")
            cn_loaded, ct_loaded = sem("d_cn_loaded"), sem("d_ct_loaded")
            tx_loaded = [sem(f"d_tx_loaded{i}") for i in range(2)]
            cn_hi, cn_lo, ct_hi, ct_lo = sem("d_cn_hi"), sem("d_cn_lo"), sem("d_ct_hi"), sem("d_ct_lo")
            scored, maxed, biased, exped = sem("d_scored"), sem("d_maxed"), sem("d_biased"), sem("d_exped")
            shifted = sem("d_shifted")
            inverted, normed, p_hi, p_lo = sem("d_inverted"), sem("d_normed"), sem("d_p_hi"), sem("d_p_lo")
            ptr, pT_ready = sem("d_ptr"), sem("d_pT_ready")
            attended, x3_ready, x3b_ready = sem("d_attended"), sem("d_x3_ready"), sem("d_x3b_ready")
            y3_ready, y3_hi, y3_lo = sem("d_y3_ready"), sem("d_y3_hi"), sem("d_y3_lo")
            y3tr, y3T_hi, y3T_lo = sem("d_y3tr"), sem("d_y3T_hi"), sem("d_y3T_lo")
            ag_done, gate, gate_exp = sem("d_ag_done"), sem("d_gate"), sem("d_gate_exp")
            low_hi, low_lo, ltr, lowT_ready = sem("d_low_hi"), sem("d_low_lo"), sem("d_ltr"), sem("d_lowT_ready")
            ffn_done, res_ready = sem("d_ffn_done"), sem("d_res_ready")
            stored = [sem(f"d_stored{i}") for i in range(2)]
            norm_measure, norm_root, norm_scaled = layernorm(sb, sem, "d_norm", neg_half)

            SCALE = D ** -0.5
            GATE_STEPS = 9

            block = st.enter_context(nc.Block())

            def split_weights(eng_steps):
                return [(w1_p[:, :, k, :], stage[:, k % 2, :]) for k in range(KD)]

            @block.sync
            def _(sp):
                sp.dma_start(ag_in[:, :, :], wag).then_inc(small_loaded, 16)
                sp.dma_start(b_in[:, :], wb).then_inc(small_loaded, 16)
                sp.dma_start(tg_b[:, :], b1.to_broadcast([P, D])).then_inc(small_loaded, 16)
                sp.dma_start(gate_bias[:, :], gate_b.to_broadcast([P, NG])).then_inc(small_loaded, 16)

                def load_context(b):
                    wait(sp, cn_lo, 3 * b)
                    for c, (a, n) in enumerate(CH):
                        sp.dma_start(cn_raw[0:n, c, :], ctx_nat[bass.ds(b, 1), a:a + n, :].rearrange(
                            "b s d -> (b s) d")).then_inc(cn_loaded, 16)
                    wait(sp, ct_lo, KD * b)
                    sp.dma_start(ct_raw[:, :, :], ctx_t[bass.ds(b, 1), :, :, :].rearrange("b p k s -> p (b k) s")
                                 ).then_inc(ct_loaded, 16)

                def load_rows(p, b):
                    wait(sp, x3_ready, 2 * (b - 1))
                    for part in range(2):
                        sp.dma_start(tT[:, p, part, :, :], t_s[part, :, :, rows(b, Q)]).then_inc(tx_loaded[p], 16)
                    sp.dma_start(x2[:, p, 0:D + 1], x2_s[rows(b, Q), 0:D + 1]).then_inc(tx_loaded[p], 16)

                load_context(0)
                load_rows(0, 0)
                for k in range(KD):
                    wait(sp, w_lo, k - 1)
                    sp.dma_start(stage[:, k % 2, :], w1[:, k, :]).then_inc(w_loaded[k % 2], 16)
                load_rows(1, 1)

                def slot(j, p, s):
                    if inside(s + 1, B):
                        load_context(s + 1)
                        if not (isinstance(s, int) and s == 0):
                            load_rows(1 - p, s + 1)
                    if inside(s - 1, B):
                        sp.wait_ge(res_ready, 2 * s)
                        sp.dma_start(out[rows(s - 1, Q), :], res[:, 1 - p, :]).then_inc(stored[1 - p], 16)

                run_slots(sp, slot, B + 2, 4)
                for i in range(2):
                    sp.wait_ge(stored[i], 16 * (B // 2))

            def split_pieces():
                cts = [(ct_raw[:, k, :], cT[:, 0, k, 0:S], cT[:, 1, k, 0:S], ct_hi, ct_lo, KD, k, ct_loaded, 16)
                       for k in range(KD)]
                cns = [(cn_raw[0:n, c, :], cn[0:n, 0, c, :], cn[0:n, 1, c, :], cn_hi, cn_lo, 3, c, cn_loaded, 48)
                       for c, (a, n) in enumerate(CH)]
                return cts, cns

            @block.gpsimd
            def _(pool):
                cts, cns = split_pieces()

                def piece(b, item):
                    raw, high, lo_dst, hi_sem, lo_sem, per, i, _, _ = item
                    pool.wait_ge(hi_sem, per * b + i + 1)
                    pool.tensor_tensor(lo_dst, raw, high, ALU.subtract).then_inc(lo_sem, 1)

                for item in cts + cns:
                    piece(0, item)

                def slot(j, p, s):
                    if inside(s, B):
                        pool.wait_ge(p_hi, s + 1)
                        wait(pool, ptr, s)
                        pool.tensor_tensor(pp[:, 1, 0:S], pn[:, 0:S], pp[:, 0, 0:S], ALU.subtract).then_inc(p_lo, 1)
                    if inside(s + 1, B):
                        for item in cts:
                            piece(s + 1, item)
                    if inside(s, B):
                        norm_root(pool, Q, s)
                        pool.wait_ge(y3_hi, s + 1)
                        pool.tensor_tensor(y3_p[:, 1, :], y3[:, :], y3_p[:, 0, :], ALU.subtract).then_inc(y3_lo, 1)
                    if inside(s + 1, B):
                        for item in cns:
                            piece(s + 1, item)

                run_slots(pool, slot, B + 2, 4)

            @block.scalar
            def _(act):
                cts, cns = split_pieces()
                act.wait_ge(small_loaded, 64)
                act.activation(wag_p[:, 0, :, :], ag_in[:, :, :], ACT.Copy, scale=WS).then_inc(small_split, 1)
                act.activation(wb_p[:, 0, :], b_in[:, :], ACT.Copy, scale=WS).then_inc(small_split, 1)

                def piece(b, item):
                    raw, high, _, hi_sem, _, per, i, ld, inc = item
                    if i == 0:
                        act.wait_ge(ld, inc * (b + 1))
                        wait(act, scored if per == KD else attended, b if per == KD else 2 * b)
                    act.activation(high, raw, ACT.Copy).then_inc(hi_sem, 1)

                for item in cts + cns:
                    piece(0, item)
                for k in range(KD):
                    act.wait_ge(w_loaded[k % 2], 16 * (k // 2 + 1))
                    act.activation(w1_p[:, 0, k, :], stage[:, k % 2, :], ACT.Copy, scale=WS).then_inc(w_hi, 1)

                def slot(j, p, s):
                    if inside(s - 1, B):
                        act.wait_ge(y3tr, s)
                        act.activation(y3T[:, 0, :, :], tr[:, 0, 0:KD * Q].rearrange("p (k r) -> p k r", k=KD),
                                       ACT.Copy).then_inc(y3T_hi, 1)
                    if inside(s, B):
                        act.wait_ge(biased, s + 1)
                        wait(act, normed, s)
                        act.activation(ex[:, 0:S], s_ps[0:Q, 0:S], ACT.Exp, bias=sm[:, 2:3], scale=SCALE,
                                       accum_out=sm[:, 3:4]).then_inc(exped, 1)
                    if inside(s - 1, B):
                        act.wait_ge(gate, GATE_STEPS * (s - 1) + 3)
                        act.activation(gp[:, :], gs[:, :], ACT.Exp, accum_out=sm[:, 12:13]).then_inc(gate_exp, 1)
                    if inside(s, B):
                        act.wait_ge(ptr, s + 1)
                        for c, (a, n) in enumerate(CH):
                            for part in range(2):
                                o = (part * 3 + c) * Q
                                act.activation(pT[0:n, part, c, :], tr[0:n, 0, o:o + Q], ACT.Copy).then_inc(pT_ready, 1)
                    if inside(s - 1, B):
                        act.wait_ge(ltr, s)
                        act.activation(lowT[:, :, :], tr[0:LR, 1, 0:2 * Q].rearrange("p (l r) -> p l r", l=2),
                                       ACT.Copy).then_inc(lowT_ready, 1)
                    if inside(s + 1, B):
                        for item in cts:
                            piece(s + 1, item)
                    if inside(s, B):
                        act.wait_ge(y3_ready, s + 1)
                        wait(act, y3tr, s)
                        act.activation(y3_p[:, 0, :], y3[:, :], ACT.Copy).then_inc(y3_hi, 1)
                    if inside(s + 1, B):
                        for item in cns:
                            piece(s + 1, item)

                run_slots(act, slot, B + 2, 4)

            @block.vector
            def _(dve):
                dve.memset(low_p[:, :, :].rearrange("q l c -> q (l c)"), 0.0).then_inc(small_ready, 1)
                dve.wait_ge(small_loaded, 64)
                dve.wait_ge(small_split, 2)
                dve.scalar_tensor_tensor(out=wag_p[:, 1, :, :], in0=ag_in[:, :, :], scalar=WS, in1=wag_p[:, 0, :, :],
                                         op0=ALU.mult, op1=ALU.subtract).then_inc(small_ready, 1)
                dve.scalar_tensor_tensor(out=wb_p[:, 1, :], in0=b_in[:, :], scalar=WS, in1=wb_p[:, 0, :],
                                         op0=ALU.mult, op1=ALU.subtract).then_inc(small_ready, 1)
                dve.tensor_scalar(tg_b[:, :], tg_b[:, :], tg[:, 3:4], None, ALU.mult).then_inc(small_ready, 1)
                for k in range(KD):
                    dve.wait_ge(w_hi, k + 1)
                    dve.scalar_tensor_tensor(out=w1_p[:, 1, k, :], in0=stage[:, k % 2, :], scalar=WS,
                                             in1=w1_p[:, 0, k, :], op0=ALU.mult, op1=ALU.subtract).then_inc(w_lo, 1)
                dve.wait_ge(small_ready, 4)

                def softmax_head(j, p, s):
                    dve.wait_ge(scored, s + 1)
                    dve.wait_ge(tx_loaded[p], 48 * (j + 1))
                    wait(dve, exped, s)
                    dve.tensor_reduce(sm[:, 0:1], s_ps[0:Q, 0:S], AX.X, ALU.max).then_inc(maxed, 1)
                    dve.wait_ge(maxed, s + 1)
                    dve.tensor_scalar(sm[:, 1:2], sm[:, 0:1], x2[:, p, D:D + 1], None, ALU.add).then_inc(shifted, 1)
                    dve.wait_ge(shifted, s + 1)
                    dve.tensor_scalar(sm[:, 2:3], x2[:, p, D:D + 1], sm[:, 1:2], SCALE, ALU.subtract,
                                      ALU.mult).then_inc(biased, 1)

                def softmax_tail(s):
                    dve.wait_ge(exped, s + 1)
                    dve.reciprocal(sm[:, 4:5], sm[:, 3:4]).then_inc(inverted, 1)
                    dve.wait_ge(inverted, s + 1)
                    wait(dve, p_lo, s)
                    dve.tensor_scalar(pn[:, 0:S], ex[:, 0:S], sm[:, 4:5], None, ALU.mult).then_inc(normed, 1)
                    dve.wait_ge(normed, s + 1)
                    wait(dve, ptr, s)
                    dve.tensor_copy(pp[:, 0, 0:S], pn[:, 0:S]).then_inc(p_hi, 1)

                def gate_head(t):
                    base = GATE_STEPS * t
                    dve.wait_ge(ag_done, t + 1)
                    dve.scalar_tensor_tensor(out=gs[:, :], in0=ag_ps[0:Q, LR:AG], scalar=1.0 / WS,
                                             in1=gate_bias[0:Q, :], op0=ALU.mult, op1=ALU.add).then_inc(gate, 1)
                    dve.wait_ge(gate, base + 1)
                    dve.tensor_reduce(sm[:, 5:6], gs[:, :], AX.X, ALU.max).then_inc(gate, 1)
                    dve.wait_ge(gate, base + 2)
                    dve.tensor_scalar(gs[:, :], gs[:, :], sm[:, 5:6], None, ALU.subtract).then_inc(gate, 1)

                def gate_tail(t):
                    base = GATE_STEPS * t
                    dve.wait_ge(gate_exp, t + 1)
                    dve.reciprocal(sm[:, 13:14], sm[:, 12:13]).then_inc(gate, 1)
                    dve.wait_ge(gate, base + 4)
                    dve.tensor_scalar(gp[:, :], gp[:, :], sm[:, 13:14], None, ALU.mult).then_inc(gate, 1)
                    dve.wait_ge(gate, base + 5)
                    dve.tensor_tensor_scan(sm[:, 8:12], gp[:, :], gp[:, :], 0.0, ALU.max, ALU.max).then_inc(gate, 1)
                    dve.wait_ge(gate, base + 6)
                    dve.reciprocal(sm[:, 14:15], sm[:, 11:12]).then_inc(gate, 1)
                    dve.tensor_scalar(sm[:, 16:19], sm[:, 8:11], sm[:, 11:12], None, ALU.is_lt).then_inc(gate, 1)
                    dve.wait_ge(gate, base + 8)
                    dve.tensor_scalar(sm[:, 15:16], sm[:, 11:12], sm[:, 14:15], 1.0 / WS, ALU.mult,
                                      ALU.mult).then_inc(gate, 1)
                    dve.wait_ge(gate, base + 9)
                    wait(dve, low_lo, t)
                    dve.tensor_scalar(low[:, 0:RANKS[0]], ag_ps[0:Q, 0:RANKS[0]], sm[:, 15:16], None,
                                      ALU.mult).then_inc(low_hi, 1)
                    for i in range(3):
                        a, b = RANKS[i], RANKS[i + 1]
                        dve.tensor_scalar(low[:, a:b], ag_ps[0:Q, a:b], sm[:, 16 + i:17 + i], sm[:, 15:16],
                                          ALU.mult, ALU.mult).then_inc(low_hi, 1)
                    dve.wait_ge(low_hi, 5 * t + 4)
                    wait(dve, ltr, t)
                    dve.tensor_copy(low_p[:, 0, 0:LR], low[:, :]).then_inc(low_hi, 1)
                    dve.wait_ge(low_hi, 5 * t + 5)
                    dve.tensor_tensor(low_p[:, 1, 0:LR], low[:, :], low_p[:, 0, 0:LR], ALU.subtract).then_inc(low_lo, 1)

                def slot(j, p, s):
                    if inside(s - 1, B):
                        dve.wait_ge(y3tr, s)
                        dve.tensor_copy(y3T[:, 1, :, :], tr[:, 1, 0:KD * Q].rearrange("p (k r) -> p k r", k=KD)
                                        ).then_inc(y3T_lo, 1)
                    if inside(s, B):
                        softmax_head(j, p, s)
                    if inside(s - 1, B):
                        gate_head(s - 1)
                    if inside(s, B):
                        softmax_tail(s)
                    if inside(s - 1, B):
                        gate_tail(s - 1)
                    if inside(s, B):
                        for h in range(2):
                            cols = slice(h * HALF, (h + 1) * HALF)
                            dve.wait_ge(attended, 2 * s + h + 1)
                            dve.scalar_tensor_tensor(out=x3[:, cols], in0=a_ps[0:Q, h, :], scalar=tg[0:Q, 2:3],
                                                     in1=x2[:, p, cols], op0=ALU.mult, op1=ALU.add
                                                     ).then_inc(x3_ready, 1)
                        dve.wait_ge(x3_ready, 2 * s + 2)
                        norm_measure(dve, x3[:, :], Q, s)
                        wait(dve, y3_lo, s)
                        norm_scaled(dve, y3[:, :], x3[:, :], Q, s).then_inc(y3_ready, 1)
                        dve.tensor_tensor(x3b[:, p, :], x3[:, :], tg_b[0:Q, :], ALU.add).then_inc(x3b_ready, 1)
                    if inside(s - 1, B):
                        if inside(s - 3, B):
                            dve.wait_ge(stored[1 - p], 16 * (j - 1 + p))
                        dve.wait_ge(x3b_ready, s)
                        for h in range(2):
                            cols = slice(h * HALF, (h + 1) * HALF)
                            dve.wait_ge(ffn_done, 2 * (s - 1) + h + 1)
                            dve.scalar_tensor_tensor(out=res[:, 1 - p, cols], in0=f_ps[0:Q, h, :],
                                                     scalar=tg_w1[0:Q, :], in1=x3b[:, 1 - p, cols],
                                                     op0=ALU.mult, op1=ALU.add).then_inc(res_ready, 1)

                run_slots(dve, slot, B + 2, 4)

            @block.tensor
            def _(pe):
                def ffn(t, h):
                    wait(pe, res_ready, 2 * (t - 1) + h + 1)
                    for n, (a, b) in enumerate(PASSES):
                        for k in range(KD):
                            mm(f_ps[0:Q, h, :], y3T[:, a, k, :], w1_p[:, b, k, h * HALF:(h + 1) * HALF],
                               start=(n == 0 and k == 0), stop=False)

                def scores(p, n):
                    for k in range(KD):
                        last = mm(s_ps[0:Q, 0:S], tT[:, p, PASSES[n][0], k, :], cT[:, PASSES[n][1], k, 0:S],
                                  start=(n == 0 and k == 0), stop=(n == 2 and k == KD - 1))
                    return last

                def low_rank(t):
                    pe.wait_ge(lowT_ready, t + 1)
                    for h in range(2):
                        for n, (a, b) in enumerate(PASSES):
                            last = mm(f_ps[0:Q, h, :], lowT[:, a, :], wb_p[:, b, h * HALF:(h + 1) * HALF],
                                      start=False, stop=(n == 2))
                        last.then_inc(ffn_done, 1)

                def slot(j, p, s):
                    if inside(s, B):
                        pe.wait_ge(ct_lo, KD * (s + 1))
                        pe.wait_ge(tx_loaded[p], 48 * (j + 1))
                        wait(pe, exped, s)
                        for n in range(2):
                            scores(p, n)
                    if inside(s - 1, B):
                        pe.wait_ge(y3_lo, s)
                        if inside(s - 2, B):
                            pe.wait_ge(lowT_ready, s - 1)
                            pe.wait_ge(pT_ready, 6 * s)
                        for part in range(2):
                            for k in range(KD):
                                last = pe.transpose(tr[:, part, k * Q:(k + 1) * Q], y3_p[:, part, k * P:(k + 1) * P],
                                                    ident[0:Q, 0:Q])
                        last.then_inc(y3tr, 1)
                    if inside(s, B):
                        scores(p, 2).then_inc(scored, 1)
                    if inside(s - 1, B):
                        pe.wait_ge(y3T_hi, s)
                        pe.wait_ge(y3T_lo, s)
                        wait(pe, low_lo, s - 1)
                        if isinstance(s, int) and s == 1:
                            pe.wait_ge(w_lo, KD)
                            pe.wait_ge(small_ready, 4)
                        for n, (a, b) in enumerate(PASSES):
                            for k in range(KD):
                                last = mm(ag_ps[0:Q, 0:AG], y3T[:, a, k, :], wag_p[:, b, k, :],
                                          start=(n == 0 and k == 0), stop=(n == 2 and k == KD - 1))
                        last.then_inc(ag_done, 1)
                        ffn(s - 1, 0)
                    if inside(s, B):
                        pe.wait_ge(p_lo, s + 1)
                        for part in range(2):
                            for c, (a, n) in enumerate(CH):
                                o = (part * 3 + c) * Q
                                last = pe.transpose(tr[0:n, 0, o:o + Q], pp[:, part, a:a + n], ident[0:Q, 0:Q])
                        last.then_inc(ptr, 1)
                    if inside(s - 1, B):
                        pe.wait_ge(low_lo, s)
                        for part in range(2):
                            last = pe.transpose(tr[:, 1, part * Q:(part + 1) * Q], low_p[:, part, :],
                                                ident[0:Q, 0:Q])
                        last.then_inc(ltr, 1)
                    if inside(s, B):
                        pe.wait_ge(cn_lo, 3 * (s + 1))
                        pe.wait_ge(pT_ready, 6 * (s + 1))
                        for h in range(2):
                            wait(pe, x3_ready, 2 * (s - 1) + h + 1)
                            for i, (a, b) in enumerate(PASSES):
                                for c, (_, n) in enumerate(CH):
                                    last = mm(a_ps[0:Q, h, :], pT[0:n, a, c, :],
                                              cn[0:n, b, c, h * HALF:(h + 1) * HALF],
                                              start=(i == 0 and c == 0), stop=(i == 2 and c == 2))
                            last.then_inc(attended, 1)
                    if inside(s - 1, B):
                        ffn(s - 1, 1)
                        low_rank(s - 1)

                run_slots(pe, slot, B + 2, 4)


def chunked(a):
    import numpy as np
    return np.ascontiguousarray(a.reshape(-1, P, a.shape[1]).transpose(1, 0, 2))


def kernel(**inputs):
    import numpy as np
    import concourse.bacc as bacc
    from concourse.bass_utils import run_bass_kernel_spmd as run

    i = {k: np.asarray(v) for k, v in inputs.items()}
    ctx = i["ctx_4096"]
    arrays = {
        "x": i["x"].reshape(R, D),
        "ctx_nat": ctx,
        "ctx_t": ctx.reshape(B, S, KD, P).transpose(0, 3, 2, 1),
        "gates": np.stack([i["g_xattn"][0], i["g_ffn"][0], i["g_xattn"][1], i["g_ffn"][1]]).reshape(1, 4),
        "wa": chunked(np.concatenate([i["L0_xattn_Wq"], i["L0_xattn_Wk"], i["L0_xattn_Wv"]], 0).T),
        "wo": chunked(i["L0_xattn_Wo"].T),
        "q4": chunked(i["L0_ffn_weight_q"].T),
        "sc4": i["L0_ffn_weight_scales"].T,
        "wq1": chunked(i["L1_xattn_Wq"]),
        "wk1": chunked(i["L1_xattn_Wk"]),
        "bq1": i["L1_xattn_bq"].reshape(KD, P).T,
        "bk1": i["L1_xattn_bk"].reshape(KD, P).T,
        "w1": chunked(i["L1_ffn_W"].T),
        "b1": i["L1_ffn_b"].reshape(1, D),
        "wag": chunked(np.concatenate([i["L1_ffn_A"], i["L1_ffn_gate_w"]], 0).T),
        "wb": i["L1_ffn_B"].T,
        "gate_b": i["L1_ffn_gate_b"].reshape(1, NG),
    }
    nc = bacc.Bacc("TRN2", target_bir_lowering=False, num_devices=1)
    arrays = {f"in_{k}": np.ascontiguousarray(v) for k, v in arrays.items()}
    args = [nc.dram_tensor(k, v.shape, mybir.dt.from_np(v.dtype), kind="ExternalInput").ap()
            for k, v in arrays.items()]
    out = nc.dram_tensor("out_rows", [R, D], F32, kind="ExternalOutput").ap()
    build(nc, *args, out)
    r = run(nc, [arrays], core_ids=[0])
    return r.results[0]["out_rows"].reshape(B, Q, D)
```

```python
from contextlib import ExitStack

import concourse.bass as bass
from concourse import mybir

F32 = mybir.dt.float32
F16 = mybir.dt.float16
BF16 = mybir.dt.bfloat16
I32 = mybir.dt.int32
ALU = mybir.AluOpType
ACT = mybir.ActivationFunctionType
AX = mybir.AxisListType

P = 128
B, Q, D = 16, 112, 1024
S = 375
R = B * Q
TILES = R // P
KD = D // P
H, KV, HD = 16, 4, 96
G = H // KV
QW, KW = H * HD, KV * HD
WA = QW + 2 * KW
KO = QW // P
KO_EARLY = 7
SA = S + Q
LR = 64
NG = 4
RANKS = (8, 16, 32, 64)
CH = [(0, 128), (128, 128), (256, 119)]
HALF = 512
RING = 4
EPS = 1e-5
WS = 64.0
MS = 16.0
PASSES = ((0, 0), (0, 1), (1, 0))


def wait(eng, sem, value):
    if isinstance(value, int) and value <= 0:
        return
    eng.wait_ge(sem, value)


def run_slots(eng, slot, n, ends=2):
    for s in range(ends):
        slot(s // 2, s % 2, s)
    with eng.Fori(ends // 2, (n - ends) // 2) as j:
        for p in (0, 1):
            slot(j, p, 2 * j + p)
    for s in range(n - ends, n):
        slot(s // 2, s % 2, s)


def inside(t, n):
    return not isinstance(t, int) or 0 <= t < n


def rows(t, size):
    return bass.ds(t * size, size)


def layernorm(sb, sem, name, neg_half):
    stats = sb(name + "_stats", [P, 2, 6], F32)
    mean_var = sb(name + "_mean_var", [P, 2], F32)
    var_eps = sb(name + "_var_eps", [P, 1], F32)
    rstd = sb(name + "_rstd", [P, 1], F32)
    waited = sb(name + "_waited", [P, 1], F32)
    stats_done = sem(name + "_stats_done")
    aggr_done = sem(name + "_aggr_done")
    var_ready = sem(name + "_var_ready")
    rstd_ready = sem(name + "_rstd_ready")

    def measure(dve, x, n, t):
        for i in range(2):
            dve.bn_stats(stats[0:n, i, :], x[:, i * HALF:(i + 1) * HALF]).then_inc(stats_done, 1)
        dve.wait_ge(stats_done, 2 * t + 2)
        dve.memset(waited[:, :], 0.0)
        dve.bn_aggr(mean_var[0:n, :], stats[0:n, :, :]).then_inc(aggr_done, 1)
        dve.wait_ge(aggr_done, t + 1)
        dve.tensor_scalar(var_eps[0:n, :], mean_var[0:n, 1:2], EPS, None, ALU.add).then_inc(var_ready, 1)

    def root(pool, n, t):
        pool.wait_ge(var_ready, t + 1)
        pool.tensor_tensor(rstd[0:n, :], var_eps[0:n, :], neg_half[0:n, :], ALU.pow).then_inc(rstd_ready, 1)

    def scaled(dve, out, x, n, t):
        dve.wait_ge(rstd_ready, t + 1)
        return dve.tensor_scalar(out, x, mean_var[0:n, 0:1], rstd[0:n, 0:1], ALU.subtract, ALU.mult)

    return measure, root, scaled


def build(nc, x, ctx_nat, ctx_t, gates, wa, wo, q4, sc4, wq1, wk1, bq1, bk1, w1, b1, wag, wb, gate_b, out):
    qk_s = nc.dram_tensor("qk_scratch", [2, HD, H + KV, R], F16).ap()
    v_s = nc.dram_tensor("v_scratch", [R, 2, KW], F16).ap()
    o_s = nc.dram_tensor("o_scratch", [2, QW, R], F16).ap()
    t_s = nc.dram_tensor("t_scratch", [2, P, KD, R], F16).ap()
    x2_s = nc.dram_tensor("x2_scratch", [R, D + 4], F32).ap()
    w4_s = nc.dram_tensor("w4_scratch", [P, KD * D], BF16).ap()

    with ExitStack() as whole:
        def alloc(scope):
            def sb(name, shape, dt):
                return scope.enter_context(nc.sbuf_tensor(name, shape, dt))

            def pb(name, shape, dt):
                return scope.enter_context(nc.psum_tensor(name, shape, dt))
            return sb, pb

        used = []

        def sem(name):
            used.append(nc.alloc_semaphore(name=name))
            return used[-1]

        def retire_semaphores():
            for s in used:
                nc.gpsimd.sem_clear(s)
                nc.release_semaphore(s)
            del used[:]

        sb, _ = alloc(whole)
        ident32 = sb("ident32", [P, P], F32)
        ident = sb("ident", [P, P], F16)
        identb = sb("identb", [P, P], BF16)
        neg_half = sb("neg_half", [P, 1], F32)
        tg = sb("tg", [P, 4], F32)
        tg_wo = sb("tg_wo", [P, 1], F32)
        tg_w1 = sb("tg_w1", [P, 1], F32)
        with ExitStack() as mid:
            sb, _ = alloc(mid)
            Mt = sb("Mt", [P, 2, KD, D], F16)
            c_bc = sb("c_bc", [P, D], F32)
            u_bc = sb("u_bc", [P, D], F32)
            s0 = sb("s0", [P, 1], F32)

            mm = nc.tensor.matmul

            with ExitStack() as ab:
                sb, _ = alloc(ab)
                wkv_p = sb("wkv_p", [P, 2, KD, 2 * KW], F16)
                with ExitStack() as aw:
                    sb, _ = alloc(aw)
                    proj_q_p = sb("proj_q_p", [P, 2, KD, QW], F16)
                    raw = sb("raw", [P, RING, D], F32)
                    xin = raw[:, 0:2, :]
                    y_p = sb("a_y_p", [P, 2, D], F16)
                    early = []

                    def early_sem(name):
                        early.append(nc.alloc_semaphore(name=name))
                        return early[-1]

                    x_loaded = [early_sem(f"a_x_loaded{i}") for i in range(2)]
                    y_ready, yh_ready, yl_ready = early_sem("a_y_ready"), early_sem("a_yh_ready"), early_sem("a_yl_ready")
                    norm_measure, norm_root, norm_scaled = layernorm(sb, early_sem, "a_norm", neg_half)

                    with ExitStack() as st:
                        sb, pb = alloc(st)
                        wq_p = sb("wq_p", [P, 2, KD, D], F16)
                        wk_p = sb("wk_p", [P, 2, KD, D], F16)
                        gate_in = sb("gate_in", [P, 4], F32)
                        bqk = sb("bqk", [P, 2, KD], F32)
                        bqk_hi = sb("bqk_hi", [P, 2, KD], F16)
                        bqk_lo32 = sb("bqk_lo32", [P, 2, KD], F32)
                        bqk_hi32 = sb("bqk_hi32", [P, 2, KD], F32)
                        bk_p = sb("bk_p", [P, 2, KD], F16)
                        ones = sb("ones", [P, P], F32)
                        bias_bc = sb("bias_bc", [P, 2, 2, KD, P], F16)
                        BANKS = 8
                        m_ps = pb("m_ps", [P, BANKS, HALF], F32)

                        loaded = [sem(f"z_loaded{i}") for i in range(RING)]
                        small_loaded = sem("z_small_loaded")
                        ident_zero, ident_ready = sem("z_ident_zero"), sem("z_ident_ready")
                        ident_cast = sem("z_ident_cast")
                        half_ready = sem("z_half_ready")
                        tanh_ready, tanh_scaled = sem("z_tanh_ready"), sem("z_tanh_scaled")
                        w_hi, w_lo = sem("z_w_hi"), sem("z_w_lo")
                        bias_split, bias_ready = sem("z_bias_split"), sem("z_bias_ready")
                        m_done, m_hi, m_lo = sem("z_m_done"), sem("z_m_hi"), sem("z_m_lo")
                        b_done, b_read = sem("z_b_done"), sem("z_b_read")

                        PC = 2 * KW
                        pieces = []
                        for k in range(KD):
                            for w, dst in ((wq1, wq_p), (wk1, wk_p)):
                                pieces.append((w[:, k, :], dst[:, 0, k, :], dst[:, 1, k, :], D))
                        for k in range(KD):
                            for c in range(0, WA, PC):
                                dst, at = (proj_q_p, c) if c < QW else (wkv_p, c - QW)
                                pieces.append((wa[:, k, c:c + PC], dst[:, 0, k, at:at + PC], dst[:, 1, k, at:at + PC], PC))
                        M_PIECES = 2 * KD
                        PER_ROW = (len(pieces) - M_PIECES) // (2 * KD - BANKS)

                        def row_pieces(i):
                            first = M_PIECES + (i - BANKS) * PER_ROW
                            return range(first, first + PER_ROW)


                        block = st.enter_context(nc.Block())

                        @block.sync
                        def _(sp):
                            for n, (src, _, _, cols) in enumerate(pieces):
                                wait(sp, w_lo, n - RING + 1)
                                sp.dma_start(raw[:, n % RING, 0:cols], src).then_inc(loaded[n % RING], 16)
                            for t in range(2):
                                sp.wait_ge(w_lo, len(pieces) - RING + t + 1)
                                sp.dma_start(xin[:, t, :], x[t * P:(t + 1) * P, :]).then_inc(x_loaded[t], 16)

                        @block.gpsimd
                        def _(pool):
                            pool.memset(ident32[:, :], 0.0).then_inc(ident_zero, 1)
                            pool.memset(neg_half[:, :], -0.5).then_inc(half_ready, 1)
                            pool.memset(ones[:, :], 1.0).then_inc(half_ready, 1)
                            pool.wait_ge(ident_zero, 1)
                            pool.affine_select(out=ident32[:, :], in_=ident32[:, :], compare_op=ALU.not_equal, fill=1.0,
                                               base=0, pattern=[[-1, P]], channel_multiplier=1).then_inc(ident_ready, 1)
                            pool.wait_ge(ident_ready, 1)
                            pool.tensor_copy(ident[:, :], ident32[:, :]).then_inc(ident_cast, 1)
                            pool.tensor_copy(identb[:, :], ident32[:, :]).then_inc(ident_cast, 1)
                            pool.wait_ge(half_ready, 2)
                            norm_root(pool, P, 0)
                            pool.wait_ge(yh_ready, 1)
                            pool.tensor_tensor(y_p[:, 1, :], xin[:, 0, :], y_p[:, 0, :], ALU.subtract).then_inc(yl_ready, 1)

                        @block.scalar
                        def _(act):
                            act.dma_start(gate_in[:, :], gates.to_broadcast([P, 4])).then_inc(small_loaded, 16)
                            act.dma_start(bqk[:, 0, :], bq1).then_inc(small_loaded, 16)
                            act.dma_start(bqk[:, 1, :], bk1).then_inc(small_loaded, 16)
                            act.wait_ge(small_loaded, 48)
                            act.activation(tg[:, :], gate_in[:, :], ACT.Tanh).then_inc(tanh_ready, 1)

                            def high(n):
                                _, dst, _, cols = pieces[n]
                                act.wait_ge(loaded[n % RING], 16 * (n // RING + 1))
                                act.activation(dst, raw[:, n % RING, 0:cols], ACT.Copy, scale=WS).then_inc(w_hi, 1)

                            for n in range(M_PIECES):
                                high(n)
                            for i in range(2 * KD):
                                m, h = divmod(i, 2)
                                act.wait_ge(m_done, i + 1)
                                act.activation(Mt[:, 0, m, h * HALF:(h + 1) * HALF], m_ps[:, i % BANKS, :], ACT.Copy,
                                               scale=MS / (WS * WS)).then_inc(m_hi, 1)
                                if i >= BANKS:
                                    for n in row_pieces(i):
                                        high(n)
                            act.wait_ge(y_ready, 1)
                            act.activation(y_p[:, 0, :], xin[:, 0, :], ACT.Copy).then_inc(yh_ready, 1)
                            for i, dst in enumerate((c_bc, u_bc)):
                                for h in range(2):
                                    act.wait_ge(b_done, 2 * i + h + 1)
                                    act.activation(dst[:, h * HALF:(h + 1) * HALF], m_ps[:, 2 * i + h, :], ACT.Copy,
                                                   scale=1.0 / WS).then_inc(b_read, 1)
                            act.wait_ge(b_done, 5)
                            act.activation(s0[:, :], m_ps[:, 4, 0:1], ACT.Copy).then_inc(b_read, 1)


                        @block.vector
                        def _(dve):
                            def low(n):
                                _, hi_part, dst, cols = pieces[n]
                                dve.wait_ge(loaded[n % RING], 16 * (n // RING + 1))
                                dve.wait_ge(w_hi, n + 1)
                                dve.scalar_tensor_tensor(out=dst, in0=raw[:, n % RING, 0:cols], scalar=WS, in1=hi_part,
                                                         op0=ALU.mult, op1=ALU.subtract).then_inc(w_lo, 1)

                            for n in range(M_PIECES):
                                low(n)
                            dve.wait_ge(small_loaded, 48)
                            dve.tensor_copy(bqk_hi[:, :, :], bqk[:, :, :]).then_inc(bias_split, 1)
                            dve.wait_ge(bias_split, 1)
                            dve.tensor_copy(bqk_hi32[:, :, :], bqk_hi[:, :, :]).then_inc(bias_split, 1)
                            dve.tensor_tensor(bqk_lo32[:, :, :], bqk[:, :, :], bqk_hi[:, :, :], ALU.subtract).then_inc(bias_split, 1)
                            dve.wait_ge(bias_split, 3)
                            dve.tensor_copy(bk_p[:, 0, :], bqk_hi[:, 1, :]).then_inc(bias_ready, 1)
                            dve.tensor_copy(bk_p[:, 1, :], bqk_lo32[:, 1, :]).then_inc(bias_ready, 1)
                            dve.wait_ge(half_ready, 2)
                            for i in range(2):
                                for part, src in ((0, bqk_hi32), (1, bqk_lo32)):
                                    for k in range(KD):
                                        dve.tensor_scalar(bias_bc[:, i, part, k, :], ones[:, :], src[:, i, k:k + 1], None,
                                                          ALU.mult).then_inc(bias_ready, 1)
                            dve.wait_ge(tanh_ready, 1)
                            dve.tensor_scalar(tg_wo[:, :], tg[:, 0:1], 1.0 / WS, None, ALU.mult).then_inc(tanh_scaled, 1)
                            dve.tensor_scalar(tg_w1[:, :], tg[:, 3:4], 1.0 / WS, None, ALU.mult).then_inc(tanh_scaled, 1)
                            for i in range(2 * KD):
                                m, h = divmod(i, 2)
                                dve.wait_ge(m_hi, i + 1)
                                dve.scalar_tensor_tensor(out=Mt[:, 1, m, h * HALF:(h + 1) * HALF],
                                                         in0=m_ps[:, i % BANKS, :], scalar=MS / (WS * WS),
                                                         in1=Mt[:, 0, m, h * HALF:(h + 1) * HALF],
                                                         op0=ALU.mult, op1=ALU.subtract).then_inc(m_lo, 1)
                                if i >= BANKS:
                                    for n in row_pieces(i):
                                        low(n)
                            dve.wait_ge(x_loaded[0], 16)
                            norm_measure(dve, xin[:, 0, :], P, 0)
                            norm_scaled(dve, xin[:, 0, :], xin[:, 0, :], P, 0).then_inc(y_ready, 1)

                        @block.tensor
                        def _(pe):
                            def product(i, part, k, start, stop):
                                m, h = divmod(i, 2)
                                return mm(m_ps[:, i % BANKS, :], wq_p[:, part[0], k, m * P:(m + 1) * P],
                                          wk_p[:, part[1], k, h * HALF:(h + 1) * HALF], start=start, stop=stop)

                            for k in range(KD):
                                pe.wait_ge(w_lo, 2 * (k + 1))
                                for i in range(BANKS):
                                    for n, part in enumerate(PASSES):
                                        last = product(i, part, k, k == 0 and n == 0, k == KD - 1 and n == 2)
                                    if k == KD - 1:
                                        last.then_inc(m_done, 1)
                            for i in range(BANKS, 2 * KD):
                                pe.wait_ge(m_lo, i - BANKS + 1)
                                for n, part in enumerate(PASSES):
                                    for k in range(KD):
                                        last = product(i, part, k, n == 0 and k == 0, n == 2 and k == KD - 1)
                                last.then_inc(m_done, 1)
                            pe.wait_ge(bias_ready, 2 + 4 * KD)
                            for i, w in enumerate((wk_p, wq_p)):
                                for h in range(2):
                                    pe.wait_ge(m_lo, BANKS + 2 * i + h + 1)
                                    for n, (a, b) in enumerate(PASSES):
                                        for k in range(KD):
                                            last = mm(m_ps[:, 2 * i + h, :], bias_bc[:, i, a, k, :],
                                                      w[:, b, k, h * HALF:(h + 1) * HALF],
                                                      start=(n == 0 and k == 0), stop=(n == 2 and k == KD - 1))
                                    last.then_inc(b_done, 1)
                            pe.wait_ge(m_lo, BANKS + 5)
                            for n, (a, b) in enumerate(PASSES):
                                for k in range(KD):
                                    last = mm(m_ps[:, 4, 0:1], bias_bc[:, 0, a, k, :], bk_p[:, b, k:k + 1],
                                              start=(n == 0 and k == 0), stop=(n == 2 and k == KD - 1))
                            last.then_inc(b_done, 1)

                    retire_semaphores()
                    used += early

                    ctx_raw = whole.enter_context(nc.sbuf_tensor("ctx_raw", [P, KD, S], F32, side="right"))
                    cT = whole.enter_context(nc.sbuf_tensor("cT", [P, 2, 2, KD, S + 1], F16, side="right"))
                    qk_stored = [nc.alloc_semaphore(name=f"a_qk_stored{i}") for i in range(2)]
                    v_stored = [nc.alloc_semaphore(name=f"a_v_stored{i}") for i in range(2)]
                    w4_stored = [nc.alloc_semaphore(name=f"a_w4_stored{i}") for i in range(2)]
                    raw_loaded = nc.alloc_semaphore(name="b_raw_loaded")
                    split_hi, split_lo = nc.alloc_semaphore(name="b_split_hi"), nc.alloc_semaphore(name="b_split_lo")

                    def load_raw(sp, n, b):
                        wait(sp, split_hi, KD * n)
                        wait(sp, split_lo, KD * n)
                        sp.dma_start(ctx_raw[:, :, :], ctx_t[bass.ds(b, 1), :, :, :].rearrange("b p k s -> p (b k) s")
                                     ).then_inc(raw_loaded, 16)

                    def split_high(act, p, n, k):
                        if k == 0:
                            act.wait_ge(raw_loaded, 16 * (n + 1))
                        act.activation(cT[:, p, 0, k, 0:S], ctx_raw[:, k, :], ACT.Copy).then_inc(split_hi, 1)

                    def split_low(pool, p, n, k):
                        pool.wait_ge(split_hi, KD * n + k + 1)
                        pool.tensor_tensor(cT[:, p, 1, k, 0:S], ctx_raw[:, k, :], cT[:, p, 0, k, 0:S],
                                           ALU.subtract).then_inc(split_lo, 1)

                    NC = WA // KW
                    HC = NC - 1
                    with ExitStack() as st:
                        sb, pb = alloc(st)
                        yT = sb("a_yT", [P, 2, 2, KD, P], F16)
                        nat = sb("a_nat", [P, 2, 2, KW], F16)
                        heads = sb("a_heads", [HD, 2, 2, H + KV, P], F16)
                        val = sb("a_val", [P, 2, 2, KW], F16)
                        codes = raw[:, 2, 0:HALF].bitcast(I32)
                        over6 = raw[:, 2, 0:HALF]
                        scale4, sign8, mag = raw[:, 2, HALF:D], raw[:, 3, 0:HALF], raw[:, 3, HALF:D]
                        over4 = sb("a_over4", [P, HALF], F32)
                        w4_out = sb("a_w4_out", [P, 2, HALF], BF16)
                        pr = pb("a_pr", [P, 3, HALF], F32)
                        tr = pb("a_tr", [P, 2, KD * P], F16)
                        ht = pb("a_ht", [P, 2, 2 * G * P], F16)

                        ytr_done, yT_hi, yT_lo = sem("a_ytr_done"), sem("a_yT_hi"), sem("a_yT_lo")
                        proj, hi, lo = sem("a_proj"), sem("a_hi"), sem("a_lo")
                        htr = sem("a_htr")
                        ht_read = [sem(f"a_ht_read{i}") for i in range(2)]
                        codes_loaded, codes_free, deq = sem("a_codes_loaded"), sem("a_codes_free"), sem("a_deq")

                        W4N = 2 * KD
                        DEQ_PARTS = NC
                        assert W4N == TILES + 2

                        def pieces_of(j, p, t):
                            return (([(0, 0, 0)] if isinstance(t, int) and t == 0 else []) + [(t + 1, j + p, 1 - p)]
                                    + ([(W4N - 1, KD - 1, 1)] if isinstance(t, int) and t == TILES - 1 else []))

                        def weight(part, k, c):
                            if c < QW // KW:
                                return proj_q_p[:, part, k, c * KW:(c + 1) * KW]
                            return wkv_p[:, part, k, (c - QW // KW) * KW:(c - QW // KW + 1) * KW]

                        block = st.enter_context(nc.Block())

                        @block.sync
                        def _(sp):
                            def load_codes(n, k, h):
                                wait(sp, codes_free, n)
                                sp.dma_start(codes[:, :], q4.rearrange("p k d -> p (k d)")[:, rows(n, HALF)]
                                             ).then_inc(codes_loaded, 16)
                                scales = sc4[rows(k, 8), h * HALF:(h + 1) * HALF]
                                sp.dma_start(scale4[:, :], scales.rearrange("b o -> b () o").to_broadcast([8, 16, HALF])
                                             ).then_inc(codes_loaded, 16)

                            def slot(j, p, t):
                                for n, k, h in pieces_of(j, p, t):
                                    load_codes(n, k, h)
                                if isinstance(t, int) and t >= TILES - 2:
                                    load_raw(sp, t - (TILES - 2), t - (TILES - 2))
                                if inside(t + 2, TILES):
                                    sp.wait_ge(yl_ready, t + 1)
                                    sp.wait_ge(yh_ready, t + 1)
                                    sp.dma_start(xin[:, p, :], x[rows(t + 2, P), :]).then_inc(x_loaded[p], 16)
                                sp.wait_ge(lo, NC * (t + 1))
                                sp.dma_start(v_s[rows(t, P), :, :], val[:, p, :, :]).then_inc(v_stored[p], 16)

                            run_slots(sp, slot, TILES)

                        @block.gpsimd
                        def _(pool):
                            def norm_of(p, t):
                                norm_root(pool, P, t)
                                pool.wait_ge(yh_ready, t + 1)
                                pool.tensor_tensor(y_p[:, 1, :], xin[:, p, :], y_p[:, 0, :], ALU.subtract).then_inc(yl_ready, 1)

                            def slot(j, p, t):
                                if inside(t + 1, TILES):
                                    norm_of(1 - p, t + 1)
                                if isinstance(t, int) and t >= TILES - 2:
                                    for k in range(KD):
                                        split_low(pool, t - (TILES - 2), t - (TILES - 2), k)

                            run_slots(pool, slot, TILES)

                        @block.scalar
                        def _(act):
                            def y_high(p, t):
                                act.wait_ge(y_ready, t + 1)
                                wait(act, ytr_done, t)
                                act.activation(y_p[:, 0, :], xin[:, p, :], ACT.Copy).then_inc(yh_ready, 1)

                            def yT_high(p, t):
                                act.wait_ge(ytr_done, t + 1)
                                act.activation(yT[:, p, 0, :, :], tr[:, 0, :].rearrange("p (k r) -> p k r", k=KD),
                                               ACT.Copy).then_inc(yT_hi, 1)

                            yT_high(0, 0)

                            def chunk(j, p, t, c):
                                act.wait_ge(proj, NC * t + c + 1)
                                if c < HC:
                                    wait(act, htr, HC * t + c - 1)
                                    dst = nat[:, (p + c) % 2, 0, :]
                                else:
                                    wait(act, v_stored[p], 16 * j)
                                    dst = val[:, p, 0, :]
                                scale = (1.0 if c >= QW // KW else HD ** -0.5) / WS
                                act.activation(dst, pr[:, c % 3, 0:KW], ACT.Copy, scale=scale).then_inc(hi, 1)

                            def head_read(j, p, t, c):
                                if (p + c) % 2 == 0:
                                    act.wait_ge(htr, HC * t + c + 1)
                                    if c < 2:
                                        wait(act, qk_stored[p], 32 * j)
                                    act.activation(heads[:, p, :, G * c:G * (c + 1), :],
                                                   ht[0:HD, 0, :].rearrange("d (l g r) -> d l g r", l=2, g=G),
                                                   ACT.Copy).then_inc(ht_read[0], 1)

                            def store_heads(j, p, t):
                                n = HC * (p + 1)
                                act.wait_ge(ht_read[0], HC * j + (n + 1) // 2)
                                act.wait_ge(ht_read[1], HC * j + n // 2)
                                for part in range(2):
                                    act.dma_start(qk_s[part, :, :, rows(t, P)], heads[:, p, part, :, :]).then_inc(qk_stored[p], 16)

                            def store_w4(j, p, t):
                                for n, k, h in pieces_of(j, p, t):
                                    act.wait_ge(codes_free, n + 1)
                                    act.dma_start(w4_s[:, rows(n, HALF)], w4_out[:, h, :]).then_inc(w4_stored[h], 16)

                            def slot(j, p, t):
                                for c in range(NC):
                                    chunk(j, p, t, c)
                                    if c == 0 and inside(t - 1, TILES):
                                        store_heads(j - 1 + p, 1 - p, t - 1)
                                        store_w4(j - 1 + p, 1 - p, t - 1)
                                    if c:
                                        head_read(j, p, t, c - 1)
                                    if c == 0 and inside(t + 1, TILES):
                                        y_high(1 - p, t + 1)
                                    if c == 3 and inside(t + 1, TILES):
                                        yT_high(1 - p, t + 1)
                                    if isinstance(t, int) and t >= TILES - 2 and c >= 2:
                                        for k in (2 * c - 4, 2 * c - 3):
                                            split_high(act, t - (TILES - 2), t - (TILES - 2), k)

                            run_slots(act, slot, TILES)
                            store_heads(TILES // 2 - 1, 1, TILES - 1)
                            store_w4(TILES // 2 - 1, 1, TILES - 1)

                        @block.vector
                        def _(dve):
                            def y_of(j, p, t):
                                dve.wait_ge(x_loaded[p], 16 * (j + 1))
                                norm_measure(dve, xin[:, p, :], P, t)
                                norm_scaled(dve, xin[:, p, :], xin[:, p, :], P, t).then_inc(y_ready, 1)

                            def yT_low(p, t):
                                dve.wait_ge(ytr_done, t + 1)
                                dve.tensor_copy(yT[:, p, 1, :, :],
                                                tr[:, 1, :].rearrange("p (k r) -> p k r", k=KD)).then_inc(yT_lo, 1)

                            yT_low(0, 0)

                            def chunk(j, p, t, c):
                                dve.wait_ge(hi, NC * t + c + 1)
                                both = nat[:, (p + c) % 2, :, :] if c < HC else val[:, p, :, :]
                                scale = (1.0 if c >= QW // KW else HD ** -0.5) / WS
                                dve.scalar_tensor_tensor(out=both[:, 1, :], in0=pr[:, c % 3, 0:KW], scalar=scale,
                                                         in1=both[:, 0, :], op0=ALU.mult, op1=ALU.subtract).then_inc(lo, 1)

                            def head_read(j, p, t, c):
                                if (p + c) % 2 == 1:
                                    dve.wait_ge(htr, HC * t + c + 1)
                                    if c < 2:
                                        wait(dve, qk_stored[p], 32 * j)
                                    dve.tensor_copy(heads[:, p, :, G * c:G * (c + 1), :],
                                                    ht[0:HD, 1, :].rearrange("d (l g r) -> d l g r", l=2, g=G)
                                                    ).then_inc(ht_read[1], 1)

                            def step(n, i, ins):
                                ins.then_inc(deq, 1)
                                dve.wait_ge(deq, 8 * n + i + 1)

                            def dequantize(n, k, h, part):
                                if part == 0:
                                    dve.wait_ge(codes_loaded, 32 * (n + 1))
                                    step(n, 0, dve.tensor_scalar(sign8[:, :], codes[:, :], 8.0, 8.0, ALU.is_ge, ALU.mult))
                                    step(n, 1, dve.tensor_tensor(mag[:, :], codes[:, :], sign8[:, :], ALU.subtract))
                                if part == 1:
                                    step(n, 2, dve.tensor_scalar(over4[:, :], mag[:, :], 4.0, 0.0, ALU.subtract, ALU.max))
                                    step(n, 3, dve.tensor_scalar(over6[:, :], mag[:, :], 6.0, 0.0, ALU.subtract, ALU.max))
                                if part == 2:
                                    step(n, 4, dve.scalar_tensor_tensor(out=over4[:, :], in0=over4[:, :], scalar=0.5,
                                                                        in1=over6[:, :], op0=ALU.mult, op1=ALU.add))
                                if part == 3:
                                    step(n, 5, dve.scalar_tensor_tensor(out=mag[:, :], in0=mag[:, :], scalar=0.5,
                                                                        in1=over4[:, :], op0=ALU.mult, op1=ALU.add))
                                if part == 4:
                                    step(n, 6, dve.tensor_scalar(sign8[:, :], sign8[:, :], -0.25, 1.0, ALU.mult, ALU.add))
                                    step(n, 7, dve.tensor_tensor(mag[:, :], mag[:, :], sign8[:, :], ALU.mult))
                                if part == 5:
                                    wait(dve, w4_stored[h], 16 * k)
                                    dve.tensor_tensor(w4_out[:, h, :], mag[:, :], scale4[:, :], ALU.mult).then_inc(codes_free, 1)
                                    dve.wait_ge(codes_free, n + 1)

                            def slot(j, p, t):
                                for n, k, h in pieces_of(j, p, t)[:-1]:
                                    for c in range(DEQ_PARTS):
                                        dequantize(n, k, h, c)
                                for c in range(NC):
                                    chunk(j, p, t, c)
                                    for n, k, h in pieces_of(j, p, t)[-1:]:
                                        dequantize(n, k, h, c)
                                    if c:
                                        head_read(j, p, t, c - 1)
                                    if c == 0 and inside(t + 1, TILES):
                                        y_of(j + p, 1 - p, t + 1)
                                    if c == 3 and inside(t + 1, TILES):
                                        yT_low(1 - p, t + 1)

                            run_slots(dve, slot, TILES)

                        @block.tensor
                        def _(pe):
                            def y_transposes(t):
                                pe.wait_ge(yl_ready, t + 1)
                                for part in range(2):
                                    for k in range(KD):
                                        last = pe.transpose(tr[:, part, k * P:(k + 1) * P], y_p[:, part, k * P:(k + 1) * P],
                                                            ident[:, :])
                                last.then_inc(ytr_done, 1)

                            def project(j, p, t, c):
                                wait(pe, lo, NC * t + c - 2)
                                for n, (a, b) in enumerate(PASSES):
                                    for k in range(KD):
                                        last = mm(pr[:, c % 3, 0:KW], yT[:, p, a, k, :], weight(b, k, c),
                                                  start=(n == 0 and k == 0), stop=(n == 2 and k == KD - 1))
                                last.then_inc(proj, 1)

                            def head_transposes(j, p, t, c):
                                bank = (p + c) % 2
                                pe.wait_ge(lo, NC * t + c + 1)
                                n = HC * p + c
                                wait(pe, ht_read[bank], HC * j + n // 2)
                                for part in range(2):
                                    for g in range(G):
                                        last = pe.transpose(ht[0:HD, bank, (part * G + g) * P:(part * G + g + 1) * P],
                                                            nat[:, bank, part, g * HD:(g + 1) * HD], ident[:, :])
                                last.then_inc(htr, 1)

                            y_transposes(0)

                            def slot(j, p, t):
                                pe.wait_ge(yT_hi, t + 1)
                                pe.wait_ge(yT_lo, t + 1)
                                for c in range(NC):
                                    project(j, p, t, c)
                                    if c:
                                        head_transposes(j, p, t, c - 1)
                                    if c == 3 and inside(t + 1, TILES):
                                        y_transposes(t + 1)

                            run_slots(pe, slot, TILES)

                    retire_semaphores()

                wo_early = mid.enter_context(nc.sbuf_tensor("wo_early", [P, 2, KO_EARLY, D], F16, side="right"))
                with ExitStack() as st:
                    sb, pb = alloc(st)
                    wo_in = sb("b_wo_in", [P, D], F32)
                    kT = sb("b_kT", [HD, 2, 2, KV, SA + 1], F16)
                    vv = sb("b_v", [P, 2, 4, 2, KW], F16)
                    qT = sb("b_qT", [HD, 2, 2, H, Q], F16)
                    kn = sb("b_kn", [P, 2, KW], F16)
                    ex = sb("b_exp", [Q, 2, SA + 1], F32)
                    pn = sb("b_prob", [Q, 2, SA + 1], F32)
                    pp = sb("b_prob_p", [Q, 2, 2, SA + 1], F16)
                    pT = sb("b_probT", [P, 2, 2, 4, G, Q], F16)
                    oo = sb("b_o", [HD, 2, 2, G * Q], F16)
                    nmax = sb("b_nmax", [Q, 4], F32)
                    esum = sb("b_esum", [Q, 4], F32)
                    rsum = sb("b_rsum", [Q, 4], F32)
                    kv_ps = pb("b_kv_ps", [P, 2, HALF], F32)
                    s_ps = pb("b_s_ps", [P, 2, HALF], F32)
                    pt_ps = pb("b_pt_ps", [P, 2, 1024], F16)
                    o_ps = pb("b_o_ps", [P, HALF], F32)
                    kt_ps = pb("b_kt_ps", [P, 1024], F16)

                    q_loaded = [sem(f"b_q_loaded{i}") for i in range(2)]
                    kv_loaded = [sem(f"b_kv_loaded{i}") for i in range(2)]
                    kv_done, kv_hi, kv_lo = sem("b_kv_done"), sem("b_kv_hi"), sem("b_kv_lo")
                    ktr, kt_read = sem("b_ktr"), sem("b_kt_read")
                    scored, maxed, exped = sem("b_scored"), sem("b_maxed"), sem("b_exped")
                    inverted, normed, p_hi, p_lo = sem("b_inverted"), sem("b_normed"), sem("b_p_hi"), sem("b_p_lo")
                    ptr = sem("b_ptr")
                    pt_read = [sem(f"b_pt_read{i}") for i in range(2)]
                    pv, o_hi, o_lo = sem("b_pv"), sem("b_o_hi"), sem("b_o_lo")
                    o_stored = [sem(f"b_o_stored{i}") for i in range(2)]
                    pt_cleared = sem("b_pt_cleared")
                    wo_loaded, wo_hi, wo_lo = sem("b_wo_loaded"), sem("b_wo_hi"), sem("b_wo_lo")

                    def wo_chunk(b, i, odd):
                        if not isinstance(b, int) or b < B - 2:
                            return None
                        n, r = divmod(H * (b - (B - 2)) + i, 2)
                        return n if r == odd and n < KO_EARLY else None

                    BLOCK = 3 * KD
                    PER_STEP = 6 * BLOCK // H
                    READ_AT = [(BLOCK * (k + 1) - 1) // PER_STEP + 1 for k in range(6)]

                    def block_out(p, k, part):
                        n = CH[k % 3][1]
                        return kn[0:n, part, :] if k < 3 else vv[0:n, p, k - 3, part, :]

                    KEYS = [(Q + a, n) for a, n in CH] + [(0, Q)]

                    block = st.enter_context(nc.Block())

                    @block.sync
                    def _(sp):
                        def load_latents(j, p, b):
                            wait(sp, pv, KV * (b - 1))
                            for part in range(2):
                                sp.dma_start(qT[:, p, part, :, :], qk_s[part, :, 0:H, rows(b, Q)]).then_inc(q_loaded[p], 16)
                                sp.dma_start(kT[:, p, part, :, 0:Q],
                                             qk_s[part, :, H:H + KV, rows(b, Q)]).then_inc(q_loaded[p], 16)
                            sp.dma_start(vv[0:Q, p, 3, :, :], v_s[rows(b, Q), :, :]).then_inc(kv_loaded[p], 16)

                        def store(b, g):
                            sp.wait_ge(o_lo, KV * b + g + 1)
                            for part in range(2):
                                dst = o_s[part, g * G * HD:(g + 1) * G * HD, rows(b, Q)].rearrange("(h d) r -> d h r", h=G)
                                src = oo[:, g % 2, part, :].rearrange("d (h r) -> d h r", h=G)
                                sp.dma_start(dst, src).then_inc(o_stored[g % 2], 16)

                        for i in range(2):
                            sp.wait_ge(v_stored[i], 16 * (TILES // 2))
                            sp.wait_ge(qk_stored[i], 32 * (TILES // 2))
                            sp.wait_ge(w4_stored[i], 16 * KD)
                        load_latents(0, 0, 0)
                        load_latents(0, 1, 1)

                        def slot(j, p, b):
                            if inside(b - 1, B):
                                store(b - 1, KV - 1)
                                if inside(b + 1, B):
                                    load_latents(j, 1 - p, b + 1)
                            if inside(b + 2, B):
                                load_raw(sp, b + 2, b + 2)
                            for g in range(KV - 1):
                                store(b, g)

                        run_slots(sp, slot, B)
                        store(B - 1, KV - 1)
                        for i in range(2):
                            sp.wait_ge(o_stored[i], 32 * B * KV // 2)

                    @block.gpsimd
                    def _(pool):
                        def split_piece(p, b, k):
                            if k == 0:
                                wait(pool, kv_done, 6 * (b - 1))
                            split_low(pool, p, b, k)

                        def prob_low(b, h):
                            n = H * b + h
                            pool.wait_ge(p_hi, n + 1)
                            wait(pool, ptr, n - 1)
                            pool.tensor_tensor(pp[:, h % 2, 1, 0:SA], pn[:, h % 2, 0:SA], pp[:, h % 2, 0, 0:SA],
                                               ALU.subtract).then_inc(p_lo, 1)

                        prob_low(0, 0)

                        def slot(j, p, b):
                            for i in range(H):
                                if i < H - 1:
                                    prob_low(b, i + 1)
                                elif inside(b + 1, B):
                                    prob_low(b + 1, 0)
                                if 4 <= i < 4 + KD and inside(b + 2, B):
                                    split_piece(p, b + 2, i - 4)

                        run_slots(pool, slot, B)

                    @block.scalar
                    def _(act):
                        def split_piece(p, b, k):
                            if k == 0:
                                wait(act, kv_done, 6 * (b - 1))
                            split_high(act, p, b, k)

                        def block_high(p, b, k):
                            n = CH[k % 3][1]
                            act.wait_ge(kv_done, 6 * b + k + 1)
                            if k < 3:
                                wait(act, ktr, 3 * b + k)
                            act.activation(block_out(p, k, 0), kv_ps[0:n, k % 2, 0:KW], ACT.Copy, scale=1.0 / WS).then_inc(kv_hi, 1)

                        def keys_read(p, b, c):
                            a, n = KEYS[c]
                            act.wait_ge(ktr, 3 * b + c + 1)
                            act.activation(kT[:, p, :, :, a:a + n],
                                           kt_ps[0:HD, :].rearrange("d (l g r) -> d l g r", l=2, g=KV)[:, :, :, 0:n],
                                           ACT.Copy).then_inc(kt_read, 1)

                        def exponent(b, h):
                            n = H * b + h
                            act.wait_ge(maxed, n + 1)
                            wait(act, normed, n - 1)
                            act.activation(ex[:, h % 2, 0:SA], s_ps[0:Q, h % 2, 0:SA], ACT.Exp, bias=nmax[:, h % 4:h % 4 + 1],
                                           accum_out=esum[:, h % 4:h % 4 + 1]).then_inc(exped, 1)

                        def probs_read(j, p, b, h):
                            if h % 2 == 0:
                                act.wait_ge(ptr, H * b + h + 1)
                                g = h // G
                                wait(act, pv, KV * b + g - 1)
                                act.activation(pT[:, g % 2, :, :, h % G, :],
                                               pt_ps[:, 0, 0:8 * Q].rearrange("s (l c r) -> s l c r", l=2, c=4),
                                               ACT.Copy).then_inc(pt_read[0], 1)

                        def out_high(b, g):
                            act.wait_ge(pv, KV * b + g + 1)
                            wait(act, o_stored[g % 2], 32 * (2 * b + g // 2))
                            act.activation(oo[:, g % 2, 0, :], o_ps[0:HD, 0:G * Q], ACT.Copy).then_inc(o_hi, 1)

                        for k in range(5):
                            block_high(0, 0, k)
                            if 1 <= k <= 3:
                                keys_read(0, 0, k - 1)
                        for h in range(2):
                            exponent(0, h)
                        block_high(0, 0, 5)

                        def wo_load(n):
                            wait(act, wo_lo, n)
                            act.dma_start(wo_in[:, :], wo[:, n, :]).then_inc(wo_loaded, 16)

                        def wo_high(n):
                            act.wait_ge(wo_loaded, 16 * (n + 1))
                            act.activation(wo_early[:, 0, n, :], wo_in[:, :], ACT.Copy, scale=WS).then_inc(wo_hi, 1)

                        def slot(j, p, b):
                            for i in range(H):
                                if i == 0 and inside(b - 1, B):
                                    block_high(p, b, 5)
                                if i in READ_AT and inside(b + 1, B):
                                    block_high(1 - p, b + 1, READ_AT.index(i))
                                if i < H - 2:
                                    exponent(b, i + 2)
                                elif inside(b + 1, B):
                                    exponent(b + 1, i + 2 - H)
                                probs_read(j, p, b, i)
                                if i - 2 in READ_AT[0:3] and inside(b + 1, B):
                                    keys_read(1 - p, b + 1, READ_AT.index(i - 2))
                                if i % G == 0:
                                    if i:
                                        out_high(b, i // G - 1)
                                    elif inside(b - 1, B):
                                        out_high(b - 1, KV - 1)
                                if 4 <= i < 4 + KD and inside(b + 2, B):
                                    split_piece(p, b + 2, i - 4)
                                if wo_chunk(b, i, 0) is not None:
                                    wo_load(wo_chunk(b, i, 0))
                                if wo_chunk(b, i, 1) is not None:
                                    wo_high(wo_chunk(b, i, 1))

                        run_slots(act, slot, B)
                        out_high(B - 1, KV - 1)

                    @block.vector
                    def _(dve):
                        for i in range(2):
                            dve.memset(pt_ps[:, i, :].bitcast(F32), 0.0).then_inc(pt_cleared, 1)

                        def block_low(p, b, k):
                            n = CH[k % 3][1]
                            dve.wait_ge(kv_hi, 6 * b + k + 1)
                            dve.scalar_tensor_tensor(out=block_out(p, k, 1), in0=kv_ps[0:n, k % 2, 0:KW], scalar=1.0 / WS,
                                                         in1=block_out(p, k, 0), op0=ALU.mult, op1=ALU.subtract).then_inc(kv_lo, 1)

                        def maximum(b, h):
                            dve.wait_ge(scored, H * b + h + 1)
                            wait(dve, exped, H * b + h - 3)
                            dve.tensor_reduce(nmax[:, h % 4:h % 4 + 1], s_ps[0:Q, h % 2, 0:SA], AX.X, ALU.max,
                                              negate=True).then_inc(maxed, 1)

                        def normalize(b, h):
                            n = H * b + h
                            c = h % 4
                            dve.wait_ge(exped, n + 1)
                            dve.reciprocal(rsum[:, c:c + 1], esum[:, c:c + 1]).then_inc(inverted, 1)
                            dve.wait_ge(inverted, n + 1)
                            wait(dve, p_lo, n - 1)
                            dve.tensor_scalar(pn[:, h % 2, 0:SA], ex[:, h % 2, 0:SA], rsum[:, c:c + 1], None,
                                              ALU.mult).then_inc(normed, 1)
                            dve.wait_ge(normed, n + 1)
                            wait(dve, ptr, n - 1)
                            dve.tensor_copy(pp[:, h % 2, 0, 0:SA], pn[:, h % 2, 0:SA]).then_inc(p_hi, 1)

                        def probs_read(j, p, b, h):
                            if h % 2 == 1:
                                dve.wait_ge(ptr, H * b + h + 1)
                                g = h // G
                                wait(dve, pv, KV * b + g - 1)
                                dve.tensor_copy(pT[:, g % 2, :, :, h % G, :],
                                                pt_ps[:, 1, 0:8 * Q].rearrange("s (l c r) -> s l c r", l=2, c=4)
                                                ).then_inc(pt_read[1], 1)

                        def out_low(b, g):
                            dve.wait_ge(o_hi, KV * b + g + 1)
                            dve.tensor_tensor(oo[:, g % 2, 1, :], o_ps[0:HD, 0:G * Q], oo[:, g % 2, 0, :],
                                              ALU.subtract).then_inc(o_lo, 1)

                        def wo_low(n):
                            dve.wait_ge(wo_loaded, 16 * (n + 1))
                            dve.wait_ge(wo_hi, n + 1)
                            dve.scalar_tensor_tensor(out=wo_early[:, 1, n, :], in0=wo_in[:, :], scalar=WS,
                                                     in1=wo_early[:, 0, n, :], op0=ALU.mult, op1=ALU.subtract).then_inc(wo_lo, 1)

                        for k in range(5):
                            block_low(0, 0, k)
                        for h in range(2):
                            maximum(0, h)
                        block_low(0, 0, 5)
                        normalize(0, 0)

                        def slot(j, p, b):
                            for i in range(H):
                                if i < H - 1:
                                    normalize(b, i + 1)
                                elif inside(b + 1, B):
                                    normalize(b + 1, 0)
                                if i == 0 and inside(b - 1, B):
                                    block_low(p, b, 5)
                                if i in READ_AT and inside(b + 1, B):
                                    block_low(1 - p, b + 1, READ_AT.index(i))
                                if i < H - 2:
                                    maximum(b, i + 2)
                                elif inside(b + 1, B):
                                    maximum(b + 1, i + 2 - H)
                                probs_read(j, p, b, i)
                                if i % G == 0:
                                    if i:
                                        out_low(b, i // G - 1)
                                    elif inside(b - 1, B):
                                        out_low(b - 1, KV - 1)
                                if wo_chunk(b, i, 1) is not None:
                                    wo_low(wo_chunk(b, i, 1))

                        run_slots(dve, slot, B)
                        out_low(B - 1, KV - 1)

                    @block.tensor
                    def _(pe):
                        def project(p, b, step, count):
                            for m in range(step * count, (step + 1) * count):
                                k, r = divmod(m, BLOCK)
                                i, d = divmod(r, KD)
                                a, n = CH[k % 3]
                                if m == 0:
                                    pe.wait_ge(split_lo, KD * (b + 1))
                                if r == 0:
                                    wait(pe, kv_lo, 6 * b + k - 1)
                                u, w = PASSES[i]
                                last = mm(kv_ps[0:n, k % 2, 0:KW], cT[:, p, u, d, a:a + n],
                                          wkv_p[:, w, d, (k // 3) * KW:(k // 3 + 1) * KW], start=(r == 0), stop=(r == BLOCK - 1))
                                if r == BLOCK - 1:
                                    last.then_inc(kv_done, 1)

                        def key_transposes(b, c):
                            n = CH[c][1]
                            pe.wait_ge(kv_lo, 6 * b + c + 1)
                            wait(pe, kt_read, 3 * b + c)
                            for part in range(2):
                                for g in range(KV):
                                    o = (part * KV + g) * P
                                    last = pe.transpose(kt_ps[0:HD, o:o + n], kn[0:n, part, g * HD:(g + 1) * HD],
                                                        ident[0:n, 0:n])
                            last.then_inc(ktr, 1)

                        def scores(j, p, b, h):
                            n = H * b + h
                            if h == 0:
                                pe.wait_ge(kt_read, 3 * (b + 1))
                                pe.wait_ge(q_loaded[p], 64 * (j + 1))
                            wait(pe, exped, n - 1)
                            for i, (u, w) in enumerate(PASSES):
                                last = mm(s_ps[0:Q, h % 2, 0:SA], qT[:, p, u, h, :], kT[:, p, w, h // G, 0:SA],
                                          start=(i == 0), stop=(i == 2))
                            last.then_inc(scored, 1)

                        def prob_transposes(j, p, b, h):
                            pe.wait_ge(p_lo, H * b + h + 1)
                            wait(pe, pt_read[h % 2], 8 * b + h // 2)
                            for part in range(2):
                                for c, (a, n) in enumerate(KEYS):
                                    o = (part * 4 + c) * Q
                                    last = pe.transpose(pt_ps[0:n, h % 2, o:o + Q], pp[:, h % 2, part, a:a + n],
                                                        ident[0:Q, 0:Q])
                            last.then_inc(ptr, 1)

                        def attend(j, p, b, g):
                            if g == 0:
                                pe.wait_ge(kv_lo, 6 * (b + 1))
                                pe.wait_ge(kv_loaded[p], 16 * (j + 1))
                            for i in range(2):
                                pe.wait_ge(pt_read[i], 8 * b + 2 * g + 2)
                            wait(pe, o_lo, KV * b + g)
                            for i, (u, w) in enumerate(PASSES):
                                for c, (a, n) in enumerate(KEYS):
                                    last = mm(o_ps[0:HD, 0:G * Q], vv[0:n, p, c, u, g * HD:(g + 1) * HD],
                                              pT[0:n, g % 2, w, c, :, :],
                                              start=(i == 0 and c == 0), stop=(i == 2 and c == 3))
                            last.then_inc(pv, 1)

                        for k in range(5):
                            project(0, 0, k, BLOCK)
                            if 1 <= k <= 3:
                                key_transposes(0, k - 1)
                        for h in range(2):
                            scores(0, 0, 0, h)
                        project(0, 0, 5, BLOCK)
                        pe.wait_ge(pt_cleared, 2)

                        def slot(j, p, b):
                            for i in range(H):
                                if i < H - 2:
                                    scores(j, p, b, i + 2)
                                elif inside(b + 1, B):
                                    scores(j + p, 1 - p, b + 1, i + 2 - H)
                                prob_transposes(j, p, b, i)
                                if i % G == 0:
                                    if i:
                                        attend(j, p, b, i // G - 1)
                                    elif inside(b - 1, B):
                                        attend(j - 1 + p, 1 - p, b - 1, KV - 1)
                                if i - 1 in READ_AT[0:3] and inside(b + 1, B):
                                    key_transposes(b + 1, READ_AT.index(i - 1))
                                if inside(b + 1, B):
                                    project(1 - p, b + 1, i, PER_STEP)

                        run_slots(pe, slot, B)
                        attend(B // 2 - 1, 1, B - 1, KV - 1)

                del used[:]

            with ExitStack() as st:
                sb, pb = alloc(st)
                xin = sb("c_x", [P, 2, D], F32)
                oT = sb("c_oT", [P, 2, 2, KO, P], F16)
                x1 = xin
                wo_late = sb("c_wo_late", [P, 2, KO - KO_EARLY, D], F16)
                w4 = sb("c_w4", [P, KD * D], BF16)
                y1 = sb("c_y1", [P, D], BF16)
                y1T = sb("c_y1T", [P, KD * P], BF16)
                f_b = sb("c_f", [P, 2, HALF], BF16)
                x2 = sb("c_x2", [P, 2, D + 4], F32)
                y2 = sb("c_y2", [P, D], F32)
                y2_p = sb("c_y2_p", [P, 2, D], F16)
                y2T = sb("c_y2T", [P, 2, KD * P], F16)
                t32 = sb("c_t32", [P, D], F32)
                t_p = sb("c_t_p", [P, 2, D], F16)
                tT = sb("c_tT", [P, 2, KD * P], F16)
                junk = sb("c_junk", [P, D], F32)
                qb = sb("c_qb", [P, 1], F32)
                stage = (junk, t32, y2)
                x_ps = pb("c_x_ps", [P, 2, HALF], F32)
                f_ps = pb("c_f_ps", [P, 2, HALF], F32)
                t_ps = pb("c_t_ps", [P, 2, HALF], F32)
                tr = pb("c_tr", [P, 2, 1024], F16)

                w4_loaded = sem("c_w4_loaded")
                w_loaded = [sem(f"c_w_loaded{i}") for i in range(len(stage))]
                w_hi, w_lo = sem("c_w_hi"), sem("c_w_lo")
                x_loaded = [sem(f"c_x_loaded{i}") for i in range(2)]
                o_loaded = [sem(f"c_o_loaded{i}") for i in range(2)]
                wo_done, x1_ready = sem("c_wo_done"), sem("c_x1_ready")
                y1_ready, y1tr, y1T_ready = sem("c_y1_ready"), sem("c_y1tr"), sem("c_y1T_ready")
                f_done, f_read, x2_ready = sem("c_f_done"), sem("c_f_read"), sem("c_x2_ready")
                y2_ready, y2_hi, y2_lo = sem("c_y2_ready"), sem("c_y2_hi"), sem("c_y2_lo")
                y2tr, y2T_hi, y2T_lo = sem("c_y2tr"), sem("c_y2T_hi"), sem("c_y2T_lo")
                dotted, qb_ready = sem("c_dotted"), sem("c_qb_ready")
                t_done, t32_ready, t_hi, t_lo = sem("c_t_done"), sem("c_t32_ready"), sem("c_t_hi"), sem("c_t_lo")
                ttr, tT_hi, tT_lo = sem("c_ttr"), sem("c_tT_hi"), sem("c_tT_lo")
                x2_stored = [sem(f"c_x2_stored{i}") for i in range(2)]
                t_stored = sem("c_t_stored")
                norm1_measure, norm1_root, norm1_scaled = layernorm(sb, sem, "c_norm1", neg_half)
                norm2_measure, norm2_root, norm2_scaled = layernorm(sb, sem, "c_norm2", neg_half)

                KO_FIRST = 10
                SLOTS = TILES + 2

                block = st.enter_context(nc.Block())

                @block.sync
                def _(sp):
                    def load(j, p, t):
                        wait(sp, x1_ready, 2 * (t - 1))
                        for part in range(2):
                            sp.dma_start(oT[:, p, part, :, :], o_s[part, :, rows(t, P)].rearrange(
                                "(k p) r -> p k r", p=P)).then_inc(o_loaded[p], 16)
                        wait(sp, x2_ready, 2 * (t - 1))
                        sp.dma_start(xin[:, p, :], x[rows(t, P), :]).then_inc(x_loaded[p], 16)

                    load(0, 0, 0)
                    for k in range(KO - KO_EARLY):
                        wait(sp, w_lo, k - len(stage) + 1)
                        sp.dma_start(stage[k % 3][:, :], wo[:, KO_EARLY + k, :]).then_inc(w_loaded[k % 3], 16)
                    sp.dma_start(w4[:, :], w4_s[:, :]).then_inc(w4_loaded, 16)
                    load(0, 1, 1)

                    def slot(j, p, s):
                        if isinstance(s, int) and s == SLOTS - 2:
                            load_raw(sp, B, 0)
                        if inside(s, TILES) and inside(s + 1, TILES) and not (isinstance(s, int) and s == 0):
                            load(j + p, 1 - p, s + 1)
                        if inside(s - 1, TILES):
                            sp.wait_ge(x2_ready, 2 * s)
                            sp.wait_ge(qb_ready, s)
                            sp.dma_start(x2_s[rows(s - 1, P), 0:D + 1], x2[:, 1 - p, 0:D + 1]
                                         ).then_inc(x2_stored[1 - p], 16)

                    run_slots(sp, slot, SLOTS, 4)
                    for i in range(2):
                        sp.wait_ge(x2_stored[i], 16 * (TILES // 2))
                    sp.wait_ge(t_stored, 32 * TILES)

                @block.gpsimd
                def _(pool):
                    def slot(j, p, s):
                        if inside(s - 2, TILES):
                            pool.wait_ge(t_hi, s - 1)
                            pool.tensor_tensor(t_p[:, 1, :], t32[:, :], t_p[:, 0, :], ALU.subtract).then_inc(t_lo, 1)
                        if inside(s - 1, TILES):
                            norm2_root(pool, P, s - 1)
                        if inside(s, TILES):
                            norm1_root(pool, P, s)
                        if isinstance(s, int) and s == SLOTS - 2:
                            for k in range(KD):
                                split_low(pool, 0, B, k)

                    run_slots(pool, slot, SLOTS, 4)

                @block.scalar
                def _(act):
                    for k in range(KO - KO_EARLY):
                        act.wait_ge(w_loaded[k % 3], 16 * (k // 3 + 1))
                        act.activation(wo_late[:, 0, k, :], stage[k % 3][:, :], ACT.Copy, scale=WS).then_inc(w_hi, 1)
                    def slot(j, p, s):
                        if inside(s - 1, TILES):
                            act.wait_ge(y1tr, s)
                            act.activation(y1T[:, :], tr[:, 0, :].bitcast(BF16), ACT.Copy).then_inc(y1T_ready, 1)
                        if inside(s - 2, TILES):
                            act.wait_ge(t32_ready, 2 * (s - 1))
                            wait(act, ttr, s - 2)
                            act.activation(t_p[:, 0, :], t32[:, :], ACT.Copy).then_inc(t_hi, 1)
                        if inside(s - 1, TILES):
                            for h in range(2):
                                act.wait_ge(f_done, 2 * (s - 1) + h + 1)
                                wait(act, x2_ready, 2 * (s - 2) + h + 1)
                                act.activation(f_b[:, h, :], f_ps[:, h, :], ACT.Copy).then_inc(f_read, 1)
                        if inside(s - 2, TILES):
                            act.wait_ge(ttr, s - 1)
                            wait(act, t_stored, 32 * (s - 2))
                            act.activation(tT[:, 0, :], tr[:, 0, :], ACT.Copy).then_inc(tT_hi, 1)
                        if inside(s - 1, TILES):
                            act.wait_ge(y2_ready, s)
                            wait(act, y2tr, s - 1)
                            for h in range(2):
                                cols = slice(h * HALF, (h + 1) * HALF)
                                act.activation(y2_p[:, 0, cols], y2[:, cols], ACT.Copy).then_inc(y2_hi, 1)
                        if inside(s - 2, TILES):
                            act.wait_ge(tT_hi, s - 1)
                            act.wait_ge(tT_lo, s - 1)
                            for part in range(2):
                                act.dma_start(t_s[part, :, :, rows(s - 2, P)],
                                              tT[:, part, :].rearrange("p (k r) -> p k r", k=KD)).then_inc(t_stored, 16)
                        if inside(s - 1, TILES):
                            act.wait_ge(y2tr, s)
                            act.activation(y2T[:, 0, :], tr[:, 0, :], ACT.Copy).then_inc(y2T_hi, 1)

                        if isinstance(s, int) and s == SLOTS - 2:
                            for k in range(KD):
                                split_high(act, 0, B, k)

                    run_slots(act, slot, SLOTS, 4)

                @block.vector
                def _(dve):
                    for k in range(KO - KO_EARLY):
                        dve.wait_ge(w_hi, k + 1)
                        dve.scalar_tensor_tensor(out=wo_late[:, 1, k, :], in0=stage[k % 3][:, :], scalar=WS,
                                                 in1=wo_late[:, 0, k, :], op0=ALU.mult, op1=ALU.subtract).then_inc(w_lo, 1)
                    def residual1(j, p, t, h):
                        cols = slice(h * HALF, (h + 1) * HALF)
                        if h == 0:
                            dve.wait_ge(x_loaded[p], 16 * (j + 1))
                        dve.wait_ge(wo_done, 2 * t + h + 1)
                        dve.scalar_tensor_tensor(out=x1[:, p, cols], in0=x_ps[:, h, :], scalar=tg_wo[:, :],
                                                 in1=xin[:, p, cols], op0=ALU.mult, op1=ALU.add).then_inc(x1_ready, 1)

                    def slot(j, p, s):
                        if inside(s, TILES):
                            residual1(j, p, s, 0)
                        if inside(s - 1, TILES):
                            t = s - 1
                            if inside(t - 2, TILES):
                                dve.wait_ge(x2_stored[1 - p], 16 * (j - 1 + p))
                            for h in range(2):
                                cols = slice(h * HALF, (h + 1) * HALF)
                                dve.wait_ge(f_read, 2 * t + h + 1)
                                dve.scalar_tensor_tensor(out=x2[:, 1 - p, cols], in0=f_b[:, h, :], scalar=tg[:, 1:2],
                                                         in1=x1[:, 1 - p, cols], op0=ALU.mult, op1=ALU.add
                                                         ).then_inc(x2_ready, 1)
                            dve.wait_ge(x2_ready, 2 * t + 2)
                            norm2_measure(dve, x2[:, 1 - p, 0:D], P, t)
                            norm2_scaled(dve, y2[:, :], x2[:, 1 - p, 0:D], P, t).then_inc(y2_ready, 1)
                            for h in range(2):
                                cols = slice(h * HALF, (h + 1) * HALF)
                                dve.wait_ge(y2_hi, 2 * t + h + 1)
                                dve.tensor_tensor(y2_p[:, 1, cols], y2[:, cols], y2_p[:, 0, cols], ALU.subtract
                                                  ).then_inc(y2_lo, 1)
                        if inside(s - 2, TILES):
                            dve.wait_ge(ttr, s - 1)
                            wait(dve, t_stored, 32 * (s - 2))
                            dve.tensor_copy(tT[:, 1, :], tr[:, 1, :]).then_inc(tT_lo, 1)
                        if inside(s - 1, TILES):
                            dve.wait_ge(y2_ready, s)
                            dve.tensor_tensor_reduce(out=junk[:, :], in0=y2[:, :], in1=u_bc[:, :], scale=1.0, scalar=0.0,
                                                     op0=ALU.mult, op1=ALU.add, accum_out=qb[:, :]).then_inc(dotted, 1)
                            dve.wait_ge(dotted, s)
                            dve.tensor_scalar(x2[:, 1 - p, D:D + 1], qb[:, :], s0[:, 0:1], None,
                                              ALU.add).then_inc(qb_ready, 1)
                        if inside(s - 1, TILES):
                            dve.wait_ge(y2tr, s)
                            dve.tensor_copy(y2T[:, 1, :], tr[:, 1, :]).then_inc(y2T_lo, 1)
                        if inside(s, TILES):
                            residual1(j, p, s, 1)
                            dve.wait_ge(x1_ready, 2 * s + 2)
                            norm1_measure(dve, x1[:, p, :], P, s)
                        if inside(s, TILES):
                            wait(dve, y1tr, s)
                            norm1_scaled(dve, y1[:, :], x1[:, p, :], P, s).then_inc(y1_ready, 1)
                        if inside(s - 1, TILES):
                            wait(dve, t_lo, s - 1)
                            for h in range(2):
                                cols = slice(h * HALF, (h + 1) * HALF)
                                dve.wait_ge(t_done, 2 * (s - 1) + h + 1)
                                dve.scalar_tensor_tensor(out=t32[:, cols], in0=t_ps[:, h, :], scalar=1.0 / MS,
                                                         in1=c_bc[:, cols], op0=ALU.mult, op1=ALU.add
                                                         ).then_inc(t32_ready, 1)

                    run_slots(dve, slot, SLOTS, 4)

                @block.tensor
                def _(pe):
                    def out_proj(j, p, t, h, first=0, end=KO):
                        if h == 0:
                            pe.wait_ge(o_loaded[p], 32 * (j + 1))
                        if first == 0:
                            wait(pe, x1_ready, 2 * (t - 1) + h + 1)
                        for k in range(first, end):
                            w, at = (wo_early, k) if k < KO_EARLY else (wo_late, k - KO_EARLY)
                            if isinstance(t, int) and t == 0 and k >= KO_EARLY:
                                pe.wait_ge(w_lo, at + 1)
                            for n, (a, b) in enumerate(PASSES):
                                last = mm(x_ps[:, h, :], oT[:, p, a, k, :], w[:, b, at, h * HALF:(h + 1) * HALF],
                                          start=(n == 0 and k == 0), stop=(n == 2 and k == KO - 1))
                        if end == KO:
                            last.then_inc(wo_done, 1)

                    def both_parts(src, done):
                        for part in range(2):
                            for k in range(KD):
                                last = pe.transpose(tr[:, part, k * P:(k + 1) * P], src[:, part, k * P:(k + 1) * P],
                                                    ident[:, :])
                        last.then_inc(done, 1)

                    def slot(j, p, s):
                        if inside(s - 1, TILES):
                            pe.wait_ge(y1_ready, s)
                            for k in range(KD):
                                last = pe.transpose(tr[:, 0, k * P:(k + 1) * P].bitcast(BF16), y1[:, k * P:(k + 1) * P],
                                                    identb[:, :])
                            last.then_inc(y1tr, 1)
                        if inside(s, TILES):
                            out_proj(j, p, s, 0)
                        if inside(s - 1, TILES):
                            pe.wait_ge(y1T_ready, s)
                            if isinstance(s, int) and s == 1:
                                pe.wait_ge(w4_loaded, 16)
                            for h in range(2):
                                wait(pe, f_read, 2 * (s - 2) + h + 1)
                                for k in range(KD):
                                    last = mm(f_ps[:, h, :], y1T[:, k * P:(k + 1) * P], w4[:, k * D + h * HALF:k * D + (h + 1) * HALF],
                                              start=(k == 0), stop=(k == KD - 1))
                                last.then_inc(f_done, 1)
                        if inside(s - 2, TILES):
                            pe.wait_ge(t_lo, s - 1)
                            both_parts(t_p, ttr)
                        if inside(s, TILES):
                            out_proj(j, p, s, 1, 0, KO_FIRST)
                        if inside(s - 1, TILES):
                            pe.wait_ge(y2_lo, 2 * s)
                            if inside(s - 2, TILES):
                                pe.wait_ge(tT_hi, s - 1)
                                pe.wait_ge(tT_lo, s - 1)
                            both_parts(y2_p, y2tr)
                        if inside(s, TILES):
                            out_proj(j, p, s, 1, KO_FIRST, KO)
                        if inside(s - 1, TILES):
                            pe.wait_ge(y2T_hi, s)
                            pe.wait_ge(y2T_lo, s)
                            for h in range(2):
                                wait(pe, t32_ready, 2 * (s - 2) + h + 1)
                                for n, (a, b) in enumerate(PASSES):
                                    for k in range(KD):
                                        last = mm(t_ps[:, h, :], y2T[:, a, k * P:(k + 1) * P],
                                                  Mt[:, b, k, h * HALF:(h + 1) * HALF],
                                                  start=(n == 0 and k == 0), stop=(n == 2 and k == KD - 1))
                                last.then_inc(t_done, 1)

                    run_slots(pe, slot, SLOTS, 4)


        AG = LR + NG
        with ExitStack() as st:
            sb, pb = alloc(st)
            w1_p = sb("d_w1_p", [P, 2, KD, D], F16)
            wag_p = sb("d_wag_p", [P, 2, KD, AG], F16)
            wb_p = sb("d_wb_p", [LR, 2, D], F16)
            stage = sb("d_stage", [P, RING, D], F32)
            ag_in = sb("d_ag_in", [P, KD, AG], F32)
            b_in = sb("d_b_in", [LR, D], F32)
            tg_b = sb("d_tg_b", [P, D], F32)
            gate_bias = sb("d_gate_bias", [P, NG], F32)
            cn_raw = sb("d_cn_raw", [P, 3, D], F32)
            cn = sb("d_cn", [P, 2, 3, D], F16)
            tT = sb("d_tT", [P, 2, 2, KD, Q], F16)
            x2 = sb("d_x2", [Q, 2, D + 4], F32)
            ex = sb("d_exp", [Q, S + 1], F32)
            pn = sb("d_prob", [Q, S + 1], F32)
            pp = sb("d_prob_p", [Q, 2, S + 1], F16)
            pT = sb("d_probT", [P, 2, 3, Q], F16)
            x3 = sb("d_x3", [Q, D], F32)
            x3b = sb("d_x3b", [Q, 2, D], F32)
            y3 = sb("d_y3", [Q, D], F32)
            y3_p = sb("d_y3_p", [Q, 2, D], F16)
            y3T = sb("d_y3T", [P, 2, KD, Q], F16)
            low = sb("d_low", [Q, LR], F32)
            low_p = sb("d_low_p", [Q, 2, P], F16)
            lowT = sb("d_lowT", [LR, 2, Q], F16)
            sm = sb("d_small", [Q, 24], F32)
            gs = sb("d_gs", [Q, NG], F32)
            gp = sb("d_gp", [Q, NG], F32)
            res = sb("d_res", [Q, 2, D], F32)
            s_ps = pb("d_s_ps", [P, HALF], F32)
            a_ps = pb("d_a_ps", [P, 2, HALF], F32)
            f_ps = pb("d_f_ps", [P, 2, HALF], F32)
            ag_ps = pb("d_ag_ps", [P, HALF], F32)
            tr = pb("d_tr", [P, 2, 1024], F16)

            w_loaded = [sem(f"d_w_loaded{i}") for i in range(RING)]
            w_hi, w_lo = sem("d_w_hi"), sem("d_w_lo")
            small_loaded, small_split, small_ready = sem("d_small_loaded"), sem("d_small_split"), sem("d_small_ready")
            cn_loaded = sem("d_cn_loaded")
            tx_loaded = [sem(f"d_tx_loaded{i}") for i in range(2)]
            cn_hi, cn_lo = sem("d_cn_hi"), sem("d_cn_lo")
            scored, maxed, biased, exped = sem("d_scored"), sem("d_maxed"), sem("d_biased"), sem("d_exped")
            shifted = sem("d_shifted")
            inverted, normed, p_hi, p_lo = sem("d_inverted"), sem("d_normed"), sem("d_p_hi"), sem("d_p_lo")
            ptr, pT_ready = sem("d_ptr"), sem("d_pT_ready")
            attended, x3_ready, x3b_ready = sem("d_attended"), sem("d_x3_ready"), sem("d_x3b_ready")
            y3_ready, y3_hi, y3_lo = sem("d_y3_ready"), sem("d_y3_hi"), sem("d_y3_lo")
            y3tr, y3T_hi, y3T_lo = sem("d_y3tr"), sem("d_y3T_hi"), sem("d_y3T_lo")
            ag_done, gate, gate_exp = sem("d_ag_done"), sem("d_gate"), sem("d_gate_exp")
            low_hi, low_lo, ltr, lowT_ready = sem("d_low_hi"), sem("d_low_lo"), sem("d_ltr"), sem("d_lowT_ready")
            ffn_done, res_ready = sem("d_ffn_done"), sem("d_res_ready")
            stored = [sem(f"d_stored{i}") for i in range(2)]
            norm_measure, norm_root, norm_scaled = layernorm(sb, sem, "d_norm", neg_half)

            SCALE = D ** -0.5
            W_EARLY = RING
            GATE_STEPS = 9

            block = st.enter_context(nc.Block())

            @block.sync
            def _(sp):
                def load_natural(b):
                    wait(sp, cn_lo, 3 * b)
                    for c, (a, n) in enumerate(CH):
                        sp.dma_start(cn_raw[0:n, c, :], ctx_nat[bass.ds(b, 1), a:a + n, :].rearrange(
                            "b s d -> (b s) d")).then_inc(cn_loaded, 16)

                def load_rows(p, b):
                    wait(sp, x3_ready, 2 * (b - 1))
                    for part in range(2):
                        sp.dma_start(tT[:, p, part, :, :], t_s[part, :, :, rows(b, Q)]).then_inc(tx_loaded[p], 16)
                    sp.dma_start(x2[:, p, 0:D + 1], x2_s[rows(b, Q), 0:D + 1]).then_inc(tx_loaded[p], 16)

                def load_weight(k):
                    wait(sp, w_lo, k - RING + 1)
                    sp.dma_start(stage[:, k % RING, :], w1[:, k, :]).then_inc(w_loaded[k % RING], 16)

                load_rows(0, 0)
                load_natural(0)
                for k in range(RING):
                    load_weight(k)
                sp.dma_start(ag_in[:, :, :], wag).then_inc(small_loaded, 16)
                sp.dma_start(b_in[:, :], wb).then_inc(small_loaded, 16)
                sp.dma_start(tg_b[:, :], b1.to_broadcast([P, D])).then_inc(small_loaded, 16)
                sp.dma_start(gate_bias[:, :], gate_b.to_broadcast([P, NG])).then_inc(small_loaded, 16)
                load_raw(sp, B + 1, 1)
                load_rows(1, 1)
                for k in range(RING, KD):
                    load_weight(k)

                def slot(j, p, s):
                    if inside(s + 1, B):
                        if not (isinstance(s, int) and s == 0):
                            load_raw(sp, s + 1 + B, s + 1)
                            load_rows(1 - p, s + 1)
                        load_natural(s + 1)
                    if inside(s - 1, B):
                        sp.wait_ge(res_ready, 2 * s)
                        sp.dma_start(out[rows(s - 1, Q), :], res[:, 1 - p, :]).then_inc(stored[1 - p], 16)

                run_slots(sp, slot, B + 2, 4)
                for i in range(2):
                    sp.wait_ge(stored[i], 16 * (B // 2))

            @block.gpsimd
            def _(pool):
                def natural_low(b):
                    for c, (a, n) in enumerate(CH):
                        pool.wait_ge(cn_hi, 3 * b + c + 1)
                        pool.tensor_tensor(cn[0:n, 1, c, :], cn_raw[0:n, c, :], cn[0:n, 0, c, :], ALU.subtract
                                           ).then_inc(cn_lo, 1)

                def slot(j, p, s):
                    if isinstance(s, int) and s == 0:
                        natural_low(0)
                    if inside(s, B):
                        pool.wait_ge(p_hi, s + 1)
                        wait(pool, ptr, s)
                        pool.tensor_tensor(pp[:, 1, 0:S], pn[:, 0:S], pp[:, 0, 0:S], ALU.subtract).then_inc(p_lo, 1)
                    if inside(s + 1, B):
                        for k in range(KD):
                            split_low(pool, 1 - p, s + 1 + B, k)
                    if inside(s, B):
                        norm_root(pool, Q, s)
                    if inside(s + 1, B):
                        natural_low(s + 1)

                run_slots(pool, slot, B + 2, 4)

            @block.scalar
            def _(act):
                def natural_high(b):
                    act.wait_ge(cn_loaded, 48 * (b + 1))
                    wait(act, attended, 2 * b)
                    for c, (a, n) in enumerate(CH):
                        act.activation(cn[0:n, 0, c, :], cn_raw[0:n, c, :], ACT.Copy).then_inc(cn_hi, 1)

                def small_high():
                    act.wait_ge(small_loaded, 64)
                    act.activation(wag_p[:, 0, :, :], ag_in[:, :, :], ACT.Copy, scale=WS).then_inc(small_split, 1)
                    act.activation(wb_p[:, 0, :], b_in[:, :], ACT.Copy, scale=WS).then_inc(small_split, 1)

                def weight_high(k):
                    act.wait_ge(w_loaded[k % RING], 16 * (k // RING + 1))
                    act.activation(w1_p[:, 0, k, :], stage[:, k % RING, :], ACT.Copy, scale=WS).then_inc(w_hi, 1)

                def slot(j, p, s):
                    if inside(s - 1, B):
                        act.wait_ge(y3tr, s)
                        act.activation(y3T[:, 0, :, :], tr[:, 0, 0:KD * Q].rearrange("p (k r) -> p k r", k=KD),
                                       ACT.Copy).then_inc(y3T_hi, 1)
                    if isinstance(s, int) and s == 1:
                        for k in range(W_EARLY, KD):
                            weight_high(k)
                        natural_high(1)
                    if isinstance(s, int) and s == 0:
                        natural_high(0)
                    if inside(s, B):
                        act.wait_ge(biased, s + 1)
                        wait(act, normed, s)
                        act.activation(ex[:, 0:S], s_ps[0:Q, 0:S], ACT.Exp, bias=sm[:, 2:3], scale=SCALE,
                                       accum_out=sm[:, 3:4]).then_inc(exped, 1)
                    if isinstance(s, int) and s == 0:
                        for k in range(W_EARLY):
                            weight_high(k)
                    if inside(s - 1, B):
                        act.wait_ge(gate, GATE_STEPS * (s - 1) + 3)
                        act.activation(gp[:, :], gs[:, :], ACT.Exp, accum_out=sm[:, 12:13]).then_inc(gate_exp, 1)
                    if inside(s, B):
                        act.wait_ge(ptr, s + 1)
                        for c, (a, n) in enumerate(CH):
                            for part in range(2):
                                o = (part * 3 + c) * Q
                                act.activation(pT[0:n, part, c, :], tr[0:n, 0, o:o + Q], ACT.Copy).then_inc(pT_ready, 1)
                    if inside(s - 1, B):
                        act.wait_ge(ltr, s)
                        act.activation(lowT[:, :, :], tr[0:LR, 1, 0:2 * Q].rearrange("p (l r) -> p l r", l=2),
                                       ACT.Copy).then_inc(lowT_ready, 1)
                    if inside(s + 1, B):
                        wait(act, scored, s)
                        for k in range(KD):
                            split_high(act, 1 - p, s + 1 + B, k)
                    if isinstance(s, int) and s == 0:
                        small_high()
                    if inside(s, B):
                        act.wait_ge(y3_ready, s + 1)
                        wait(act, y3tr, s)
                        for h in range(2):
                            cols = slice(h * HALF, (h + 1) * HALF)
                            act.activation(y3_p[:, 0, cols], y3[:, cols], ACT.Copy).then_inc(y3_hi, 1)
                    if inside(s + 1, B):
                        if not (isinstance(s, int) and s == 0):
                            natural_high(s + 1)

                run_slots(act, slot, B + 2, 4)

            @block.vector
            def _(dve):
                dve.memset(low_p[:, :, :].rearrange("q l c -> q (l c)"), 0.0).then_inc(small_ready, 1)

                def small_low():
                    dve.wait_ge(small_loaded, 64)
                    dve.wait_ge(small_split, 2)
                    dve.scalar_tensor_tensor(out=wag_p[:, 1, :, :], in0=ag_in[:, :, :], scalar=WS, in1=wag_p[:, 0, :, :],
                                             op0=ALU.mult, op1=ALU.subtract).then_inc(small_ready, 1)
                    dve.scalar_tensor_tensor(out=wb_p[:, 1, :], in0=b_in[:, :], scalar=WS, in1=wb_p[:, 0, :],
                                             op0=ALU.mult, op1=ALU.subtract).then_inc(small_ready, 1)
                    dve.tensor_scalar(tg_b[:, :], tg_b[:, :], tg[:, 3:4], None, ALU.mult).then_inc(small_ready, 1)
                    dve.wait_ge(small_ready, 4)

                def weight_low(k):
                    dve.wait_ge(w_hi, k + 1)
                    dve.scalar_tensor_tensor(out=w1_p[:, 1, k, :], in0=stage[:, k % RING, :], scalar=WS,
                                             in1=w1_p[:, 0, k, :], op0=ALU.mult, op1=ALU.subtract).then_inc(w_lo, 1)

                def softmax_head(j, p, s):
                    dve.wait_ge(scored, s + 1)
                    dve.wait_ge(tx_loaded[p], 48 * (j + 1))
                    wait(dve, exped, s)
                    dve.tensor_reduce(sm[:, 0:1], s_ps[0:Q, 0:S], AX.X, ALU.max).then_inc(maxed, 1)
                    dve.wait_ge(maxed, s + 1)
                    dve.tensor_scalar(sm[:, 1:2], sm[:, 0:1], x2[:, p, D:D + 1], None, ALU.add).then_inc(shifted, 1)
                    dve.wait_ge(shifted, s + 1)
                    dve.tensor_scalar(sm[:, 2:3], x2[:, p, D:D + 1], sm[:, 1:2], SCALE, ALU.subtract,
                                      ALU.mult).then_inc(biased, 1)

                def softmax_tail(s):
                    dve.wait_ge(exped, s + 1)
                    dve.reciprocal(sm[:, 4:5], sm[:, 3:4]).then_inc(inverted, 1)
                    dve.wait_ge(inverted, s + 1)
                    wait(dve, p_lo, s)
                    dve.tensor_scalar(pn[:, 0:S], ex[:, 0:S], sm[:, 4:5], None, ALU.mult).then_inc(normed, 1)
                    dve.wait_ge(normed, s + 1)
                    wait(dve, ptr, s)
                    dve.tensor_copy(pp[:, 0, 0:S], pn[:, 0:S]).then_inc(p_hi, 1)

                def gate_head(t):
                    base = GATE_STEPS * t
                    dve.wait_ge(ag_done, t + 1)
                    dve.scalar_tensor_tensor(out=gs[:, :], in0=ag_ps[0:Q, LR:AG], scalar=1.0 / WS,
                                             in1=gate_bias[0:Q, :], op0=ALU.mult, op1=ALU.add).then_inc(gate, 1)
                    dve.wait_ge(gate, base + 1)
                    dve.tensor_reduce(sm[:, 5:6], gs[:, :], AX.X, ALU.max).then_inc(gate, 1)
                    dve.wait_ge(gate, base + 2)
                    dve.tensor_scalar(gs[:, :], gs[:, :], sm[:, 5:6], None, ALU.subtract).then_inc(gate, 1)

                def gate_tail(t):
                    base = GATE_STEPS * t
                    dve.wait_ge(gate_exp, t + 1)
                    dve.reciprocal(sm[:, 13:14], sm[:, 12:13]).then_inc(gate, 1)
                    dve.wait_ge(gate, base + 4)
                    dve.tensor_scalar(gp[:, :], gp[:, :], sm[:, 13:14], None, ALU.mult).then_inc(gate, 1)
                    dve.wait_ge(gate, base + 5)
                    dve.tensor_tensor_scan(sm[:, 8:12], gp[:, :], gp[:, :], 0.0, ALU.max, ALU.max).then_inc(gate, 1)
                    dve.wait_ge(gate, base + 6)
                    dve.reciprocal(sm[:, 14:15], sm[:, 11:12]).then_inc(gate, 1)
                    dve.tensor_scalar(sm[:, 16:19], sm[:, 8:11], sm[:, 11:12], None, ALU.is_lt).then_inc(gate, 1)
                    dve.wait_ge(gate, base + 8)
                    dve.tensor_scalar(sm[:, 15:16], sm[:, 11:12], sm[:, 14:15], 1.0 / WS, ALU.mult,
                                      ALU.mult).then_inc(gate, 1)
                    dve.wait_ge(gate, base + 9)
                    wait(dve, low_lo, t)
                    dve.tensor_scalar(low[:, 0:RANKS[0]], ag_ps[0:Q, 0:RANKS[0]], sm[:, 15:16], None,
                                      ALU.mult).then_inc(low_hi, 1)
                    for i in range(3):
                        a, b = RANKS[i], RANKS[i + 1]
                        dve.tensor_scalar(low[:, a:b], ag_ps[0:Q, a:b], sm[:, 16 + i:17 + i], sm[:, 15:16],
                                          ALU.mult, ALU.mult).then_inc(low_hi, 1)
                    dve.wait_ge(low_hi, 5 * t + 4)
                    wait(dve, ltr, t)
                    dve.tensor_copy(low_p[:, 0, 0:LR], low[:, :]).then_inc(low_hi, 1)
                    dve.wait_ge(low_hi, 5 * t + 5)
                    dve.tensor_tensor(low_p[:, 1, 0:LR], low[:, :], low_p[:, 0, 0:LR], ALU.subtract).then_inc(low_lo, 1)

                def slot(j, p, s):
                    if inside(s - 1, B):
                        dve.wait_ge(y3tr, s)
                        dve.tensor_copy(y3T[:, 1, :, :], tr[:, 1, 0:KD * Q].rearrange("p (k r) -> p k r", k=KD)
                                        ).then_inc(y3T_lo, 1)
                    if isinstance(s, int) and s == 1:
                        for k in range(W_EARLY, KD):
                            weight_low(k)
                    if inside(s, B):
                        softmax_head(j, p, s)
                    if inside(s - 1, B):
                        gate_head(s - 1)
                    if inside(s, B):
                        softmax_tail(s)
                    if inside(s - 1, B):
                        gate_tail(s - 1)
                    if isinstance(s, int) and s == 0:
                        for k in range(W_EARLY):
                            weight_low(k)
                    if inside(s, B):
                        for h in range(2):
                            cols = slice(h * HALF, (h + 1) * HALF)
                            dve.wait_ge(attended, 2 * s + h + 1)
                            dve.scalar_tensor_tensor(out=x3[:, cols], in0=a_ps[0:Q, h, :], scalar=tg[0:Q, 2:3],
                                                     in1=x2[:, p, cols], op0=ALU.mult, op1=ALU.add
                                                     ).then_inc(x3_ready, 1)
                        dve.wait_ge(x3_ready, 2 * s + 2)
                        norm_measure(dve, x3[:, :], Q, s)
                        norm_scaled(dve, y3[:, :], x3[:, :], Q, s).then_inc(y3_ready, 1)
                        for h in range(2):
                            cols = slice(h * HALF, (h + 1) * HALF)
                            dve.wait_ge(y3_hi, 2 * s + h + 1)
                            dve.tensor_tensor(y3_p[:, 1, cols], y3[:, cols], y3_p[:, 0, cols], ALU.subtract
                                              ).then_inc(y3_lo, 1)
                        if isinstance(s, int) and s == 0:
                            small_low()
                        dve.tensor_tensor(x3b[:, p, :], x3[:, :], tg_b[0:Q, :], ALU.add).then_inc(x3b_ready, 1)
                    if inside(s - 1, B):
                        if inside(s - 3, B):
                            dve.wait_ge(stored[1 - p], 16 * (j - 1 + p))
                        dve.wait_ge(x3b_ready, s)
                        for h in range(2):
                            cols = slice(h * HALF, (h + 1) * HALF)
                            dve.wait_ge(ffn_done, 2 * (s - 1) + h + 1)
                            dve.scalar_tensor_tensor(out=res[:, 1 - p, cols], in0=f_ps[0:Q, h, :],
                                                     scalar=tg_w1[0:Q, :], in1=x3b[:, 1 - p, cols],
                                                     op0=ALU.mult, op1=ALU.add).then_inc(res_ready, 1)

                run_slots(dve, slot, B + 2, 4)

            @block.tensor
            def _(pe):
                def ffn(t, h, passes):
                    if passes[0] == 0:
                        wait(pe, res_ready, 2 * (t - 1) + h + 1)
                    for n in passes:
                        a, b = PASSES[n]
                        for k in range(KD):
                            mm(f_ps[0:Q, h, :], y3T[:, a, k, :], w1_p[:, b, k, h * HALF:(h + 1) * HALF],
                               start=(n == 0 and k == 0), stop=False)

                def scores(p, n):
                    for k in range(KD):
                        last = mm(s_ps[0:Q, 0:S], tT[:, p, PASSES[n][0], k, :], cT[:, p, PASSES[n][1], k, 0:S],
                                  start=(n == 0 and k == 0), stop=(n == 2 and k == KD - 1))
                    return last

                def low_rank(t):
                    pe.wait_ge(lowT_ready, t + 1)
                    for h in range(2):
                        for n, (a, b) in enumerate(PASSES):
                            last = mm(f_ps[0:Q, h, :], lowT[:, a, :], wb_p[:, b, h * HALF:(h + 1) * HALF],
                                      start=False, stop=(n == 2))
                        last.then_inc(ffn_done, 1)

                def slot(j, p, s):
                    if inside(s, B):
                        pe.wait_ge(split_lo, KD * (s + 1 + B))
                        pe.wait_ge(tx_loaded[p], 48 * (j + 1))
                        wait(pe, exped, s)
                        for n in range(2):
                            scores(p, n)
                    if inside(s - 1, B):
                        pe.wait_ge(y3_lo, 2 * s)
                        if inside(s - 2, B):
                            pe.wait_ge(lowT_ready, s - 1)
                            pe.wait_ge(pT_ready, 6 * s)
                        for part in range(2):
                            for k in range(KD):
                                last = pe.transpose(tr[:, part, k * Q:(k + 1) * Q], y3_p[:, part, k * P:(k + 1) * P],
                                                    ident[0:Q, 0:Q])
                        last.then_inc(y3tr, 1)
                    if inside(s, B):
                        scores(p, 2).then_inc(scored, 1)
                    if inside(s - 1, B):
                        pe.wait_ge(y3T_hi, s)
                        pe.wait_ge(y3T_lo, s)
                        wait(pe, low_lo, s - 1)
                        if isinstance(s, int) and s == 1:
                            pe.wait_ge(w_lo, KD)
                            pe.wait_ge(small_ready, 4)
                        for n, (a, b) in enumerate(PASSES):
                            for k in range(KD):
                                last = mm(ag_ps[0:Q, 0:AG], y3T[:, a, k, :], wag_p[:, b, k, :],
                                          start=(n == 0 and k == 0), stop=(n == 2 and k == KD - 1))
                        last.then_inc(ag_done, 1)
                        ffn(s - 1, 0, (0, 1))
                    if inside(s, B):
                        pe.wait_ge(p_lo, s + 1)
                        for part in range(2):
                            for c, (a, n) in enumerate(CH):
                                o = (part * 3 + c) * Q
                                last = pe.transpose(tr[0:n, 0, o:o + Q], pp[:, part, a:a + n], ident[0:Q, 0:Q])
                        last.then_inc(ptr, 1)
                    if inside(s - 1, B):
                        ffn(s - 1, 0, (2,))
                        pe.wait_ge(low_lo, s)
                        for part in range(2):
                            last = pe.transpose(tr[:, 1, part * Q:(part + 1) * Q], low_p[:, part, :],
                                                ident[0:Q, 0:Q])
                        last.then_inc(ltr, 1)
                    if inside(s, B):
                        pe.wait_ge(cn_lo, 3 * (s + 1))
                        pe.wait_ge(pT_ready, 6 * (s + 1))
                        for h in range(2):
                            wait(pe, x3_ready, 2 * (s - 1) + h + 1)
                            for i, (a, b) in enumerate(PASSES):
                                for c, (_, n) in enumerate(CH):
                                    last = mm(a_ps[0:Q, h, :], pT[0:n, a, c, :],
                                              cn[0:n, b, c, h * HALF:(h + 1) * HALF],
                                              start=(i == 0 and c == 0), stop=(i == 2 and c == 2))
                            last.then_inc(attended, 1)
                    if inside(s - 1, B):
                        ffn(s - 1, 1, (0, 1, 2))
                        low_rank(s - 1)

                run_slots(pe, slot, B + 2, 4)


def chunked(a):
    import numpy as np
    return np.ascontiguousarray(a.reshape(-1, P, a.shape[1]).transpose(1, 0, 2))


def kernel(**inputs):
    import numpy as np
    import concourse.bacc as bacc
    from concourse.bass_utils import run_bass_kernel_spmd as run

    i = {k: np.asarray(v) for k, v in inputs.items()}
    ctx = i["ctx_4096"]
    arrays = {
        "x": i["x"].reshape(R, D),
        "ctx_nat": ctx,
        "ctx_t": ctx.reshape(B, S, KD, P).transpose(0, 3, 2, 1),
        "gates": np.stack([i["g_xattn"][0], i["g_ffn"][0], i["g_xattn"][1], i["g_ffn"][1]]).reshape(1, 4),
        "wa": chunked(np.concatenate([i["L0_xattn_Wq"], i["L0_xattn_Wk"], i["L0_xattn_Wv"]], 0).T),
        "wo": chunked(i["L0_xattn_Wo"].T),
        "q4": chunked(i["L0_ffn_weight_q"].T),
        "sc4": i["L0_ffn_weight_scales"].T,
        "wq1": chunked(i["L1_xattn_Wq"]),
        "wk1": chunked(i["L1_xattn_Wk"]),
        "bq1": i["L1_xattn_bq"].reshape(KD, P).T,
        "bk1": i["L1_xattn_bk"].reshape(KD, P).T,
        "w1": chunked(i["L1_ffn_W"].T),
        "b1": i["L1_ffn_b"].reshape(1, D),
        "wag": chunked(np.concatenate([i["L1_ffn_A"], i["L1_ffn_gate_w"]], 0).T),
        "wb": i["L1_ffn_B"].T,
        "gate_b": i["L1_ffn_gate_b"].reshape(1, NG),
    }
    nc = bacc.Bacc("TRN2", target_bir_lowering=False, num_devices=1)
    arrays = {f"in_{k}": np.ascontiguousarray(v) for k, v in arrays.items()}
    args = [nc.dram_tensor(k, v.shape, mybir.dt.from_np(v.dtype), kind="ExternalInput").ap()
            for k, v in arrays.items()]
    out = nc.dram_tensor("out_rows", [R, D], F32, kind="ExternalOutput").ap()
    build(nc, *args, out)
    r = run(nc, [arrays], core_ids=[0])
    return r.results[0]["out_rows"].reshape(B, Q, D)
```
